# Optimizing a Trainium2 kernel written in Bass

```python
import numpy as np
import jax
import jax.numpy as jnp

def _softmax(x, axis=-1):
    return jax.nn.softmax(x, axis=axis)

def _gelu(x):
    return jax.nn.gelu(x, approximate=True)

def _silu(x):
    return jax.nn.silu(x)

def _sigmoid(x):
    return jax.nn.sigmoid(x)

def _layernorm(x, axis=-1, eps=1e-05):
    m = jnp.mean(x, axis=axis, keepdims=True)
    v = jnp.var(x, axis=axis, keepdims=True)
    return (x - m) / jnp.sqrt(v + eps)

def _scatter_add(tgt, idx, src, axis=0):
    return tgt.at[idx].add(src)

def _segment_sum(src, seg, n):
    return jax.ops.segment_sum(src, seg, n)
kernel_name = 'mk_seq_postln_d2_jaxref_r8_05e4ea'

def setup_inputs(seed: int=0):
    np.random.seed(seed)
    _w = jnp.asarray

    def _L0_attn_setup():
        import jax, jax.numpy as jnp
        import numpy as np
        EPS = 1e-05
        CHUNK = 64

        def _short_conv(x, w):
            K = w.shape[1]
            T = x.shape[1]
            xp = jnp.pad(x, ((0, 0), (K - 1, 0), (0, 0)))
            y = sum((xp[:, i:i + T, :] * w[:, i] for i in range(K)))
            return jax.nn.silu(y)

        def _l2norm(x):
            return x * jax.lax.rsqrt(jnp.sum(x * x, -1, keepdims=True) + 1e-06)

        def _forward(hidden_states, Wq, Wk, Wv, conv_q, conv_k, conv_v, Wf1, Wf2, Wb, A_log, dt_bias, Wg, bg, o_norm_w, Wo):
            B, T, _ = hidden_states.shape
            H = A_log.shape[0]
            x = hidden_states
            q = _short_conv(x @ Wq, conv_q)
            k = _short_conv(x @ Wk, conv_k)
            v = _short_conv(x @ Wv, conv_v)
            Dk = q.shape[-1] // H
            Dv = v.shape[-1] // H
            q = _l2norm(q.reshape(B, T, H, Dk))
            k = _l2norm(k.reshape(B, T, H, Dk))
            v = v.reshape(B, T, H, Dv)
            beta = jax.nn.sigmoid(x @ Wb)
            g = (x @ Wf1 @ Wf2).reshape(B, T, H, Dk)
            g = -jnp.exp(A_log)[:, None] * jax.nn.softplus(g + dt_bias.reshape(H, Dk))
            gexp = jnp.exp(g)
            scale = Dk ** (-0.5)

            def step(S, inp):
                q_t, k_t, v_t, ge_t, b_t = inp
                S = S * ge_t[..., None]
                kv = jnp.einsum('bhk,bhkv->bhv', k_t, S)
                upd = (v_t - kv) * b_t[..., None]
                S = S + jnp.einsum('bhk,bhv->bhkv', k_t, upd)
                o_t = jnp.einsum('bhk,bhkv->bhv', q_t, S) * scale
                return (S, o_t)

            @jax.checkpoint
            def chunk_fn(S, chunk):
                return jax.lax.scan(step, S, chunk)

            def tm(a):
                a = jnp.moveaxis(a, 1, 0)
                return a.reshape((T // CHUNK, CHUNK) + a.shape[1:])
            S0 = jnp.zeros((B, H, Dk, Dv), dtype=q.dtype)
            _, o = jax.lax.scan(chunk_fn, S0, (tm(q), tm(k), tm(v), tm(gexp), tm(beta)))
            o = jnp.moveaxis(o.reshape((T, B, H, Dv)), 0, 1)
            gate_o = (x @ Wg + bg).reshape(B, T, H, Dv)
            on = o * jax.lax.rsqrt(jnp.mean(o * o, -1, keepdims=True) + EPS) * o_norm_w
            on = on * jax.nn.silu(gate_o)
            return on.reshape(B, T, H * Dv) @ Wo
        key = jax.random.key(seed)
        ks = jax.random.split(key, 16)
        B, T, D = (2, 256, 256)
        H, Dk, Dv, K = (16, 128, 128, 4)
        n = jax.random.normal
        return {'hidden_states': n(ks[0], (B, T, D), jnp.float32), 'Wq': n(ks[1], (D, H * Dk), jnp.float32) * D ** (-0.5), 'Wk': n(ks[2], (D, H * Dk), jnp.float32) * D ** (-0.5), 'Wv': n(ks[3], (D, H * Dv), jnp.float32) * D ** (-0.5), 'conv_q': n(ks[4], (H * Dk, K), jnp.float32) * 0.5, 'conv_k': n(ks[5], (H * Dk, K), jnp.float32) * 0.5, 'conv_v': n(ks[6], (H * Dv, K), jnp.float32) * 0.5, 'Wf1': n(ks[7], (D, Dv), jnp.float32) * D ** (-0.5), 'Wf2': n(ks[8], (Dv, H * Dk), jnp.float32) * Dv ** (-0.5), 'Wb': n(ks[9], (D, H), jnp.float32) * D ** (-0.5), 'A_log': jnp.log(jax.random.uniform(ks[10], (H,), jnp.float32, 1.0, 16.0)), 'dt_bias': jnp.zeros((H * Dk,), jnp.float32), 'Wg': n(ks[11], (D, H * Dv), jnp.float32) * D ** (-0.5), 'bg': jnp.zeros((H * Dv,), jnp.float32), 'o_norm_w': jnp.ones((Dv,), jnp.float32), 'Wo': n(ks[12], (H * Dv, D), jnp.float32) * (H * Dv) ** (-0.5)}
    _L0_attn_in = _L0_attn_setup()

    def _L0_ffn_setup():
        import jax, jax.numpy as jnp
        import numpy as np
        TOP_K = 2
        key = jax.random.key(seed)
        ks = jax.random.split(key, 5)
        B, S, H, F, E = (2, 128, 256, 512, 8)
        scale_h = 1.0 / np.sqrt(H)
        scale_f = 1.0 / np.sqrt(F)
        return {'hidden_states': jax.random.normal(ks[0], (B, S, H), dtype=jnp.float32), 'gate_w': jax.random.normal(ks[1], (E, H), dtype=jnp.float32) * scale_h, 'w_gate': jax.random.normal(ks[2], (E, F, H), dtype=jnp.float32) * scale_h, 'w_up': jax.random.normal(ks[3], (E, F, H), dtype=jnp.float32) * scale_h, 'w_down': jax.random.normal(ks[4], (E, H, F), dtype=jnp.float32) * scale_f}
    _L0_ffn_in = _L0_ffn_setup()

    def _L1_attn_setup():
        import jax, jax.numpy as jnp
        import numpy as np
        N_HEADS = 16
        N_KV_HEADS = 4
        MAX_TIMESCALE = 10000.0

        def rms_norm(x):
            var = jnp.mean(jnp.square(x.astype(jnp.float32)), axis=-1, keepdims=True)
            return (x * jax.lax.rsqrt(var + 1e-06)).astype(x.dtype)

        def rotate_half(x):
            x1, x2 = jnp.split(x, 2, axis=-1)
            return jnp.concatenate([-x2, x1], axis=-1)

        def sine_table(features, length):
            fraction = jnp.arange(0, features, 2, dtype=jnp.float32) / features
            inv_freq = 1.0 / MAX_TIMESCALE ** fraction
            sinusoid = jnp.arange(length, dtype=jnp.float32)[:, None] * inv_freq[None, :]
            sinusoid = jnp.concatenate([sinusoid, sinusoid], axis=-1)
            return (jnp.sin(sinusoid), jnp.cos(sinusoid))
        key = jax.random.key(seed)
        ks = jax.random.split(key, 5)
        B, T, C = (2, 128, 256)
        N, K = (N_HEADS, N_KV_HEADS)
        H = C // N
        init_std = np.sqrt(2.0 / (5.0 * C))
        wang_std = 2.0 / 24 / np.sqrt(N * H)
        x = jax.random.normal(ks[0], (B, T, C), dtype=jnp.float32)
        q_kernel = jax.random.normal(ks[1], (C, N * H), dtype=jnp.float32) * init_std
        k_kernel = jax.random.normal(ks[2], (C, K * H), dtype=jnp.float32) * init_std
        v_kernel = jax.random.normal(ks[3], (C, K * H), dtype=jnp.float32) * init_std
        out_kernel = jax.random.normal(ks[4], (N * H, C), dtype=jnp.float32) * wang_std
        return {'x': x, 'q_kernel': q_kernel, 'k_kernel': k_kernel, 'v_kernel': v_kernel, 'out_kernel': out_kernel}
    _L1_attn_in = _L1_attn_setup()

    def _L1_ffn_setup():
        import jax, jax.numpy as jnp
        import numpy as np
        import math
        B, S, D = (2, 256, 256)
        H, HD = (16, 128)
        E, I = (4, 256)
        TOP_K = 2
        ROPE_THETA = 10000.0

        def _layernorm(x, w, b):
            mu = jnp.mean(x, axis=-1, keepdims=True)
            var = jnp.mean(jnp.square(x - mu), axis=-1, keepdims=True)
            return (x - mu) * jax.lax.rsqrt(var + 1e-05) * w + b

        def _rotate_half(x):
            x1, x2 = jnp.split(x, 2, axis=-1)
            return jnp.concatenate((-x2, x1), axis=-1)

        def _attention(h, wq, bq, wk, bk, wv, bv, wo, bo):
            b, s, _ = h.shape
            q = (h @ wq + bq).reshape(b, s, H, HD).transpose(0, 2, 1, 3)
            k = (h @ wk + bk).reshape(b, s, H, HD).transpose(0, 2, 1, 3)
            v = (h @ wv + bv).reshape(b, s, H, HD).transpose(0, 2, 1, 3)
            inv_freq = 1.0 / ROPE_THETA ** (jnp.arange(0, HD, 2, dtype=jnp.float32) / HD)
            freqs = jnp.arange(s, dtype=jnp.float32)[:, None] * inv_freq[None, :]
            emb = jnp.concatenate((freqs, freqs), axis=-1)
            cos = jnp.cos(emb)[None, None]
            sin = jnp.sin(emb)[None, None]
            q = q * cos + _rotate_half(q) * sin
            k = k * cos + _rotate_half(k) * sin
            scores = jnp.einsum('bhqd,bhkd->bhqk', q, k) / math.sqrt(HD)
            causal = jnp.tril(jnp.ones((s, s), bool))
            scores = jnp.where(causal[None, None], scores, jnp.finfo(jnp.float32).min)
            probs = jax.nn.softmax(scores.astype(jnp.float32), axis=-1).astype(q.dtype)
            out = jnp.einsum('bhqk,bhkd->bhqd', probs, v)
            out = out.transpose(0, 2, 1, 3).reshape(b, s, H * HD)
            return out @ wo + bo

        def _moe(h, w_gate, we1, be1, we2, be2):
            b, s, d = h.shape
            x = h.reshape(-1, d)
            t = x.shape[0]
            raw = jax.nn.softmax(x @ w_gate, axis=-1)
            top_vals, top_idx = jax.lax.top_k(raw, TOP_K)
            w = jax.nn.softmax(top_vals, axis=-1)
            comb = jnp.zeros((t, E), x.dtype).at[jnp.arange(t)[:, None], top_idx].add(w)
            hmid = jax.nn.gelu(jnp.einsum('td,edi->tei', x, we1) + be1[None], approximate=False)
            eout = jnp.einsum('tei,eid->ted', hmid, we2) + be2[None]
            out = jnp.einsum('te,ted->td', comb, eout)
            return out.reshape(b, s, d)
        key = jax.random.key(seed)
        ks = jax.random.split(key, 20)
        s = 0.02
        p = {'hidden_states': jax.random.normal(ks[0], (B, S, D), jnp.float32), 'wq': jax.random.normal(ks[1], (D, H * HD), jnp.float32) * s, 'bq': jnp.zeros((H * HD,), jnp.float32), 'wk': jax.random.normal(ks[2], (D, H * HD), jnp.float32) * s, 'bk': jnp.zeros((H * HD,), jnp.float32), 'wv': jax.random.normal(ks[3], (D, H * HD), jnp.float32) * s, 'bv': jnp.zeros((H * HD,), jnp.float32), 'wo': jax.random.normal(ks[4], (H * HD, D), jnp.float32) * s, 'bo': jnp.zeros((D,), jnp.float32), 'ln1_w': jnp.ones((D,), jnp.float32), 'ln1_b': jnp.zeros((D,), jnp.float32), 'ln2_w': jnp.ones((D,), jnp.float32), 'ln2_b': jnp.zeros((D,), jnp.float32), 'w_gate': jax.random.normal(ks[5], (D, E), jnp.float32) * s, 'we1': jax.random.normal(ks[6], (E, D, I), jnp.float32) * s, 'be1': jnp.zeros((E, I), jnp.float32), 'we2': jax.random.normal(ks[7], (E, I, D), jnp.float32) * s, 'be2': jnp.zeros((E, D), jnp.float32)}
        return p
    _L1_ffn_in = _L1_ffn_setup()
    _d = {'L0_attn_hidden_states': _L0_attn_in['hidden_states'], 'L0_attn_Wq': _L0_attn_in['Wq'], 'L0_attn_Wk': _L0_attn_in['Wk'], 'L0_attn_Wv': _L0_attn_in['Wv'], 'L0_attn_conv_q': _L0_attn_in['conv_q'], 'L0_attn_conv_k': _L0_attn_in['conv_k'], 'L0_attn_conv_v': _L0_attn_in['conv_v'], 'L0_attn_Wf1': _L0_attn_in['Wf1'], 'L0_attn_Wf2': _L0_attn_in['Wf2'], 'L0_attn_Wb': _L0_attn_in['Wb'], 'L0_attn_A_log': _L0_attn_in['A_log'], 'L0_attn_dt_bias': _L0_attn_in['dt_bias'], 'L0_attn_Wg': _L0_attn_in['Wg'], 'L0_attn_bg': _L0_attn_in['bg'], 'L0_attn_o_norm_w': _L0_attn_in['o_norm_w'], 'L0_attn_Wo': _L0_attn_in['Wo'], 'L0_ffn_gate_w': _L0_ffn_in['gate_w'], 'L0_ffn_w_gate': _L0_ffn_in['w_gate'], 'L0_ffn_w_up': _L0_ffn_in['w_up'], 'L0_ffn_w_down': _L0_ffn_in['w_down'], 'L1_attn_q_kernel': _L1_attn_in['q_kernel'], 'L1_attn_k_kernel': _L1_attn_in['k_kernel'], 'L1_attn_v_kernel': _L1_attn_in['v_kernel'], 'L1_attn_out_kernel': _L1_attn_in['out_kernel'], 'L1_ffn_wq': _L1_ffn_in['wq'], 'L1_ffn_bq': _L1_ffn_in['bq'], 'L1_ffn_wk': _L1_ffn_in['wk'], 'L1_ffn_bk': _L1_ffn_in['bk'], 'L1_ffn_wv': _L1_ffn_in['wv'], 'L1_ffn_bv': _L1_ffn_in['bv'], 'L1_ffn_wo': _L1_ffn_in['wo'], 'L1_ffn_bo': _L1_ffn_in['bo'], 'L1_ffn_ln1_w': _L1_ffn_in['ln1_w'], 'L1_ffn_ln1_b': _L1_ffn_in['ln1_b'], 'L1_ffn_ln2_w': _L1_ffn_in['ln2_w'], 'L1_ffn_ln2_b': _L1_ffn_in['ln2_b'], 'L1_ffn_w_gate': _L1_ffn_in['w_gate'], 'L1_ffn_we1': _L1_ffn_in['we1'], 'L1_ffn_be1': _L1_ffn_in['be1'], 'L1_ffn_we2': _L1_ffn_in['we2'], 'L1_ffn_be2': _L1_ffn_in['be2']}
    _x0 = _d['L0_attn_hidden_states']
    _d['L0_attn_hidden_states'] = jax.random.normal(jax.random.fold_in(jax.random.key(seed), 1), (8, 256, 256), dtype=_x0.dtype)
    del _x0
    return _d

def reference(L0_attn_hidden_states, L0_attn_Wq, L0_attn_Wk, L0_attn_Wv, L0_attn_conv_q, L0_attn_conv_k, L0_attn_conv_v, L0_attn_Wf1, L0_attn_Wf2, L0_attn_Wb, L0_attn_A_log, L0_attn_dt_bias, L0_attn_Wg, L0_attn_bg, L0_attn_o_norm_w, L0_attn_Wo, L0_ffn_gate_w, L0_ffn_w_gate, L0_ffn_w_up, L0_ffn_w_down, L1_attn_q_kernel, L1_attn_k_kernel, L1_attn_v_kernel, L1_attn_out_kernel, L1_ffn_wq, L1_ffn_bq, L1_ffn_wk, L1_ffn_bk, L1_ffn_wv, L1_ffn_bv, L1_ffn_wo, L1_ffn_bo, L1_ffn_ln1_w, L1_ffn_ln1_b, L1_ffn_ln2_w, L1_ffn_ln2_b, L1_ffn_w_gate, L1_ffn_we1, L1_ffn_be1, L1_ffn_we2, L1_ffn_be2):

    def _L0_attn_ref(hidden_states, Wq, Wk, Wv, conv_q, conv_k, conv_v, Wf1, Wf2, Wb, A_log, dt_bias, Wg, bg, o_norm_w, Wo):
        import jax, jax.numpy as jnp
        import numpy as np
        EPS = 1e-05
        CHUNK = 64

        def _short_conv(x, w):
            K = w.shape[1]
            T = x.shape[1]
            xp = jnp.pad(x, ((0, 0), (K - 1, 0), (0, 0)))
            y = sum((xp[:, i:i + T, :] * w[:, i] for i in range(K)))
            return jax.nn.silu(y)

        def _l2norm(x):
            return x * jax.lax.rsqrt(jnp.sum(x * x, -1, keepdims=True) + 1e-06)

        def _forward(hidden_states, Wq, Wk, Wv, conv_q, conv_k, conv_v, Wf1, Wf2, Wb, A_log, dt_bias, Wg, bg, o_norm_w, Wo):
            B, T, _ = hidden_states.shape
            H = A_log.shape[0]
            x = hidden_states
            q = _short_conv(x @ Wq, conv_q)
            k = _short_conv(x @ Wk, conv_k)
            v = _short_conv(x @ Wv, conv_v)
            Dk = q.shape[-1] // H
            Dv = v.shape[-1] // H
            q = _l2norm(q.reshape(B, T, H, Dk))
            k = _l2norm(k.reshape(B, T, H, Dk))
            v = v.reshape(B, T, H, Dv)
            beta = jax.nn.sigmoid(x @ Wb)
            g = (x @ Wf1 @ Wf2).reshape(B, T, H, Dk)
            g = -jnp.exp(A_log)[:, None] * jax.nn.softplus(g + dt_bias.reshape(H, Dk))
            gexp = jnp.exp(g)
            scale = Dk ** (-0.5)

            def step(S, inp):
                q_t, k_t, v_t, ge_t, b_t = inp
                S = S * ge_t[..., None]
                kv = jnp.einsum('bhk,bhkv->bhv', k_t, S)
                upd = (v_t - kv) * b_t[..., None]
                S = S + jnp.einsum('bhk,bhv->bhkv', k_t, upd)
                o_t = jnp.einsum('bhk,bhkv->bhv', q_t, S) * scale
                return (S, o_t)

            @jax.checkpoint
            def chunk_fn(S, chunk):
                return jax.lax.scan(step, S, chunk)

            def tm(a):
                a = jnp.moveaxis(a, 1, 0)
                return a.reshape((T // CHUNK, CHUNK) + a.shape[1:])
            S0 = jnp.zeros((B, H, Dk, Dv), dtype=q.dtype)
            _, o = jax.lax.scan(chunk_fn, S0, (tm(q), tm(k), tm(v), tm(gexp), tm(beta)))
            o = jnp.moveaxis(o.reshape((T, B, H, Dv)), 0, 1)
            gate_o = (x @ Wg + bg).reshape(B, T, H, Dv)
            on = o * jax.lax.rsqrt(jnp.mean(o * o, -1, keepdims=True) + EPS) * o_norm_w
            on = on * jax.nn.silu(gate_o)
            return on.reshape(B, T, H * Dv) @ Wo
        return _forward(hidden_states, Wq, Wk, Wv, conv_q, conv_k, conv_v, Wf1, Wf2, Wb, A_log, dt_bias, Wg, bg, o_norm_w, Wo)

    def _L0_ffn_ref(hidden_states, gate_w, w_gate, w_up, w_down):
        import jax, jax.numpy as jnp
        import numpy as np
        TOP_K = 2
        B, S, H = hidden_states.shape
        E = gate_w.shape[0]
        x = hidden_states.reshape(-1, H)
        T = x.shape[0]
        router_logits = x @ gate_w.T
        routing_weights = jax.nn.softmax(router_logits, axis=-1)
        topk_w, topk_i = jax.lax.top_k(routing_weights, TOP_K)
        topk_w = topk_w / jnp.sum(topk_w, axis=-1, keepdims=True)
        dense_w = jnp.zeros((T, E), dtype=x.dtype).at[jnp.arange(T)[:, None], topk_i].set(topk_w)
        g = jnp.einsum('th,efh->tef', x, w_gate)
        u = jnp.einsum('th,efh->tef', x, w_up)
        h = jax.nn.silu(g) * u
        y = jnp.einsum('tef,ehf->teh', h, w_down)
        out = jnp.einsum('te,teh->th', dense_w, y)
        return out.reshape(B, S, H)

    def _L1_attn_ref(x, q_kernel, k_kernel, v_kernel, out_kernel):
        import jax, jax.numpy as jnp
        import numpy as np
        N_HEADS = 16
        N_KV_HEADS = 4
        MAX_TIMESCALE = 10000.0

        def rms_norm(x):
            var = jnp.mean(jnp.square(x.astype(jnp.float32)), axis=-1, keepdims=True)
            return (x * jax.lax.rsqrt(var + 1e-06)).astype(x.dtype)

        def rotate_half(x):
            x1, x2 = jnp.split(x, 2, axis=-1)
            return jnp.concatenate([-x2, x1], axis=-1)

        def sine_table(features, length):
            fraction = jnp.arange(0, features, 2, dtype=jnp.float32) / features
            inv_freq = 1.0 / MAX_TIMESCALE ** fraction
            sinusoid = jnp.arange(length, dtype=jnp.float32)[:, None] * inv_freq[None, :]
            sinusoid = jnp.concatenate([sinusoid, sinusoid], axis=-1)
            return (jnp.sin(sinusoid), jnp.cos(sinusoid))
        B, T, C = x.shape
        N, K = (N_HEADS, N_KV_HEADS)
        G = N // K
        H = C // N
        q = rms_norm(jnp.dot(x, q_kernel))
        k = rms_norm(jnp.dot(x, k_kernel))
        v = jnp.dot(x, v_kernel)
        q = q.reshape(B, T, K, G, H)
        k = k.reshape(B, T, K, H)
        v = v.reshape(B, T, K, H)
        sin, cos = sine_table(H, T)
        qcos = cos[None, :, None, None, :]
        qsin = sin[None, :, None, None, :]
        kcos = cos[None, :, None, :]
        ksin = sin[None, :, None, :]
        q = (q * qcos + rotate_half(q) * qsin).astype(x.dtype)
        k = (k * kcos + rotate_half(k) * ksin).astype(x.dtype)
        scale = jax.lax.rsqrt(jnp.array(H, dtype=jnp.float32)).astype(q.dtype)
        logits = jnp.einsum('btkgh,bskh->bkgts', q * scale, k)
        probs = jax.nn.softmax(logits.astype(jnp.float32), axis=-1).astype(logits.dtype)
        encoded = jnp.einsum('bkgts,bskh->btkgh', probs, v)
        encoded = encoded.reshape(B, T, N * H)
        return jnp.dot(encoded, out_kernel)

    def _L1_ffn_ref(hidden_states, wq, bq, wk, bk, wv, bv, wo, bo, ln1_w, ln1_b, ln2_w, ln2_b, w_gate, we1, be1, we2, be2):
        import jax, jax.numpy as jnp
        import numpy as np
        import math
        B, S, D = (2, 256, 256)
        H, HD = (16, 128)
        E, I = (4, 256)
        TOP_K = 2
        ROPE_THETA = 10000.0

        def _layernorm(x, w, b):
            mu = jnp.mean(x, axis=-1, keepdims=True)
            var = jnp.mean(jnp.square(x - mu), axis=-1, keepdims=True)
            return (x - mu) * jax.lax.rsqrt(var + 1e-05) * w + b

        def _rotate_half(x):
            x1, x2 = jnp.split(x, 2, axis=-1)
            return jnp.concatenate((-x2, x1), axis=-1)

        def _attention(h, wq, bq, wk, bk, wv, bv, wo, bo):
            b, s, _ = h.shape
            q = (h @ wq + bq).reshape(b, s, H, HD).transpose(0, 2, 1, 3)
            k = (h @ wk + bk).reshape(b, s, H, HD).transpose(0, 2, 1, 3)
            v = (h @ wv + bv).reshape(b, s, H, HD).transpose(0, 2, 1, 3)
            inv_freq = 1.0 / ROPE_THETA ** (jnp.arange(0, HD, 2, dtype=jnp.float32) / HD)
            freqs = jnp.arange(s, dtype=jnp.float32)[:, None] * inv_freq[None, :]
            emb = jnp.concatenate((freqs, freqs), axis=-1)
            cos = jnp.cos(emb)[None, None]
            sin = jnp.sin(emb)[None, None]
            q = q * cos + _rotate_half(q) * sin
            k = k * cos + _rotate_half(k) * sin
            scores = jnp.einsum('bhqd,bhkd->bhqk', q, k) / math.sqrt(HD)
            causal = jnp.tril(jnp.ones((s, s), bool))
            scores = jnp.where(causal[None, None], scores, jnp.finfo(jnp.float32).min)
            probs = jax.nn.softmax(scores.astype(jnp.float32), axis=-1).astype(q.dtype)
            out = jnp.einsum('bhqk,bhkd->bhqd', probs, v)
            out = out.transpose(0, 2, 1, 3).reshape(b, s, H * HD)
            return out @ wo + bo

        def _moe(h, w_gate, we1, be1, we2, be2):
            b, s, d = h.shape
            x = h.reshape(-1, d)
            t = x.shape[0]
            raw = jax.nn.softmax(x @ w_gate, axis=-1)
            top_vals, top_idx = jax.lax.top_k(raw, TOP_K)
            w = jax.nn.softmax(top_vals, axis=-1)
            comb = jnp.zeros((t, E), x.dtype).at[jnp.arange(t)[:, None], top_idx].add(w)
            hmid = jax.nn.gelu(jnp.einsum('td,edi->tei', x, we1) + be1[None], approximate=False)
            eout = jnp.einsum('tei,eid->ted', hmid, we2) + be2[None]
            out = jnp.einsum('te,ted->td', comb, eout)
            return out.reshape(b, s, d)
        a = _attention(_layernorm(hidden_states, ln1_w, ln1_b), wq, bq, wk, bk, wv, bv, wo, bo)
        h = hidden_states + a
        m = _moe(_layernorm(h, ln2_w, ln2_b), w_gate, we1, be1, we2, be2)
        return h + m
    x = L0_attn_hidden_states
    x = _layernorm(x + _L0_attn_ref(x, L0_attn_Wq, L0_attn_Wk, L0_attn_Wv, L0_attn_conv_q, L0_attn_conv_k, L0_attn_conv_v, L0_attn_Wf1, L0_attn_Wf2, L0_attn_Wb, L0_attn_A_log, L0_attn_dt_bias, L0_attn_Wg, L0_attn_bg, L0_attn_o_norm_w, L0_attn_Wo), axis=-1)
    x = _layernorm(x + _L0_ffn_ref(x, L0_ffn_gate_w, L0_ffn_w_gate, L0_ffn_w_up, L0_ffn_w_down), axis=-1)
    x = _layernorm(x + _L1_attn_ref(x, L1_attn_q_kernel, L1_attn_k_kernel, L1_attn_v_kernel, L1_attn_out_kernel), axis=-1)
    x = _layernorm(x + _L1_ffn_ref(x, L1_ffn_wq, L1_ffn_bq, L1_ffn_wk, L1_ffn_bk, L1_ffn_wv, L1_ffn_bv, L1_ffn_wo, L1_ffn_bo, L1_ffn_ln1_w, L1_ffn_ln1_b, L1_ffn_ln2_w, L1_ffn_ln2_b, L1_ffn_w_gate, L1_ffn_we1, L1_ffn_be1, L1_ffn_we2, L1_ffn_be2), axis=-1)
    return x

_drawn_inputs = setup_inputs


def setup_inputs(seed=0):
    import zlib

    import numpy as np

    out = dict(_drawn_inputs(seed))
    spreads = {'L0_attn_dt_bias': (0.0, 0.424),
     'L0_attn_bg': (0.0, 0.1),
     'L0_attn_o_norm_w': (1.0, 0.2),
     'L1_ffn_bq': (0.0, 0.8),
     'L1_ffn_bk': (0.0, 0.8),
     'L1_ffn_bv': (0.0, 0.1),
     'L1_ffn_bo': (0.0, 0.1),
     'L1_ffn_ln1_w': (1.0, 0.6),
     'L1_ffn_ln1_b': (0.0, 0.562),
     'L1_ffn_ln2_w': (1.0, 0.6),
     'L1_ffn_ln2_b': (0.0, 0.796),
     'L1_ffn_be1': (0.0, 0.8),
     'L1_ffn_be2': (0.0, 0.1)}
    factors = {'L1_attn_q_kernel': 8.0,
     'L1_attn_k_kernel': 8.0,
     'L1_attn_v_kernel': 8.0,
     'L1_attn_out_kernel': 8.0,
     'L1_ffn_wq': 8.0,
     'L1_ffn_wk': 8.0,
     'L1_ffn_we1': 2.855}
    for name, (base, spread) in spreads.items():
        noise = np.random.default_rng([zlib.crc32(name.encode()), seed]).standard_normal(out[name].shape)
        drawn = base * np.exp(spread * noise) if base else spread * noise
        out[name] = jnp.asarray(drawn.astype(out[name].dtype))
    for name, factor in factors.items():
        out[name] = (out[name] * factor).astype(out[name].dtype)
    return out
```

```python
from contextlib import ExitStack

import concourse.bass as bass
from concourse import mybir

F32 = mybir.dt.float32
U32 = mybir.dt.uint32
ALU = mybir.AluOpType
ACT = mybir.ActivationFunctionType
AX = mybir.AxisListType

P = 128
B, TB, D = 8, 256, 256
TOK = B * TB
NT = TOK // P
H, KC = 16, 4
N = 2 * TB
NB2 = TOK // N
ITERS = H * NB2
E0, F0 = 8, 512
NH1, NKV, HD1 = 16, 4, 16
G1 = NH1 // NKV
H2, HD2, HG = 16, 128, 4
E1, F1 = 4, 256
E8 = 8


class Signal:

    def __init__(self, sem, per):
        self.sem, self.per = sem, per

    def at(self, n, k):
        return n * self.per + k if self.per > 1 else n + k


def new_semaphore(nc, T, name):
    T["semaphores"].append(nc.alloc_semaphore(name))
    return T["semaphores"][-1]


def reuse_semaphores(nc, T):
    nc.clear_and_free_semaphores(T["semaphores"])
    T["semaphores"] = []
    nc.all_engine_barrier()


def kda_phase(nc, ctx, T, W, K):
    def sb(name, shape):
        return ctx.enter_context(nc.sbuf_tensor(name, shape, F32))

    def signal(name, per):
        return Signal(new_semaphore(nc, T, name), per)

    xT, f1T, xres = T["xT"], T["f1T"], T["xres"]
    bank = T["bank"]
    w_proj = sb("w_proj", [P, 4, 2, P])
    w_f2 = sb("w_f2", [P, P])
    w_out = sb("w_out", [P, D])
    w_beta = sb("w_beta", [P, 2, P])
    taps = sb("taps", [P, 3, KC])
    head_c = sb("head_c", [P, 4])
    y = [sb(f"y{m}", [P, N]) for m in "qkv"]
    th = [sb(f"th{m}", [P, N]) for m in "qkv"]
    beta, vb, um, ex = sb("beta", [P, N]), sb("vb", [P, N]), sb("um", [P, N]), sb("ex", [P, N])
    zz, tz = sb("zz", [P, N]), sb("tz", [P, N])
    KQ = [sb("KQ0", [P, 2, N]), sb("KQ1", [P, 2, N])]
    KR = [sb("KR0", [P, N]), sb("KR1", [P, N])]
    gate = sb("gate", [P, N])
    tots = sb("tots", [P, N])
    stack = sb("stack", [P, 6, 4, 64])
    near = sb("near", [P, 4, 64])
    Nf, Af = sb("Nf", [P, 4, P]), sb("Af", [P, 4, P])
    Nh = [sb("Nh0", [P, 4, P]), sb("Nh1", [P, 4, P])]
    U, Ti, Xs = sb("U", [P, 4, P]), sb("Ti", [P, 4, P]), sb("Xs", [P, 4, P])
    vt, vp, kt = sb("vt", [P, 4, P]), sb("vp", [P, 4, P]), sb("kt", [P, 2, P])
    Ss, r1 = sb("Ss", [P, 2, P]), sb("r1", [P, 2, P])
    osq, orms, on = sb("osq", [P, N]), sb("orms", [P, N]), sb("on", [P, N])

    def tot(half):
        if half == 1:
            return gate[:, :]
        off = N - 2 * N // half
        return tots[:, off:off + N // half]

    s_wproj = signal("kda_weights_landed", 16 * 5)
    s_wout = signal("kda_out_weights_landed", 16)
    s_head = signal("kda_head_constants", 4)
    s_proj = [signal(f"kda_proj_{m}", 1) for m in "qkvzub"]
    s_tap = [signal(f"kda_tap_{m}", 1) for m in "qkv"]
    s_conv = [signal(f"kda_conv_{m}", 3) for m in "qkv"]
    s_tanh = [signal(f"kda_tanh_{m}", 1) for m in "qkvzb"]
    s_silu = [signal(f"kda_silu_{m}", 1) for m in "qkv"]
    s_sq = [signal(f"kda_square_{m}", 1) for m in "qk"]
    s_ss = [signal(f"kda_sumsq_{m}", 1) for m in "qk"]
    s_ln = [signal(f"kda_ln_{m}", 1) for m in "qk"]
    s_rs = [signal(f"kda_rsqrt_{m}", 1) for m in "qk"]
    s_u = signal("kda_u_clamped", 2)
    s_eu = signal("kda_exp_u", 1)
    s_sp = signal("kda_softplus_low", 1)
    s_exc = signal("kda_softplus_excess", 1)
    s_sp2 = signal("kda_softplus", 1)
    s_gate = signal("kda_gate", 1)
    s_beta = signal("kda_beta", 1)
    s_z = signal("kda_z", 1)
    s_gz = signal("kda_output_gate", 1)
    s_qn = signal("kda_q_normed", 1)
    s_kn = signal("kda_k_normed", 1)
    s_kb = signal("kda_k_beta", 1)
    s_vb = signal("kda_v_beta", 1)
    s_kq = signal("kda_kq_level", 8)
    s_kqc = signal("kda_kq_copied", 7)
    s_kr = signal("kda_kr_level", 7)
    s_krc = signal("kda_kr_copied", 7)
    s_tot = signal("kda_totals", 6)
    s_gram = signal("kda_gram", 8)
    s_mask = signal("kda_gram_masked", 6)
    s_near = signal("kda_near_summed", 1)
    s_place = signal("kda_placed", 14)
    s_nh = signal("kda_level_masked", 7)
    s_ui = signal("kda_inverse_seed", 1)
    s_tt = signal("kda_seed_transposed", 1)
    s_ti = signal("kda_seed_copied", 1)
    s_x = signal("kda_x", 6)
    s_xs = signal("kda_x_copied", 6)
    s_tx = signal("kda_tx_xu", 6)
    s_tu = signal("kda_inverse_grown", 12)
    s_vt = signal("kda_v_transposed", 1)
    s_vtc = signal("kda_v_transposed_copied", 1)
    s_kt = signal("kda_k_transposed", 1)
    s_ktc = signal("kda_k_transposed_copied", 1)
    s_v0 = signal("kda_v_even", 1)
    s_v0c = signal("kda_v_even_copied", 1)
    s_s = signal("kda_state", 1)
    s_sc = signal("kda_state_copied", 1)
    s_yy = signal("kda_state_read", 1)
    s_r1 = signal("kda_rhs_odd", 1)
    s_v1 = signal("kda_v_odd", 1)
    s_v1c = signal("kda_v_odd_copied", 1)
    s_o = signal("kda_o", 1)
    s_osq = signal("kda_o_square", 1)
    s_oss = signal("kda_o_sumsq", 1)
    s_oln = signal("kda_o_ln", 1)
    s_ors = signal("kda_o_rsqrt", 1)
    s_on1 = signal("kda_o_scaled", 1)
    s_on = signal("kda_o_gated", 1)
    s_wo = signal("kda_out", 1)
    s_acc = signal("kda_out_added", 2)
    T["kda_done"] = s_acc

    BQ, BK, BV = bank[0], bank[1], bank[2]
    BN, BG0, BG1, BX, BT = bank[3], bank[4], bank[5], bank[6], bank[7]
    halves = [0, 1, 2, 4, 8, 16, 32, 64]

    def chunks(ap):
        return ap.rearrange("p (c i) -> p c i", c=4)

    s_zero = new_semaphore(nc, T, "kda_zeroed")
    with nc.Block() as zero_block:
        @zero_block.vector
        def _(dve):
            dve.memset(Nf[:, :, :], 0.0).then_inc(s_zero, 1)
            dve.memset(Af[:, :, :], 0.0).then_inc(s_zero, 1)

    block = ctx.enter_context(nc.Block())

    @block.sync
    def _(sp):
        with sp.Fori(0, H) as h:
            sp.wait_ge(s_proj[5].sem, h * NB2)
            for m, name in enumerate(("Wq", "Wk", "Wv", "Wg")):
                sp.dma_start(w_proj[:, m, :, :], W[name].rearrange("(k p) n -> p k n", p=P)[:, :, bass.ds(h * P, P)]).then_inc(s_wproj.sem, 16)
            sp.dma_start(w_f2[:, :], W["Wf2"][:, bass.ds(h * P, P)]).then_inc(s_wproj.sem, 16)
            sp.wait_ge(s_wo.sem, h * NB2)
            sp.dma_start(w_out[:, :], W["Wo"][bass.ds(h * P, P), :]).then_inc(s_wout.sem, 16)

    @block.gpsimd
    def _(pool):
        with pool.Fori(0, ITERS) as n:
            pool.wait_ge(s_u.sem, s_u.at(n, 2))
            pool.tensor_tensor(ex[:, :], ex[:, :], K["forty"][:, :], ALU.subtract).then_inc(s_exc.sem, 1)
            pool.wait_ge(s_sp.sem, s_sp.at(n, 1))
            pool.wait_ge(s_exc.sem, s_exc.at(n, 1))
            pool.tensor_tensor(um[:, :], um[:, :], ex[:, :], ALU.add).then_inc(s_sp2.sem, 1)
            for i in range(7):
                if i == 0:
                    pool.wait_ge(s_place.sem, s_place.at(n, 14))
                if i == 2:
                    pool.wait_ge(s_ui.sem, s_ui.at(n, 1))
                elif i > 2:
                    pool.wait_ge(s_x.sem, s_x.at(n, i - 2))
                pool.tensor_tensor(Nh[i % 2][:, :, :], Nf[:, :, :], K["level"][:, i:i + 1, :].broadcast_to([P, 4, P]), ALU.mult).then_inc(s_nh.sem, 1)

    @block.tensor
    def _(pe):
        with pe.Fori(0, H) as h:
            with pe.Fori(0, NB2) as b:
                n = h * NB2 + b
                xs = [xT[:, k, bass.ds(b * N, N)] for k in range(2)]
                pe.wait_ge(s_wproj.sem, s_wproj.at(h, 80))
                pe.wait_ge(s_head.sem, s_head.at(h, 4))
                for m, (bk, src) in enumerate([(BQ, 0), (BK, 1), (BV, 2), (BQ, 3), (BK, None), (BV, "b")]):
                    if m >= 3:
                        pe.wait_ge(s_conv[m - 3].sem, s_conv[m - 3].at(n, 3))
                    else:
                        r = [s_z, s_u, s_tanh[4]][m]
                        pe.wait_ge(r.sem, r.at(n, 0))
                        if m == 0:
                            pe.wait_ge(s_tanh[3].sem, s_tanh[3].at(n, 0))
                    if src is None:
                        pe.matmul(bk, w_f2[:, :], f1T[:, bass.ds(b * N, N)], start=True, stop=True).then_inc(s_proj[m].sem, 1)
                        continue
                    lhs = w_beta if src == "b" else w_proj[:, src]
                    pe.matmul(bk, lhs[:, 0, :], xs[0], start=True, stop=False)
                    pe.matmul(bk, lhs[:, 1, :], xs[1], start=False, stop=True).then_inc(s_proj[m].sem, 1)
                for m in range(2):
                    pe.wait_ge(s_sq[m].sem, s_sq[m].at(n, 1))
                    if m == 0:
                        pe.wait_ge(s_kn.sem, s_kn.at(n, 0))
                    else:
                        pe.wait_ge(s_qn.sem, s_qn.at(n, 1))
                    pe.matmul(BN, K["ones"][:, m, :], th[m][:, :], start=True, stop=True).then_inc(s_ss[m].sem, 1)
                pe.wait_ge(s_vb.sem, s_vb.at(n, 1))
                pe.wait_ge(s_acc.sem, s_acc.at(n, 0))
                for c in range(4):
                    ins = pe.transpose(chunks(BX)[:, c, :], chunks(vb[:, :])[:, c, :], K["ident"])
                ins.then_inc(s_vt.sem, 1)
                for i, g in enumerate(halves):
                    kq, kr = (KQ[0], KR[0]) if g == 0 else (KQ[(i - 1) % 2 ^ 1], KR[(i - 1) % 2])
                    out = BG0 if i % 2 == 0 else BG1
                    if g == 0:
                        pe.wait_ge(s_kb.sem, s_kb.at(n, 1))
                        pe.wait_ge(s_qn.sem, s_qn.at(n, 1))
                    else:
                        pe.wait_ge(s_kq.sem, s_kq.at(n, i))
                        if g >= 2:
                            pe.wait_ge(s_kqc.sem, s_kqc.at(n, i - 1))
                            pe.wait_ge(s_kr.sem, s_kr.at(n, i - 1))
                            pe.wait_ge(s_krc.sem, s_krc.at(n, i - 1))
                    if i < 2:
                        pe.wait_ge(s_place.sem, s_place.at(n, 0))
                    else:
                        pe.wait_ge(s_mask.sem, s_mask.at(n, i - 1))
                    for c in range(4):
                        t = c * P
                        if g < 32:
                            spans = [(32 * j, 32 * j, 32) for j in range(4)]
                        elif g == 32:
                            spans = [(0, 32, 32), (64, 96, 32)]
                        else:
                            spans = [(0, 64, 64)]
                        for j0, i0, w in spans:
                            o = out[j0:j0 + w, c * 2 * w:(c + 1) * 2 * w]
                            ins = pe.matmul(o.rearrange("p (a i) -> p a i", a=2), kr[:, t + j0:t + j0 + w], kq[:, :, t + i0:t + i0 + w], start=True, stop=True)
                    ins.then_inc(s_gram.sem, 1)
                pe.wait_ge(s_ui.sem, s_ui.at(n, 1))
                pe.wait_ge(s_place.sem, s_place.at(n, 14))
                for c in range(4):
                    ins = pe.transpose(chunks(BG0)[:, c, :], U[:, c, :], K["ident"])
                ins.then_inc(s_tt.sem, 1)
                for l in range(6):
                    pe.wait_ge(s_nh.sem, s_nh.at(n, l + 2))
                    if l == 0:
                        pe.wait_ge(s_ti.sem, s_ti.at(n, 1))
                        pe.wait_ge(s_vtc.sem, s_vtc.at(n, 1))
                    else:
                        pe.wait_ge(s_tu.sem, s_tu.at(n, 2 * l))
                    for c in range(4):
                        ins = pe.matmul(chunks(BX)[:, c, :], Nh[(l + 1) % 2][:, c, :], Ti[:, c, :], start=True, stop=True)
                    ins.then_inc(s_x.sem, 1)
                    pe.wait_ge(s_xs.sem, s_xs.at(n, l + 1))
                    for c in range(4):
                        pe.matmul(chunks(BT)[:, c, :], U[:, c, :], Xs[:, c, :], start=True, stop=True)
                    for c in range(4):
                        ins = pe.matmul(chunks(BG1)[:, c, :], Xs[:, c, :], U[:, c, :], start=True, stop=True)
                    ins.then_inc(s_tx.sem, 1)
                pe.wait_ge(s_kr.sem, s_kr.at(n, 7))
                pe.wait_ge(s_krc.sem, s_krc.at(n, 7))
                for e in range(2):
                    ins = pe.transpose(BG0[:, e * P:(e + 1) * P], KR[1][:, 2 * e * P:(2 * e + 1) * P], K["ident"])
                ins.then_inc(s_kt.sem, 1)
                pe.wait_ge(s_tu.sem, s_tu.at(n, 12))
                for e in range(2):
                    ins = pe.matmul(BX[:, e * P:(e + 1) * P], U[:, 2 * e, :], vt[:, 2 * e, :], start=True, stop=True)
                ins.then_inc(s_v0.sem, 1)
                pe.wait_ge(s_v0c.sem, s_v0c.at(n, 1))
                pe.wait_ge(s_ktc.sem, s_ktc.at(n, 1))
                for e in range(2):
                    ins = pe.matmul(BG0[:, e * P:(e + 1) * P], kt[:, e, :], vp[:, 2 * e, :], start=True, stop=True)
                ins.then_inc(s_s.sem, 1)
                pe.wait_ge(s_sc.sem, s_sc.at(n, 1))
                pe.wait_ge(s_kq.sem, s_kq.at(n, 8))
                for e in range(2):
                    ins = pe.matmul(BT[:, e * P:(e + 1) * P], KQ[0][:, 0, (2 * e + 1) * P:(2 * e + 2) * P], Ss[:, e, :], start=True, stop=True)
                ins.then_inc(s_yy.sem, 1)
                pe.wait_ge(s_r1.sem, s_r1.at(n, 1))
                for e in range(2):
                    ins = pe.matmul(BX[:, e * P:(e + 1) * P], U[:, 2 * e + 1, :], r1[:, e, :], start=True, stop=True)
                ins.then_inc(s_v1.sem, 1)
                for e in range(2):
                    pe.matmul(chunks(BG1)[:, 2 * e, :], vp[:, 2 * e, :], Af[:, 2 * e, :], start=True, stop=True)
                pe.wait_ge(s_v1c.sem, s_v1c.at(n, 1))
                for e in range(2):
                    c = 2 * e + 1
                    pe.matmul(chunks(BG1)[:, c, :], vp[:, c, :], Af[:, c, :], start=True, stop=False)
                    ins = pe.matmul(chunks(BG1)[:, c, :], Ss[:, e, :], KQ[0][:, 1, c * P:(c + 1) * P], start=False, stop=True)
                ins.then_inc(s_o.sem, 1)
                pe.wait_ge(s_osq.sem, s_osq.at(n, 1))
                pe.matmul(BG0, K["ones"][:, 2, :], osq[:, :], start=True, stop=True).then_inc(s_oss.sem, 1)
                pe.wait_ge(s_on.sem, s_on.at(n, 1))
                pe.wait_ge(s_wout.sem, s_wout.at(h, 16))
                for c in range(4):
                    o = [BX, BT][c // 2][:, (c % 2) * D:(c % 2 + 1) * D]
                    ins = pe.matmul(o, on[:, c * P:(c + 1) * P], w_out[:, :], start=True, stop=True)
                ins.then_inc(s_wo.sem, 1)

    @block.scalar
    def _(act):
        with act.Fori(0, ITERS) as n:
            for m in range(3):
                act.wait_ge(s_proj[m].sem, s_proj[m].at(n, 1))
                act.activation(y[m][:, :], [BQ, BK, BV][m], ACT.Copy, scale=taps[:, m, KC - 1:KC]).then_inc(s_tap[m].sem, 1)
            for m in range(3):
                act.wait_ge(s_conv[m].sem, s_conv[m].at(n, 3))
                act.activation(th[m][:, :], y[m][:, :], ACT.Tanh, scale=0.5).then_inc(s_tanh[m].sem, 1)
            act.wait_ge(s_proj[3].sem, s_proj[3].at(n, 1))
            act.activation(tz[:, :], BQ, ACT.Tanh, scale=0.5, bias=head_c[:, 1:2]).then_inc(s_tanh[3].sem, 1)
            act.wait_ge(s_proj[5].sem, s_proj[5].at(n, 1))
            act.activation(beta[:, :], BV, ACT.Tanh, scale=0.5).then_inc(s_tanh[4].sem, 1)
            for m in range(2):
                act.wait_ge(s_silu[m].sem, s_silu[m].at(n, 1))
                act.activation(th[m][:, :], y[m][:, :], ACT.Square).then_inc(s_sq[m].sem, 1)
            act.wait_ge(s_u.sem, s_u.at(n, 1))
            act.activation(um[:, :], um[:, :], ACT.Exp).then_inc(s_eu.sem, 1)
            for m in range(2):
                act.wait_ge(s_ss[m].sem, s_ss[m].at(n, 1))
                act.activation(th[m][:, :], BN, ACT.Ln, bias=K["eps"][:, m:m + 1]).then_inc(s_ln[m].sem, 1)
                act.wait_ge(s_ln[m].sem, s_ln[m].at(n, 1))
                act.activation(BN, th[m][:, :], ACT.Exp, scale=-0.5).then_inc(s_rs[m].sem, 1)
            act.wait_ge(s_eu.sem, s_eu.at(n, 1))
            act.activation(um[:, :], um[:, :], ACT.Ln, bias=1.0).then_inc(s_sp.sem, 1)
            act.wait_ge(s_sp2.sem, s_sp2.at(n, 1))
            act.activation(gate[:, :], um[:, :], ACT.Exp, scale=head_c[:, 3:4]).then_inc(s_gate.sem, 1)
            act.wait_ge(s_vt.sem, s_vt.at(n, 1))
            act.copy(vt[:, :, :], chunks(BX)).then_inc(s_vtc.sem, 1)
            for s in range(1, 8):
                half = 1 << (s - 1)
                src, dst = KQ[s % 2], KQ[(s + 1) % 2]
                act.wait_ge(s_kq.sem, s_kq.at(n, s))
                act.wait_ge(s_gram.sem, s_gram.at(n, s))
                if s > 1:
                    act.wait_ge(s_kqc.sem, s_kqc.at(n, s - 1))
                v = lambda t: t[:, :, :].rearrange("p a (n s h) -> p a n s h", s=2, h=half)[:, :, :, 0, :]
                act.copy(v(dst), v(src)).then_inc(s_kqc.sem, 1)
                src, dst = KR[(s + 1) % 2], KR[s % 2]
                if s > 1:
                    act.wait_ge(s_kr.sem, s_kr.at(n, s - 1))
                    act.wait_ge(s_krc.sem, s_krc.at(n, s - 1))
                else:
                    act.wait_ge(s_kt.sem, s_kt.at(n, 0))
                v = lambda t: t[:, :].rearrange("p (n s h) -> p n s h", s=2, h=half)[:, :, 1, :]
                act.copy(v(dst), v(src)).then_inc(s_krc.sem, 1)
            act.wait_ge(s_near.sem, s_near.at(n, 1))
            for a, dst in enumerate((Nf, Af)):
                for j in range(4):
                    q = slice(32 * j, 32 * j + 32)
                    act.copy(dst[q, :, q], near[q, :, 32 * a:32 * a + 32]).then_inc(s_place.sem, 1)
            for i, (j0, i0, w) in ((6, (0, 32, 32)), (6, (64, 96, 32)), (7, (0, 64, 64))):
                act.wait_ge(s_gram.sem, s_gram.at(n, i + 1))
                g = [BG0, BG1][i % 2][j0:j0 + w, 0:8 * w].rearrange("p (c a i) -> p c a i", c=4, a=2)
                for a, dst in enumerate((Nf, Af)):
                    act.copy(dst[j0:j0 + w, :, i0:i0 + w], g[:, :, a, :]).then_inc(s_place.sem, 1)
            act.wait_ge(s_tt.sem, s_tt.at(n, 1))
            act.copy(Ti[:, :, :], chunks(BG0)).then_inc(s_ti.sem, 1)
            for l in range(6):
                act.wait_ge(s_x.sem, s_x.at(n, l + 1))
                act.copy(Xs[:, :, :], chunks(BX)).then_inc(s_xs.sem, 1)
            act.wait_ge(s_kt.sem, s_kt.at(n, 1))
            act.copy(kt[:, :, :], BG0[:, 0:2 * P].rearrange("p (e i) -> p e i", e=2)).then_inc(s_ktc.sem, 1)
            pair = lambda t, k: t[:, :, :].rearrange("p (e k) i -> p e k i", k=2)[:, :, k, :]
            two = lambda t: t[:, 0:2 * P].rearrange("p (e i) -> p e i", e=2)
            act.wait_ge(s_v0.sem, s_v0.at(n, 1))
            act.copy(pair(vp, 0), two(BX)).then_inc(s_v0c.sem, 1)
            act.wait_ge(s_s.sem, s_s.at(n, 1))
            act.copy(Ss[:, :, :], two(BG0)).then_inc(s_sc.sem, 1)
            act.wait_ge(s_v1.sem, s_v1.at(n, 1))
            act.copy(pair(vp, 1), two(BX)).then_inc(s_v1c.sem, 1)
            act.wait_ge(s_o.sem, s_o.at(n, 1))
            act.activation(osq[:, :], BG1, ACT.Square).then_inc(s_osq.sem, 1)
            act.wait_ge(s_oss.sem, s_oss.at(n, 1))
            act.activation(orms[:, :], BG0, ACT.Ln, bias=K["eps"][:, 2:3]).then_inc(s_oln.sem, 1)
            act.wait_ge(s_oln.sem, s_oln.at(n, 1))
            act.activation(orms[:, :], orms[:, :], ACT.Exp, scale=-0.5).then_inc(s_ors.sem, 1)

    @block.vector
    def _(dve):
        with dve.Fori(0, H) as h:
            dve.wait_ge(s_gate.sem, h * NB2)
            dve.wait_ge(s_proj[5].sem, h * NB2)
            dve.tensor_scalar(taps[:, :, :].rearrange("p m k -> p (m k)"), K["conv"][:, bass.ds(h, 1), :].rearrange("p a k -> p (a k)"), 1.0, None, ALU.mult).then_inc(s_head.sem, 1)
            dve.tensor_scalar(head_c[:, :], K["heads"][:, bass.ds(h, 1), :].rearrange("p a k -> p (a k)"), 1.0, None, ALU.mult).then_inc(s_head.sem, 1)
            for k in range(2):
                dve.tensor_scalar(w_beta[:, k, :], K["wb"][:, k, bass.ds(h, 1)].broadcast_to([P, P]), 1.0, None, ALU.mult).then_inc(s_head.sem, 1)
            with dve.Fori(0, NB2) as b:
                n = h * NB2 + b
                dve.wait_ge(s_head.sem, s_head.at(h, 4))
                for m in range(3):
                    for j in range(1, KC):
                        if j == 1:
                            dve.wait_ge(s_tap[m].sem, s_tap[m].at(n, 1))
                        else:
                            dve.wait_ge(s_conv[m].sem, s_conv[m].at(n, j - 1))
                        src = [BQ, BK, BV][m].rearrange("p (e t) -> p e t", e=2)[:, :, 0:TB - j]
                        dst = y[m][:, :].rearrange("p (e t) -> p e t", e=2)[:, :, j:TB]
                        dve.scalar_tensor_tensor(dst, src, taps[:, m, KC - 1 - j:KC - j], dst, ALU.mult, ALU.add).then_inc(s_conv[m].sem, 1)
                dve.wait_ge(s_proj[4].sem, s_proj[4].at(n, 1))
                dve.wait_ge(s_gate.sem, s_gate.at(n, 0))
                dve.tensor_scalar(um[:, :], BK, head_c[:, 2:3], 40.0, ALU.add, ALU.min).then_inc(s_u.sem, 1)
                dve.tensor_scalar(ex[:, :], BK, head_c[:, 2:3], 40.0, ALU.add, ALU.max).then_inc(s_u.sem, 1)
                for m in range(3):
                    dve.wait_ge(s_tanh[m].sem, s_tanh[m].at(n, 1))
                    dve.scalar_tensor_tensor(y[m][:, :], th[m][:, :], 1.0, y[m][:, :], ALU.add, ALU.mult).then_inc(s_silu[m].sem, 1)
                dve.wait_ge(s_tanh[3].sem, s_tanh[3].at(n, 1))
                dve.tensor_scalar(zz[:, :], BQ, head_c[:, 0:1], K["onw"][:, 0:1], ALU.add, ALU.mult).then_inc(s_z.sem, 1)
                dve.wait_ge(s_tanh[4].sem, s_tanh[4].at(n, 1))
                dve.tensor_scalar(beta[:, :], beta[:, :], 0.5, 0.5, ALU.mult, ALU.add).then_inc(s_beta.sem, 1)
                dve.wait_ge(s_z.sem, s_z.at(n, 1))
                dve.scalar_tensor_tensor(zz[:, :], tz[:, :], 1.0, zz[:, :], ALU.add, ALU.mult).then_inc(s_gz.sem, 1)
                dve.wait_ge(s_beta.sem, s_beta.at(n, 1))
                dve.wait_ge(s_silu[2].sem, s_silu[2].at(n, 1))
                dve.scalar_tensor_tensor(vb[:, :], y[2][:, :], 0.5, beta[:, :], ALU.mult, ALU.mult).then_inc(s_vb.sem, 1)
                dve.wait_ge(s_rs[0].sem, s_rs[0].at(n, 1))
                dve.tensor_tensor(KQ[0][:, 1, :], BN, y[0][:, :], ALU.mult).then_inc(s_qn.sem, 1)
                dve.wait_ge(s_rs[1].sem, s_rs[1].at(n, 1))
                dve.tensor_tensor(KR[0][:, :], BN, y[1][:, :], ALU.mult).then_inc(s_kn.sem, 1)
                dve.wait_ge(s_kn.sem, s_kn.at(n, 1))
                dve.tensor_tensor(KQ[0][:, 0, :], KR[0][:, :], beta[:, :], ALU.mult).then_inc(s_kb.sem, 1)
                dve.wait_ge(s_kb.sem, s_kb.at(n, 1))
                dve.wait_ge(s_qn.sem, s_qn.at(n, 1))
                dve.wait_ge(s_gate.sem, s_gate.at(n, 1))
                dve.tensor_tensor(KQ[1][:, :, :], KQ[0][:, :, :], gate[:, :].rearrange("p (a t) -> p a t", a=1).broadcast_to([P, 2, N]), ALU.mult).then_inc(s_kq.sem, 1)
                for s in range(1, 8):
                    half = 1 << (s - 1)
                    nb = N // (2 * half)
                    t2 = tot(half).rearrange("p (n s) -> p n s", s=2)
                    if s > 1:
                        dve.wait_ge(s_tot.sem, s_tot.at(n, s - 1))
                    if s < 7:
                        dve.tensor_tensor(tot(2 * half), t2[:, :, 0], t2[:, :, 1], ALU.mult).then_inc(s_tot.sem, 1)
                    src, dst = KR[(s + 1) % 2], KR[s % 2]
                    if s > 1:
                        dve.wait_ge(s_kr.sem, s_kr.at(n, s - 1))
                        dve.wait_ge(s_krc.sem, s_krc.at(n, s - 1))
                    dve.wait_ge(s_gram.sem, s_gram.at(n, s))
                    v = lambda t: t[:, :].rearrange("p (n s h) -> p n s h", s=2, h=half)[:, :, 0, :]
                    dve.tensor_tensor(v(dst), v(src), t2[:, :, 1:2].broadcast_to([P, nb, half]), ALU.mult).then_inc(s_kr.sem, 1)
                    src, dst = KQ[s % 2], KQ[(s + 1) % 2]
                    dve.wait_ge(s_kq.sem, s_kq.at(n, s))
                    if s > 1:
                        dve.wait_ge(s_kqc.sem, s_kqc.at(n, s - 1))
                    for a in range(2):
                        v = lambda t: t[:, a, :].rearrange("p (n s h) -> p n s h", s=2, h=half)[:, :, 1, :]
                        ins = dve.tensor_tensor(v(dst), v(src), t2[:, :, 0:1].broadcast_to([P, nb, half]), ALU.mult)
                    ins.then_inc(s_kq.sem, 1)
                    if s <= 6:
                        i = s - 1
                        dve.wait_ge(s_gram.sem, s_gram.at(n, i + 1))
                        g = [BG0, BG1][i % 2][:, 0:256].rearrange("p (c x) -> p c x", c=4)
                        dve.tensor_tensor(stack[:, i, :, :], g, K["near"][:, i:i + 1, :].broadcast_to([P, 4, 64]), ALU.mult).then_inc(s_mask.sem, 1)
                dve.wait_ge(s_mask.sem, s_mask.at(n, 6))
                dve.tensor_reduce(near[:, :, :], stack[:, :, :, :].rearrange("p l c x -> p c x l"), AX.X, ALU.add).then_inc(s_near.sem, 1)
                dve.wait_ge(s_nh.sem, s_nh.at(n, 1))
                dve.tensor_tensor(U[:, :, :], K["ident"].rearrange("p (a i) -> p a i", a=1).broadcast_to([P, 4, P]), Nh[0][:, :, :], ALU.subtract).then_inc(s_ui.sem, 1)
                for l in range(6):
                    dve.wait_ge(s_tx.sem, s_tx.at(n, l + 1))
                    if l == 0:
                        dve.wait_ge(s_ti.sem, s_ti.at(n, 1))
                        dve.wait_ge(s_ui.sem, s_ui.at(n, 1))
                    else:
                        dve.wait_ge(s_tu.sem, s_tu.at(n, 2 * l))
                    dve.tensor_tensor(Ti[:, :, :], Ti[:, :, :], chunks(BT), ALU.subtract).then_inc(s_tu.sem, 1)
                    dve.tensor_tensor(U[:, :, :], U[:, :, :], chunks(BG1), ALU.subtract).then_inc(s_tu.sem, 1)
                dve.wait_ge(s_yy.sem, s_yy.at(n, 1))
                dve.tensor_tensor(r1[:, :, :], vt[:, :, :].rearrange("p (e k) i -> p e k i", k=2)[:, :, 1, :], BT[:, 0:2 * P].rearrange("p (e i) -> p e i", e=2), ALU.subtract).then_inc(s_r1.sem, 1)
                dve.wait_ge(s_ors.sem, s_ors.at(n, 1))
                dve.tensor_tensor(on[:, :], orms[:, :], BG1, ALU.mult).then_inc(s_on1.sem, 1)
                dve.wait_ge(s_on1.sem, s_on1.at(n, 1))
                dve.wait_ge(s_gz.sem, s_gz.at(n, 1))
                dve.tensor_tensor(on[:, :], on[:, :], zz[:, :], ALU.mult).then_inc(s_on.sem, 1)
                dve.wait_ge(s_wo.sem, s_wo.at(n, 1))
                for e in range(2):
                    xs = xres[:, bass.ds(b * 4 + 2 * e, 2), :]
                    dve.tensor_tensor(xs, xs, [BX, BT][e].rearrange("p (a d) -> p a d", a=2), ALU.add).then_inc(s_acc.sem, 1)


def norm_phase(nc, ctx, T, K, name, dst, affine=None, out=None):
    def sb(n, shape):
        return ctx.enter_context(nc.sbuf_tensor(f"{name}_{n}", shape, F32))

    def sem(n):
        return new_semaphore(nc, T, f"{name}_{n}")

    xres, xT, bank = T["xres"], T["xT"], T["bank"]
    stats, mv = sb("stats", [P, NT, 6]), sb("mv", [P, NT, 2])
    rstd, shift = sb("rstd", [P, NT]), sb("shift", [P, NT])
    stats_done, mv_done, ln_done, rstd_done, shift_done = (sem(s) for s in ("stats", "mv", "ln", "rstd", "shift"))
    even_done, odd_done, turned, copied, stored = (sem(s) for s in ("even", "odd", "turned", "copied", "stored"))
    block = ctx.enter_context(nc.Block())

    @block.vector
    def _(dve):
        for t in range(NT):
            dve.bn_stats(stats[:, t, :], xres[:, t, :]).then_inc(stats_done, 1)
        for t in range(NT):
            dve.wait_ge(stats_done, t + 1)
            dve.bn_aggr(mv[:, t, :], stats[:, t, :]).then_inc(mv_done, 1)
        dve.wait_ge(mv_done, NT)
        dve.wait_ge(rstd_done, 1)
        dve.scalar_tensor_tensor(shift[:, :], mv[:, :, 0], -1.0, rstd[:, :], ALU.mult, ALU.mult).then_inc(shift_done, 1)
        for t in range(0, NT, 2):
            dve.tensor_scalar(dst[:, t, :], xres[:, t, :], mv[:, t, 0:1], rstd[:, t:t + 1], ALU.subtract, ALU.mult).then_inc(even_done, 1)
        if out is None and affine is None:
            for g in range(NT // 4):
                dve.wait_ge(turned, 2 * g + 1)
                dve.tensor_copy(xT[:, 0, g * 512:(g + 1) * 512], bank[(2 * g) % 8]).then_inc(copied, 1)

    @block.scalar
    def _(act):
        act.wait_ge(mv_done, NT)
        act.activation(rstd[:, :], mv[:, :, 1], ACT.Ln, bias=K["eps"][:, 2:3]).then_inc(ln_done, 1)
        act.wait_ge(ln_done, 1)
        act.activation(rstd[:, :], rstd[:, :], ACT.Exp, scale=-0.5).then_inc(rstd_done, 1)
        act.wait_ge(shift_done, 1)
        for t in range(1, NT, 2):
            act.activation(dst[:, t, :], xres[:, t, :], ACT.Identity, bias=shift[:, t:t + 1], scale=rstd[:, t:t + 1]).then_inc(odd_done, 1)
        if out is None:
            for g in range(NT // 4):
                for k in range(2):
                    if affine is None and k == 0:
                        continue
                    act.wait_ge(turned, 2 * g + k + 1)
                    d = xT[:, k, g * 512:(g + 1) * 512]
                    if affine is None:
                        act.copy(d, bank[(2 * g + k) % 8]).then_inc(copied, 1)
                    else:
                        act.activation(d, bank[(2 * g + k) % 8], ACT.Identity, scale=K[affine][:, k:k + 1], bias=K[affine][:, 2 + k:3 + k]).then_inc(copied, 1)

    @block.tensor
    def _(pe):
        if out is None:
            for g in range(NT // 4):
                pe.wait_ge(even_done, 2 * g + 2)
                pe.wait_ge(odd_done, 2 * g + 2)
                for k in range(2):
                    for t in range(4):
                        ins = pe.transpose(bank[(2 * g + k) % 8][:, t * P:(t + 1) * P], dst[:, 4 * g + t, k * P:(k + 1) * P], K["ident"])
                    ins.then_inc(turned, 1)

    @block.sync
    def _(sp):
        if out is not None:
            for g in range(NT // 4):
                sp.wait_ge(even_done, 2 * g + 2)
                sp.wait_ge(odd_done, 2 * g + 2)
                sp.dma_start(out[:, 4 * g:4 * g + 4, :], dst[:, 4 * g:4 * g + 4, :]).then_inc(stored, 16)
            sp.wait_ge(stored, 16 * NT // 4)


def route_phase(nc, ctx, T, K, name, experts, softmax_of_top, scale, add_input=False):
    def sb(n, shape, dt=F32):
        return ctx.enter_context(nc.sbuf_tensor(f"{name}_{n}", shape, dt))

    def sem(n):
        return new_semaphore(nc, T, f"{name}_{n}")

    xT, bank, comb = T["xT"], T["bank"], T["comb"]
    wr = K[name + "_wr"]
    lg, pr, hot = sb("lg", [P, NT, E8]), sb("pr", [P, NT, E8]), sb("hot", [P, NT, E8])
    mx, top, at, atf = sb("mx", [P, NT]), sb("top", [P, NT, 8]), sb("at", [P, NT, 8], U32), sb("atf", [P, NT, 8])
    w = sb("w", [P, 2, NT])
    logits_done, chain, expd, two_exp = sem("logits"), sem("chain"), sem("exp"), sem("exp2")
    block = ctx.enter_context(nc.Block())
    L = bank[0][:, 0:NT * experts].rearrange("p (t e) -> p t e", e=experts)

    def wide(a, e):
        return a.rearrange("p (t a) -> p t a", a=1).broadcast_to([P, NT, e])

    @block.gpsimd
    def _(pool):
        if add_input:
            added = sem("input_added")
            for i in range(4):
                q = slice(4 * i, 4 * i + 4)
                pool.tensor_tensor(T["xres"][:, q, :], T["xres"][:, q, :], T["x_in"][:, q, :], ALU.add).then_inc(added, 1)

    @block.tensor
    def _(pe):
        for t in range(NT):
            for k in range(2):
                ins = pe.matmul(L[:, t, :], xT[:, k, t * P:(t + 1) * P], wr[:, k, 0:experts], start=(k == 0), stop=(k == 1))
        ins.then_inc(logits_done, 1)

    @block.scalar
    def _(act):
        act.wait_ge(chain, 3)
        act.activation(pr[:, :, 0:experts], lg[:, :, 0:experts], ACT.Exp).then_inc(expd, 1)
        if softmax_of_top:
            act.wait_ge(chain, 6 + 2 * NT + 1)
            act.activation(w[:, 1, :], w[:, 0, :], ACT.Exp).then_inc(two_exp, 1)

    @block.vector
    def _(dve):
        done = [0]

        def step(ins):
            ins.then_inc(chain, 1)
            done[0] += 1
            dve.wait_ge(chain, done[0])

        step(dve.memset(pr[:, :, :], -1.0))
        dve.wait_ge(logits_done, 1)
        step(dve.tensor_reduce(mx[:, :], L, AX.X, ALU.max))
        step(dve.tensor_tensor(lg[:, :, 0:experts], L, wide(mx[:, :], experts), ALU.subtract))
        dve.wait_ge(expd, 1)
        step(dve.tensor_reduce(mx[:, :], pr[:, :, 0:experts], AX.X, ALU.add))
        step(dve.reciprocal(mx[:, :], mx[:, :]))
        step(dve.tensor_tensor(pr[:, :, 0:experts], pr[:, :, 0:experts], wide(mx[:, :], experts), ALU.mult))
        for t in range(NT):
            dve.max(top[:, t, :], pr[:, t, :]).then_inc(chain, 1)
        dve.wait_ge(chain, 6 + NT)
        for t in range(NT):
            dve.max_index(at[:, t, :], top[:, t, :], pr[:, t, :]).then_inc(chain, 1)
        done[0] += 2 * NT
        dve.wait_ge(chain, done[0])
        if softmax_of_top:
            step(dve.tensor_tensor(w[:, 0, :], top[:, :, 1], top[:, :, 0], ALU.subtract))
            dve.wait_ge(two_exp, 1)
            step(dve.tensor_scalar(mx[:, :], w[:, 1, :], 1.0, None, ALU.add))
            step(dve.reciprocal(mx[:, :], mx[:, :]))
            step(dve.tensor_scalar(w[:, 0, :], mx[:, :], scale, None, ALU.mult))
            step(dve.tensor_tensor(w[:, 1, :], w[:, 1, :], w[:, 0, :], ALU.mult))
        else:
            step(dve.tensor_tensor(mx[:, :], top[:, :, 1], top[:, :, 0], ALU.add))
            step(dve.reciprocal(mx[:, :], mx[:, :]))
            step(dve.tensor_scalar(mx[:, :], mx[:, :], scale, None, ALU.mult))
            for i in range(2):
                step(dve.tensor_tensor(w[:, i, :], top[:, :, i], mx[:, :], ALU.mult))
        step(dve.tensor_copy(atf[:, :, :], at[:, :, :]))
        iota = K["iota"].rearrange("p (a e) -> p a e", a=1).broadcast_to([P, NT, E8])
        for i, d in enumerate((comb, hot)):
            step(dve.tensor_tensor(d[:, :, :], iota, atf[:, :, i:i + 1].broadcast_to([P, NT, E8]), ALU.is_equal))
            step(dve.tensor_tensor(d[:, :, :], d[:, :, :], wide(w[:, i, :], E8), ALU.mult))
        step(dve.tensor_tensor(comb[:, :, :], comb[:, :, :], hot[:, :, :], ALU.add))


def expert_phase(nc, ctx, T, K, W, name, experts, F, glu):
    def sb(n, shape):
        return ctx.enter_context(nc.sbuf_tensor(f"{name}_{n}", shape, F32))

    def signal(n, per):
        return Signal(new_semaphore(nc, T, f"{name}_{n}"), per)

    xT, xres, comb, bank = T["xT"], T["xres"], T["comb"], T["bank"]
    FT = F // P
    up = 2 if glu else 1
    TBL = TOK // 512
    w_in = [sb(f"w_in{s}", [P, up, 2, F]) for s in range(2)]
    w_dn = [sb(f"w_dn{s}", [P, FT, D]) for s in range(2)]
    b_dn = [sb(f"b_dn{s}", [P, D]) for s in range(2)]
    b_in = sb("b_in", [P, experts, FT])
    th = [sb(f"th{s}", [P, 512]) for s in range(2)]
    hid = sb("hid", [P, FT, 512])
    landed = [signal(f"landed{s}", 16 * 3) for s in range(2)]
    s_in, s_act, s_g, s_hid = signal("in", FT), signal("act", FT), signal("g", FT), signal("hid", FT)
    s_dn = [signal(f"down{s}", 2) for s in range(2)]
    s_add = signal("added", 4)
    block = ctx.enter_context(nc.Block())

    def pairs(eng, body):
        if glu:
            with eng.Fori(0, experts // 2) as e2:
                body(e2)
        else:
            for e2 in range(experts // 2):
                body(e2)

    @block.sync
    def _(sp):
        def load(e2):
            for s in range(2):
                e = e2 * 2 + s
                sp.wait_ge(s_dn[s].sem, s_dn[s].at(e2 * TBL, 0))
                if glu:
                    for i, m in enumerate(("gate", "up")):
                        sp.dma_start(w_in[s][:, i, :, :], W[m][bass.ds(e, 1), :, :].rearrange("a (k p) f -> p (a k) f", p=P)).then_inc(landed[s].sem, 16)
                else:
                    sp.dma_start(w_in[s][:, 0, :, :], W["up"][e, :, :].rearrange("(k p) f -> p k f", p=P)).then_inc(landed[s].sem, 16)
                    sp.dma_start(b_dn[s][0:1, :], W["b_dn"][e:e + 1, :]).then_inc(landed[s].sem, 16)
                sp.dma_start(w_dn[s][:, :, :], W["down"][bass.ds(e, 1), :, :].rearrange("a (f p) d -> p (a f) d", p=P)).then_inc(landed[s].sem, 16)
        pairs(sp, load)

    @block.tensor
    def _(pe):
        def work(e2):
            for s in range(2):
                with pe.Fori(0, TBL) as tb:
                    pe.wait_ge(landed[s].sem, landed[s].at(e2, landed[s].per))
                    n = (e2 * 2 + s) * TBL + tb
                    read = s_hid if glu else s_act
                    for f in range(FT):
                        pe.wait_ge(read.sem, read.at(n, max(f - 1, 0)))
                        for i, o in enumerate((bank[f % 2], bank[2 + f % 2])[:up]):
                            for k in range(2):
                                ins = pe.matmul(o, w_in[s][:, i, k, f * P:(f + 1) * P], xT[:, k, bass.ds(tb * 512, 512)], start=(k == 0), stop=(k == 1))
                        ins.then_inc(s_in.sem, 1)
                    pe.wait_ge(read.sem, read.at(n, FT))
                    pe.wait_ge(s_add.sem, s_add.at(n, 0))
                    for t in range(4):
                        o = bank[4 + t][:, 0:D]
                        for f in range(FT):
                            ins = pe.matmul(o, hid[:, f, t * P:(t + 1) * P], w_dn[s][:, f, :], start=(f == 0), stop=(glu and f == FT - 1))
                        if not glu:
                            ins = pe.matmul(o, K["onerow"], b_dn[s][0:1, :], start=False, stop=True)
                        if t % 2:
                            ins.then_inc(s_dn[s].sem, 1)
        pairs(pe, work)

    @block.scalar
    def _(act):
        def work(e2):
            for s in range(2):
                with act.Fori(0, TBL) as tb:
                    n = (e2 * 2 + s) * TBL + tb
                    for f in range(FT):
                        act.wait_ge(s_in.sem, s_in.at(n, f + 1))
                        if glu:
                            act.activation(th[f % 2][:, :], bank[f % 2], ACT.Tanh, scale=0.5).then_inc(s_act.sem, 1)
                        else:
                            if f == 0:
                                act.wait_ge(s_add.sem, s_add.at(n, 0))
                            act.activation(hid[:, f, :], bank[f % 2], ACT.Gelu, bias=K["be1"][:, e2 * 2 + s, f:f + 1]).then_inc(s_act.sem, 1)
        pairs(act, work)

    @block.vector
    def _(dve):
        def work(e2):
            for s in range(2):
                with dve.Fori(0, TBL) as tb:
                    n = (e2 * 2 + s) * TBL + tb
                    if glu:
                        for f in range(FT):
                            dve.wait_ge(s_act.sem, s_act.at(n, f + 1))
                            dve.scalar_tensor_tensor(th[f % 2][:, :], th[f % 2][:, :], 1.0, bank[f % 2], ALU.add, ALU.mult).then_inc(s_g.sem, 1)
                            dve.wait_ge(s_g.sem, s_g.at(n, f + 1))
                            dve.tensor_tensor(hid[:, f, :], th[f % 2][:, :], bank[2 + f % 2], ALU.mult).then_inc(s_hid.sem, 1)
                    for t in range(4):
                        if t % 2 == 0:
                            dve.wait_ge(s_dn[s].sem, s_dn[s].at(e2 * TBL + tb, t // 2 + 1))
                        row = xres[:, bass.ds(tb * 4 + t, 1), :].rearrange("p a d -> p (a d)")
                        c = comb[:, :, :].rearrange("p t e -> p (t e)")[:, bass.ds(tb * (4 * E8) + e2 * 2 + (t * E8 + s), 1)]
                        dve.scalar_tensor_tensor(row, bank[4 + t][:, 0:D], c, row, ALU.mult, ALU.add).then_inc(s_add.sem, 1)
        pairs(dve, work)


def gqa_phase(nc, ctx, T, K):
    def sb(n, shape):
        return ctx.enter_context(nc.sbuf_tensor(f"gqa_{n}", shape, F32))

    def signal(n, per):
        return Signal(new_semaphore(nc, T, f"gqa_{n}"), per)

    xT, xres, bank = T["xT"], T["xres"], T["bank"]
    wqkv, wo = K["gqa_qkv"], K["gqa_out"]
    QW, KW = NH1 * HD1, NKV * HD1
    xs = sb("xs", [P, 2, TB])
    sq, ss = sb("sq", [P, QW]), sb("ss", [P, 4])
    t1, t2, t3 = sb("t1", [P, 4, QW]), sb("t2", [P, 4, QW]), sb("zero", [P, 1])
    qpad, kpad = sb("qpad", [P, 2, G1, NKV, 32]), sb("kpad", [P, 2, NKV, 32])
    v1 = sb("v1", [P, 2, NKV, HD1 + 1])
    qT, kT = sb("qT", [P, G1, TB]), sb("kT", [P, TB])
    pT = [sb(f"pT{i}", [P, 2, 512]) for i in range(2)]
    rec, enc, encT = sb("rec", [P, 2, NH1]), sb("enc", [P, 2, QW]), sb("encT", [P, 2, TB])
    s_pad = signal("pads_zeroed", 1)
    s_xs, s_qkv, s_ssq, s_ln, s_rs = signal("xs", 2), signal("qkv", 2), signal("sumsq", 4), signal("ln", 2), signal("rsqrt", 1)
    s_v, s_t1, s_t2, s_rope = signal("v", 2), signal("t1", 4), signal("t2", 8), signal("rope", 4)
    s_qt, s_kt, s_qtc, s_ktc = signal("q_turned", 2), signal("k_turned", 1), signal("q_copied", 2), signal("k_copied", 1)
    s_sc, s_ex, s_pv = signal("scores", 16), signal("exp", 16), signal("pv", 8)
    s_rec, s_enc, s_et, s_etc = signal("rec", 2), signal("enc", 2), signal("enc_turned", 1), signal("enc_copied", 1)
    s_out, s_add = signal("out", 1), signal("added", 1)
    block = ctx.enter_context(nc.Block())
    heads = lambda a: a.rearrange("p (h d) -> p h d", d=HD1)

    @block.tensor
    def _(pe):
        pe.wait_ge(s_pad.sem, 4)
        with pe.Fori(0, B) as n:
            pe.wait_ge(s_xs.sem, s_xs.at(n, 2))
            for t in range(2):
                for k in range(2):
                    ins = pe.matmul(bank[t][:, 0:384], xs[:, k, t * P:(t + 1) * P], wqkv[:, k, :], start=(k == 0), stop=(k == 1))
                ins.then_inc(s_qkv.sem, 1)
            pe.wait_ge(s_rope.sem, s_rope.at(n, 4))
            pe.wait_ge(s_v.sem, s_v.at(n, 2))
            for g2 in range(2):
                for g in range(2):
                    for t in range(2):
                        ins = pe.transpose(bank[2 + g2][:, (g * 2 + t) * P:(g * 2 + t + 1) * P], qpad[:, t, 2 * g2 + g, :, :].rearrange("p a b -> p (a b)"), K["ident"])
                ins.then_inc(s_qt.sem, 1)
            for t in range(2):
                ins = pe.transpose(bank[4][:, t * P:(t + 1) * P], kpad[:, t, :, :].rearrange("p a b -> p (a b)"), K["ident"])
            ins.then_inc(s_kt.sem, 1)
            pe.wait_ge(s_qtc.sem, s_qtc.at(n, 2))
            pe.wait_ge(s_ktc.sem, s_ktc.at(n, 1))

            def score(i):
                kk, g2 = i // 2, i % 2
                r = slice(32 * kk, 32 * kk + 32)
                for s in range(2):
                    j = 2 * i + s
                    if j >= 4:
                        pe.wait_ge(s_ex.sem, s_ex.at(n, j - 3))
                    pe.matmul(bank[2 + j % 4], kT[r, s * P:(s + 1) * P], qT[r, 2 * g2:2 * g2 + 2, :].rearrange("p g t -> p (g t)"), start=True, stop=True).then_inc(s_sc.sem, 1)

            def mix(i):
                kk, g2 = i // 2, i % 2
                pe.wait_ge(s_ex.sem, s_ex.at(n, 2 * i + 2))
                for g in range(2):
                    head = kk * G1 + 2 * g2 + g
                    for t in range(2):
                        for s in range(2):
                            ins = pe.matmul(bank[6 + t][:, head * 17:head * 17 + 17], pT[i % 2][:, s, g * TB + t * P:g * TB + (t + 1) * P], v1[:, s, kk, :], start=(s == 0), stop=(s == 1))
                ins.then_inc(s_pv.sem, 1)

            score(0)
            for i in range(8):
                if i < 7:
                    score(i + 1)
                mix(i)
            pe.wait_ge(s_enc.sem, s_enc.at(n, 2))
            for k in range(2):
                for t in range(2):
                    ins = pe.transpose(bank[0][:, (k * 2 + t) * P:(k * 2 + t + 1) * P], enc[:, t, k * P:(k + 1) * P], K["ident"])
            ins.then_inc(s_et.sem, 1)
            pe.wait_ge(s_etc.sem, s_etc.at(n, 1))
            for t in range(2):
                for k in range(2):
                    ins = pe.matmul(bank[1][:, t * D:(t + 1) * D], encT[:, k, t * P:(t + 1) * P], wo[:, k, :], start=(k == 0), stop=(k == 1))
            ins.then_inc(s_out.sem, 1)

    @block.scalar
    def _(act):
        with act.Fori(0, B) as n:
            for t in range(2):
                act.wait_ge(s_qkv.sem, s_qkv.at(n, t + 1))
                if t > 0:
                    act.wait_ge(s_ssq.sem, s_ssq.at(n, 2 * t))
                act.activation(sq[:, :], bank[t][:, 0:QW], ACT.Square, accum_out=ss[:, t:t + 1]).then_inc(s_ssq.sem, 1)
                act.wait_ge(s_ssq.sem, s_ssq.at(n, 2 * t + 1))
                act.activation(sq[:, 0:KW], bank[t][:, QW:QW + KW], ACT.Square, accum_out=ss[:, 2 + t:3 + t]).then_inc(s_ssq.sem, 1)
            act.wait_ge(s_ssq.sem, s_ssq.at(n, 4))
            act.activation(ss[:, 0:2], ss[:, 0:2], ACT.Ln, scale=1.0 / QW, bias=K["eps"][:, 3:4]).then_inc(s_ln.sem, 1)
            act.activation(ss[:, 2:4], ss[:, 2:4], ACT.Ln, scale=1.0 / KW, bias=K["eps"][:, 3:4]).then_inc(s_ln.sem, 1)
            act.wait_ge(s_ln.sem, s_ln.at(n, 2))
            act.activation(ss[:, :], ss[:, :], ACT.Exp, scale=-0.5).then_inc(s_rs.sem, 1)
            for t in range(2):
                act.copy(v1[:, t, :, 0:HD1], bank[t][:, QW + KW:QW + 2 * KW].rearrange("p (k d) -> p k d", d=HD1)).then_inc(s_v.sem, 1)
            for g2 in range(2):
                act.wait_ge(s_qt.sem, s_qt.at(n, g2 + 1))
                act.copy(qT[:, 2 * g2:2 * g2 + 2, :].rearrange("p g t -> p (g t)"), bank[2 + g2]).then_inc(s_qtc.sem, 1)
            act.wait_ge(s_kt.sem, s_kt.at(n, 1))
            act.copy(kT[:, :], bank[4][:, 0:TB]).then_inc(s_ktc.sem, 1)
            for j in range(16):
                i, s = j // 2, j % 2
                act.wait_ge(s_sc.sem, s_sc.at(n, j + 1))
                if i >= 2:
                    act.wait_ge(s_pv.sem, s_pv.at(n, i - 1))
                act.activation(pT[i % 2][:, s, :], bank[2 + j % 4], ACT.Exp, scale=float(HD1) ** -0.5).then_inc(s_ex.sem, 1)
            act.wait_ge(s_et.sem, s_et.at(n, 1))
            act.copy(encT[:, :, :].rearrange("p k t -> p (k t)"), bank[0]).then_inc(s_etc.sem, 1)

    @block.vector
    def _(dve):
        dve.memset(qpad[:, :, :, :, :], 0.0).then_inc(s_pad.sem, 1)
        dve.memset(kpad[:, :, :, :], 0.0).then_inc(s_pad.sem, 1)
        dve.memset(v1[:, :, :, :], 1.0).then_inc(s_pad.sem, 1)
        dve.wait_ge(s_pad.sem, 3)
        dve.memset(t3[:, :], 0.0).then_inc(s_pad.sem, 1)
        half = HD1 // 2
        with dve.Fori(0, B) as n:
            for k in range(2):
                dve.tensor_scalar(xs[:, k, :], xT[:, k, bass.ds(n * TB, TB)], 1.0, None, ALU.mult).then_inc(s_xs.sem, 1)
            dve.wait_ge(s_rs.sem, s_rs.at(n, 1))
            dve.wait_ge(s_v.sem, s_v.at(n, 2))
            for j in range(4):
                t, isk = j % 2, j // 2
                w = KW if isk else QW
                nh = w // HD1
                src = heads(bank[t][:, QW:QW + KW] if isk else bank[t][:, 0:QW])
                r = ss[:, j:j + 1]
                cos = K["rope16"][:, t:t + 1, 0:HD1].broadcast_to([P, nh, HD1])
                sin = K["rope16"][:, t:t + 1, HD1:2 * HD1]
                dve.scalar_tensor_tensor(heads(t1[:, j, 0:w]), src, r, cos, ALU.mult, ALU.mult).then_inc(s_t1.sem, 1)
                for s in range(2):
                    o, i = slice(s * half, (s + 1) * half), slice((1 - s) * half, (2 - s) * half)
                    dve.scalar_tensor_tensor(heads(t2[:, j, 0:w])[:, :, o], src[:, :, i], r, sin[:, :, o].broadcast_to([P, nh, half]), ALU.mult, ALU.mult).then_inc(s_t2.sem, 1)
            for j in range(4):
                t, isk = j % 2, j // 2
                dve.wait_ge(s_t1.sem, s_t1.at(n, 4))
                dve.wait_ge(s_t2.sem, s_t2.at(n, 8))
                if isk:
                    dve.tensor_tensor(kpad[:, t, :, 0:HD1], heads(t1[:, j, 0:KW]), heads(t2[:, j, 0:KW]), ALU.add).then_inc(s_rope.sem, 1)
                else:
                    v = lambda a: a[:, j, :].rearrange("p (k g d) -> p g k d", k=NKV, g=G1)
                    dve.tensor_tensor(qpad[:, t, :, :, 0:HD1], v(t1), v(t2), ALU.add).then_inc(s_rope.sem, 1)
            dve.wait_ge(s_pv.sem, s_pv.at(n, 8))
            for t in range(2):
                o = bank[6 + t][:, 0:NH1 * 17].rearrange("p (h d) -> p h d", d=17)
                dve.reciprocal(rec[:, t, :], o[:, :, 16]).then_inc(s_rec.sem, 1)
            for t in range(2):
                o = bank[6 + t][:, 0:NH1 * 17].rearrange("p (h d) -> p h d", d=17)
                dve.wait_ge(s_rec.sem, s_rec.at(n, 2))
                dve.tensor_tensor(heads(enc[:, t, :]), o[:, :, 0:HD1], rec[:, t, :].rearrange("p (h a) -> p h a", a=1).broadcast_to([P, NH1, HD1]), ALU.mult).then_inc(s_enc.sem, 1)
            dve.wait_ge(s_out.sem, s_out.at(n, 1))
            x = xres[:, bass.ds(n * 2, 2), :]
            dve.tensor_tensor(x, x, bank[1].rearrange("p (t d) -> p t d", t=2), ALU.add).then_inc(s_add.sem, 1)


def mha_phase(nc, ctx, T, K, W):
    def sb(n, shape):
        return ctx.enter_context(nc.sbuf_tensor(f"mha_{n}", shape, F32))

    def signal(n, per):
        return Signal(new_semaphore(nc, T, f"mha_{n}"), per)

    xT, xres, bank = T["xT"], T["xres"], T["bank"]
    NG = H2 // HG
    GW = HG * HD2
    wm = [sb(f"w{m}", [P, 2, H2 * HD2]) for m in "qkv"]
    wo = sb("wo", [P, H2, D])
    bias = sb("bias", [P, 3, GW])
    rb = sb("rb", [P, 2, 2, GW])
    xs = sb("xs", [P, 2, TB])
    t1, t2 = [sb(f"t1_{j}", [P, GW]) for j in range(4)], [sb(f"t2_{j}", [P, GW]) for j in range(2)]
    v = sb("v", [P, 2, GW])
    qT, kT = sb("qT", [P, HG, TB]), sb("kT", [P, HG, TB])
    sc0, sc1 = sb("sc0", [P, HG, P]), sb("sc1", [P, HG, TB])
    mx, sm = sb("mx", [P, 2 * HG]), sb("sm", [P, 2 * HG])
    pt = sb("pt", [P, HG, 3, P])
    oT = sb("oT", [P, HG, TB])
    s_w, s_bias, s_xs = signal("weights", 0), signal("bias", 48), signal("xs", 2)
    s_qkv, s_t1, s_t2 = signal("qkv", 6), signal("t1", 4), signal("t2", 8)
    s_r1, s_r2, s_rb, s_rbt = signal("rope", 4), signal("rope_bias", 4), signal("rb", 4), signal("rbt", 12)
    s_v = signal("v", 2)
    s_tq, s_tqc = signal("turned", 4), signal("turned_copied", 4)
    s_s, s_sm, s_mx, s_neg, s_e = signal("scores", 3), signal("masked", 3), signal("max", 2), signal("neg", 1), signal("exp", 8)
    s_rec, s_p = signal("rec", 1), signal("probs", 8)
    s_pt, s_ptc, s_o, s_oc = signal("probs_turned", 3), signal("probs_copied", 3), signal("o", 2), signal("o_copied", 2)
    s_out, s_add = signal("out", 1), signal("added", 1)
    block = ctx.enter_context(nc.Block())
    rows = lambda a, j=HG: a.rearrange("p (h d) -> p h d", h=j)

    @block.sync
    def _(sp):
        for m, name in enumerate(("wq", "wk", "wv")):
            sp.dma_start(wm[m][:, :, :], W[name].rearrange("(k p) n -> p k n", p=P)).then_inc(s_w.sem, 16)
        sp.dma_start(wo[:, :, :], W["wo"].rearrange("(h p) n -> p h n", p=P)).then_inc(s_w.sem, 16)
        with sp.Fori(0, NG) as g:
            sp.wait_ge(s_add.sem, g * B)
            for m, name in enumerate(("bq", "bk", "bv")):
                sp.dma_start(bias[:, m, :], W[name][:, bass.ds(g * GW, GW)].broadcast_to([P, GW])).then_inc(s_bias.sem, 16)

    @block.tensor
    def _(pe):
        pe.wait_ge(s_w.sem, 64)
        with pe.Fori(0, NG) as g:
            with pe.Fori(0, B) as b:
                n = g * B + b
                pe.wait_ge(s_xs.sem, s_xs.at(n, 2))
                for m in range(3):
                    for t in range(2):
                        if m == 0 and t == 0:
                            pe.wait_ge(s_add.sem, s_add.at(n, 0))
                        for k in range(2):
                            ins = pe.matmul(bank[2 * m + t], xs[:, k, t * P:(t + 1) * P], wm[m][:, k, bass.ds(g * GW, GW)], start=(k == 0), stop=(k == 1))
                        ins.then_inc(s_qkv.sem, 1)
                for j in range(4):
                    m, hh = j // 2, j % 2
                    if hh == 0:
                        pe.wait_ge(s_r2.sem, s_r2.at(n, 2 * m + 2))
                    if j >= 2:
                        pe.wait_ge(s_tqc.sem, s_tqc.at(n, j - 1))
                    for h in range(2):
                        for t in range(2):
                            ins = pe.transpose(bank[6 + hh][:, (h * 2 + t) * P:(h * 2 + t + 1) * P], t1[2 * m + t][:, (2 * hh + h) * P:(2 * hh + h + 1) * P], K["ident"])
                    ins.then_inc(s_tq.sem, 1)
                pe.wait_ge(s_tqc.sem, s_tqc.at(n, 4))
                pe.wait_ge(s_v.sem, s_v.at(n, 2))
                for h in range(HG):
                    ins = pe.matmul(rows(bank[0])[:, h, :], qT[:, h, 0:P], kT[:, h, 0:P], start=True, stop=True)
                ins.then_inc(s_s.sem, 1)
                for hh in range(2):
                    for h in range(2):
                        ins = pe.matmul(bank[1 + hh][:, h * TB:(h + 1) * TB], qT[:, 2 * hh + h, P:TB], kT[:, 2 * hh + h, :], start=True, stop=True)
                    ins.then_inc(s_s.sem, 1)
                for j in range(3):
                    pe.wait_ge(s_p.sem, s_p.at(n, 4 if j == 0 else 8))
                    for h in range(HG):
                        src = sc0[:, h, :] if j == 0 else sc1[:, h, (j - 1) * P:j * P]
                        ins = pe.transpose(bank[3 + j][:, h * P:(h + 1) * P], src, K["ident"])
                    ins.then_inc(s_pt.sem, 1)
                pe.wait_ge(s_ptc.sem, s_ptc.at(n, 3))
                for hh in range(2):
                    for h in range(2):
                        i = 2 * hh + h
                        o = bank[6 + hh][:, h * TB:(h + 1) * TB]
                        pe.matmul(o, v[:, 0, i * P:(i + 1) * P], pt[:, i, 0:2, :].rearrange("p a t -> p (a t)"), start=True, stop=False)
                        ins = pe.matmul(o[:, P:TB], v[:, 1, i * P:(i + 1) * P], pt[:, i, 2, :], start=False, stop=True)
                    ins.then_inc(s_o.sem, 1)
                pe.wait_ge(s_oc.sem, s_oc.at(n, 2))
                for t in range(2):
                    for h in range(HG):
                        ins = pe.matmul(bank[0][:, t * D:(t + 1) * D], oT[:, h, t * P:(t + 1) * P], wo[:, bass.ds(g * HG + h, 1), :].rearrange("p a d -> p (a d)"), start=(h == 0), stop=(h == HG - 1))
                ins.then_inc(s_out.sem, 1)

    @block.gpsimd
    def _(pool):
        with pool.Fori(0, NG * B) as n:
            for j in range(4):
                pool.wait_ge(s_t1.sem, s_t1.at(n, j + 1))
                pool.wait_ge(s_t2.sem, s_t2.at(n, 2 * j + 2))
                pool.tensor_tensor(t1[j][:, :], t1[j][:, :], t2[j % 2][:, :], ALU.add).then_inc(s_r1.sem, 1)
                pool.wait_ge(s_r1.sem, s_r1.at(n, j + 1))
                pool.tensor_tensor(t1[j][:, :], t1[j][:, :], rb[:, j // 2, j % 2, :], ALU.add).then_inc(s_r2.sem, 1)

    @block.scalar
    def _(act):
        with act.Fori(0, NG * B) as n:
            for j in range(4):
                act.wait_ge(s_tq.sem, s_tq.at(n, j + 1))
                d = (qT, kT)[j // 2][:, 2 * (j % 2):2 * (j % 2) + 2, :].rearrange("p h t -> p (h t)")
                act.copy(d, bank[6 + j % 2]).then_inc(s_tqc.sem, 1)
            act.wait_ge(s_neg.sem, s_neg.at(n, 1))
            for t in range(2):
                for h in range(HG):
                    s = (sc0, sc1)[t][:, h, :]
                    i = t * HG + h
                    act.activation(s, s, ACT.Exp, bias=mx[:, i:i + 1], accum_out=sm[:, i:i + 1]).then_inc(s_e.sem, 1)
            for j in range(3):
                act.wait_ge(s_pt.sem, s_pt.at(n, j + 1))
                act.copy(pt[:, :, j, :], rows(bank[3 + j])).then_inc(s_ptc.sem, 1)
            for hh in range(2):
                act.wait_ge(s_o.sem, s_o.at(n, hh + 1))
                act.copy(oT[:, 2 * hh:2 * hh + 2, :].rearrange("p h t -> p (h t)"), bank[6 + hh]).then_inc(s_oc.sem, 1)

    @block.vector
    def _(dve):
        half = HD2 // 2
        cos = [K["rope128"][:, t:t + 1, 0:HD2].broadcast_to([P, HG, HD2]) for t in range(2)]
        sin = [[K["rope128"][:, t:t + 1, HD2 + s * half:HD2 + (s + 1) * half].broadcast_to([P, HG, half]) for s in range(2)] for t in range(2)]

        def turn(dst1, dst2, src, t, c_sem, s_sem):
            dve.tensor_tensor(rows(dst1), rows(src), cos[t], ALU.mult).then_inc(c_sem, 1)
            for s in range(2):
                o, i = slice(s * half, (s + 1) * half), slice((1 - s) * half, (2 - s) * half)
                dve.tensor_tensor(rows(dst2)[:, :, o], rows(src)[:, :, i], sin[t][s], ALU.mult).then_inc(s_sem, 1)

        with dve.Fori(0, NG) as g:
            dve.wait_ge(s_bias.sem, s_bias.at(g, 48))
            dve.wait_ge(s_r2.sem, g * (4 * B))
            for j in range(4):
                if j >= 1:
                    dve.wait_ge(s_rb.sem, s_rb.at(g, j))
                turn(rb[:, j // 2, j % 2, :], t2[j % 2][:, :], bias[:, j // 2, :], j % 2, s_rbt.sem, s_rbt.sem)
                dve.wait_ge(s_rbt.sem, s_rbt.at(g, 3 * j + 3))
                dve.tensor_tensor(rb[:, j // 2, j % 2, :], rb[:, j // 2, j % 2, :], t2[j % 2][:, :], ALU.add).then_inc(s_rb.sem, 1)
            with dve.Fori(0, B) as b:
                n = g * B + b
                dve.wait_ge(s_rb.sem, s_rb.at(g, 4))
                for k in range(2):
                    dve.tensor_scalar(xs[:, k, :], xT[:, k, bass.ds(b * TB, TB)], 1.0, None, ALU.mult).then_inc(s_xs.sem, 1)
                for j in range(4):
                    dve.wait_ge(s_qkv.sem, s_qkv.at(n, j + 1))
                    if j >= 2:
                        dve.wait_ge(s_r1.sem, s_r1.at(n, j - 1))
                    turn(t1[j][:, :], t2[j % 2][:, :], bank[j], j % 2, s_t1.sem, s_t2.sem)
                for t in range(2):
                    dve.wait_ge(s_qkv.sem, s_qkv.at(n, 5 + t))
                    dve.tensor_tensor(v[:, t, :], bias[:, 2, :], bank[4 + t], ALU.add).then_inc(s_v.sem, 1)
                tri = K["causal"].rearrange("p (a t) -> p a t", a=1)
                dve.wait_ge(s_s.sem, s_s.at(n, 1))
                dve.scalar_tensor_tensor(sc0[:, :, :], rows(bank[0]), float(HD2) ** -0.5, tri[:, :, P:2 * P].broadcast_to([P, HG, P]), ALU.mult, ALU.add).then_inc(s_sm.sem, 1)
                for hh in range(2):
                    dve.wait_ge(s_s.sem, s_s.at(n, hh + 2))
                    dve.scalar_tensor_tensor(sc1[:, 2 * hh:2 * hh + 2, :], rows(bank[1 + hh], 2), float(HD2) ** -0.5, tri.broadcast_to([P, 2, TB]), ALU.mult, ALU.add).then_inc(s_sm.sem, 1)
                dve.wait_ge(s_sm.sem, s_sm.at(n, 3))
                dve.tensor_reduce(mx[:, 0:HG], sc0[:, :, :], AX.X, ALU.max).then_inc(s_mx.sem, 1)
                dve.tensor_reduce(mx[:, HG:2 * HG], sc1[:, :, :], AX.X, ALU.max).then_inc(s_mx.sem, 1)
                dve.wait_ge(s_mx.sem, s_mx.at(n, 2))
                dve.tensor_scalar(mx[:, :], mx[:, :], -1.0, None, ALU.mult).then_inc(s_neg.sem, 1)
                dve.wait_ge(s_e.sem, s_e.at(n, 8))
                dve.reciprocal(sm[:, :], sm[:, :]).then_inc(s_rec.sem, 1)
                dve.wait_ge(s_rec.sem, s_rec.at(n, 1))
                for i in range(8):
                    s = (sc0, sc1)[i // HG][:, i % HG, :]
                    dve.tensor_scalar(s, s, sm[:, i:i + 1], None, ALU.mult).then_inc(s_p.sem, 1)
                dve.wait_ge(s_out.sem, s_out.at(n, 1))
                x = xres[:, bass.ds(b * 2, 2), :]
                dve.tensor_tensor(x, x, bank[0].rearrange("p (t d) -> p t d", t=2), ALU.add).then_inc(s_add.sem, 1)


def _const_layout():
    widths = [("ident", P), ("ones", 3 * P), ("eps", 4), ("forty", N), ("level", 7 * P), ("near", 6 * 64), ("iota", E8),
              ("causal", TB), ("rope16", 2 * 2 * HD1), ("rope128", 2 * 2 * HD2)]
    at, out = 0, {}
    for name, w in widths:
        out[name] = (at, w)
        at += w
    return out, at


def two_layers(nc, W, const, out):
    with ExitStack() as ctx:
        def sb(name, shape, dt=F32):
            return ctx.enter_context(nc.sbuf_tensor(name, shape, dt))

        psum = ctx.enter_context(nc.psum_tensor("psum", [P, 8, 512], F32))
        T = {"semaphores": [], "bank": [psum[:, i, :] for i in range(8)], "xres": sb("xres", [P, NT, D]), "xT": sb("xT", [P, 2, TOK]), "comb": sb("comb", [P, NT, E8])}
        layout, width = _const_layout()
        table = sb("table", [P, width])
        K = {k: table[:, a:a + w] for k, (a, w) in layout.items()}
        K["onerow"] = K["ones"][0:1, P:2 * P]
        K["ones"] = K["ones"].rearrange("p (m i) -> p m i", m=3)
        K["level"] = K["level"].rearrange("p (l i) -> p l i", l=7)
        K["near"] = K["near"].rearrange("p (l i) -> p l i", l=6)
        K["rope16"] = K["rope16"].rearrange("p (t i) -> p t i", t=2)
        K["rope128"] = K["rope128"].rearrange("p (t i) -> p t i", t=2)
        K["ln1"], K["ln2"] = sb("ln1", [P, 4]), sb("ln2", [P, 4])
        K["r0_wr"], K["r1_wr"] = sb("r0_wr", [P, 2, E0]), sb("r1_wr", [P, 2, E1])
        K["gqa_qkv"], K["gqa_out"] = sb("gqa_qkv", [P, 2, 384]), sb("gqa_out", [P, 2, D])
        K["be1"] = sb("be1", [P, E1, F1 // P])
        xdram = W["x"].rearrange("(t p) d -> p t d", p=P)
        bo = sb("bo", [P, D])
        loads = [(T["xres"][:, 4 * i:4 * i + 4, :], xdram[:, 4 * i:4 * i + 4, :]) for i in range(4)]
        loads += [(table[:, :], const)]
        loads += [(bo[:, :], W["bo"].broadcast_to([P, D]))]
        for m, wb in (("ln1", ("ln1_w", "ln1_b")), ("ln2", ("ln2_w", "ln2_b"))):
            for i, a in enumerate(wb):
                loads.append((K[m][:, 2 * i:2 * i + 2], W[a]))
        loads += [(K["r0_wr"][:, :, :], W["gate_w"].rearrange("(k p) e -> p k e", p=P)),
                  (K["r1_wr"][:, :, :], W["w_gate"].rearrange("(k p) e -> p k e", p=P)),
                  (K["gqa_out"][:, :, :], W["out_kernel"].rearrange("(k p) e -> p k e", p=P)),
                  (K["be1"][:, :, :], W["be1"])]
        for name, a, w in (("q_kernel", 0, 256), ("k_kernel", 256, 64), ("v_kernel", 320, 64)):
            loads.append((K["gqa_qkv"][:, :, a:a + w], W[name].rearrange("(k p) e -> p k e", p=P)))

        with ExitStack() as c1:
            def sb1(name, shape):
                return c1.enter_context(nc.sbuf_tensor(name, shape, F32))

            K["conv"], K["heads"], K["wb"] = sb1("conv", [P, H, 3 * KC]), sb1("heads", [P, H, 4]), sb1("wb", [P, 2, H])
            K["onw"], T["f1T"] = sb1("onw", [P, 1]), sb1("f1T", [P, TOK])
            w_f1, alog, bg, dt_bias = sb1("w_f1", [P, 2, P]), sb1("alog", [P, H]), sb1("bg", [P, H]), sb1("dt_bias", [P, H])
            loads += [(w_f1[:, :, :], W["Wf1"].rearrange("(k p) e -> p k e", p=P)), (K["wb"][:, :, :], W["Wb"].rearrange("(k p) e -> p k e", p=P)),
                      (alog[:, :], W["A_log"].broadcast_to([P, H])), (K["onw"][:, :], W["o_norm_w"]),
                      (bg[:, :], W["bg"]), (dt_bias[:, :], W["dt_bias"])]
            for m, name in enumerate(("conv_q", "conv_k", "conv_v")):
                loads.append((K["conv"][:, :, m * KC:(m + 1) * KC], W[name].rearrange("(h p) k -> p h k", p=P)))
            with ExitStack() as c2:
                landed, turned, copied = (new_semaphore(nc, T, s) for s in ("inputs_landed", "x_turned", "x_copied"))
                f1_done, f1_copied, a_exp, prep = (new_semaphore(nc, T, s) for s in ("f1_done", "f1_copied", "a_exp", "prep"))
                block = c2.enter_context(nc.Block())
                bank, xT = T["bank"], T["xT"]

                @block.sync
                def _(sp):
                    for d, s in loads:
                        sp.dma_start(d, s).then_inc(landed, 16)

                @block.tensor
                def _(pe):
                    pe.wait_ge(landed, 16 * len(loads))
                    for i in range(8):
                        for t in range(4):
                            ins = pe.transpose(bank[i][:, t * P:(t + 1) * P], T["xres"][:, 4 * (i // 2) + t, (i % 2) * P:(i % 2 + 1) * P], K["ident"])
                        ins.then_inc(turned, 1)
                    for i in range(4):
                        pe.wait_ge(copied, 8)
                        for k in range(2):
                            ins = pe.matmul(bank[i], w_f1[:, k, :], xT[:, k, i * 512:(i + 1) * 512], start=(k == 0), stop=(k == 1))
                        ins.then_inc(f1_done, 1)

                @block.scalar
                def _(act):
                    for i in range(8):
                        act.wait_ge(turned, i + 1)
                        act.copy(xT[:, i % 2, (i // 2) * 512:(i // 2 + 1) * 512], bank[i]).then_inc(copied, 1)
                    act.activation(alog[:, :], alog[:, :], ACT.Exp).then_inc(a_exp, 1)
                    for i in range(4):
                        act.wait_ge(f1_done, i + 1)
                        act.copy(T["f1T"][:, i * 512:(i + 1) * 512], bank[i]).then_inc(f1_copied, 1)

                @block.vector
                def _(dve):
                    dve.wait_ge(landed, 16 * len(loads))
                    hd = K["heads"]
                    for i, (src, by) in enumerate(((bg, 1.0), (bg, 0.5), (dt_bias, 1.0))):
                        dve.tensor_scalar(hd[:, :, i], src[:, :], by, None, ALU.mult).then_inc(prep, 1)
                    dve.tensor_scalar(K["onw"][:, :], K["onw"][:, :], 0.5, None, ALU.mult).then_inc(prep, 1)
                    dve.wait_ge(a_exp, 1)
                    dve.tensor_scalar(hd[:, :, 3], alog[:, :], -1.0, None, ALU.mult).then_inc(prep, 1)
            with ExitStack() as c2:
                kda_phase(nc, c2, T, W, K)
        reuse_semaphores(nc, T)
        with ExitStack() as c2:
            norm_phase(nc, c2, T, K, "norm0", T["xres"])
        with ExitStack() as c2:
            route_phase(nc, c2, T, K, "r0", E0, False, 0.5)
        with ExitStack() as c2:
            expert_phase(nc, c2, T, K, {"gate": W["moe0_gate"], "up": W["moe0_up"], "down": W["moe0_down"]}, "moe0", E0, F0, True)
        with ExitStack() as c2:
            norm_phase(nc, c2, T, K, "norm1", T["xres"])
        with ExitStack() as c2:
            gqa_phase(nc, c2, T, K)
        reuse_semaphores(nc, T)
        with ExitStack() as c2:
            norm_phase(nc, c2, T, K, "norm2", T["xres"])
        with ExitStack() as c2:
            xn = c2.enter_context(nc.sbuf_tensor("xn1", [P, NT, D], F32))
            norm_phase(nc, c2, T, K, "ln1", xn, affine="ln1")
        T["x_in"] = sb("x_in", [P, NT, D])
        with ExitStack() as c2:
            x_kept, bo_added = (new_semaphore(nc, T, s) for s in ("x_kept", "bo_added"))
            block = c2.enter_context(nc.Block())

            @block.scalar
            def _(act):
                act.copy(T["x_in"][:, :, :], T["xres"][:, :, :]).then_inc(x_kept, 1)

            @block.vector
            def _(dve):
                dve.wait_ge(x_kept, 1)
                dve.tensor_tensor(T["xres"][:, :, :], T["xres"][:, :, :], bo[:, :].rearrange("p (a d) -> p a d", a=1).broadcast_to([P, NT, D]), ALU.add).then_inc(bo_added, 1)
        with ExitStack() as c2:
            mha_phase(nc, c2, T, K, W)
        with ExitStack() as c2:
            xn = c2.enter_context(nc.sbuf_tensor("xn2", [P, NT, D], F32))
            norm_phase(nc, c2, T, K, "ln2", xn, affine="ln2")
        with ExitStack() as c2:
            route_phase(nc, c2, T, K, "r1", E1, True, 1.0, add_input=True)
        with ExitStack() as c2:
            expert_phase(nc, c2, T, K, {"up": W["we1"], "down": W["we2"], "b_dn": W["be2"]}, "moe1", E1, F1, False)
        with ExitStack() as c2:
            norm_phase(nc, c2, T, K, "last", T["xres"], out=out.rearrange("(t p) d -> p t d", p=P))


def _constants():
    import numpy as np

    layout, width = _const_layout()
    c = np.zeros((P, width), np.float32)

    def put(name, a):
        a0, w = layout[name]
        c[:, a0:a0 + w] = a.reshape(P, w)

    i, j = np.arange(P)[None, :], np.arange(P)[:, None]

    def split(g, j, i):
        return (j // (2 * g) == i // (2 * g)) & (j // g % 2 == 0) & (i // g % 2 == 1)

    put("ident", np.eye(P))
    put("ones", np.stack([np.full((P, P), v) for v in (128.0, 1.0, 1.0 / 128)], 1))
    put("eps", np.tile(np.array([4e-6 * 128, 4e-6, 1e-5, 1e-6]), (P, 1)))
    put("forty", np.full((P, N), 40.0))
    put("level", np.stack([split(1 << l, j, i) for l in range(7)], 1))
    i32, j32 = np.arange(32)[None, :], np.arange(P)[:, None] % 32
    near = [np.concatenate([np.zeros((P, 32)), j32 == i32], 1)]
    near += [np.concatenate([split(1 << l, j32, i32)] * 2, 1) for l in range(5)]
    put("near", np.stack(near, 1))
    put("iota", np.tile(np.arange(E8), (P, 1)))
    tri = np.zeros((P, TB))
    tri[:, P:] = np.where(i > j, -1e30, 0.0)
    put("causal", tri)
    for name, hd in (("rope16", HD1), ("rope128", HD2)):
        inv = (1.0 / 10000.0 ** (np.arange(0, hd, 2, dtype=np.float32) / hd)).astype(np.float32)
        ang = np.arange(TB, dtype=np.float32)[:, None] * inv[None, :]
        cos, sin = np.cos(ang), np.sin(ang)
        tab = np.concatenate([cos, cos, -sin, sin], 1).reshape(2, P, 2 * hd).transpose(1, 0, 2)
        put(name, tab)
    return c


def kernel(**inputs):
    import numpy as _np
    import concourse.bacc as _bacc
    from concourse import mybir as _mybir
    from concourse.bass_utils import run_bass_kernel_spmd as _run

    a0, f0, a1, f1 = "L0_attn_", "L0_ffn_", "L1_attn_", "L1_ffn_"
    get = lambda n: _np.asarray(inputs[n])
    row = lambda n: get(n).reshape(1, -1)
    arrays = {"x": get(a0 + "hidden_states").reshape(TOK, D)}
    for n in ("Wq", "Wk", "Wv", "Wg", "Wo", "Wf1", "Wf2", "Wb", "conv_q", "conv_k", "conv_v"):
        arrays[n] = get(a0 + n)
    arrays["A_log"] = row(a0 + "A_log")
    for n in ("dt_bias", "bg", "o_norm_w"):
        arrays[n] = get(a0 + n).reshape(-1, P).T
    arrays["gate_w"] = get(f0 + "gate_w").T
    for n, m in (("moe0_gate", "w_gate"), ("moe0_up", "w_up"), ("moe0_down", "w_down")):
        arrays[n] = get(f0 + m).transpose(0, 2, 1)
    for n in ("q_kernel", "k_kernel", "v_kernel", "out_kernel"):
        arrays[n] = get(a1 + n)
    for n in ("wq", "wk", "wv", "wo", "w_gate", "we1", "be1", "we2", "be2"):
        arrays[n] = get(f1 + n)
    arrays["be1"] = arrays["be1"].reshape(E1, F1 // P, P).transpose(2, 0, 1)
    for n in ("bq", "bk", "bv", "bo"):
        arrays[n] = row(f1 + n)
    for n in ("ln1_w", "ln1_b", "ln2_w", "ln2_b"):
        arrays[n] = get(f1 + n).reshape(-1, P).T
    arrays["table"] = _constants()
    arrays = {"in_" + n: _np.ascontiguousarray(a) for n, a in arrays.items()}

    nc = _bacc.Bacc("TRN2", target_bir_lowering=False, num_devices=1)
    aps = {n[3:]: nc.dram_tensor(n, a.shape, _mybir.dt.from_np(a.dtype), kind="ExternalInput").ap() for n, a in arrays.items()}
    out = nc.dram_tensor("out", (TOK, D), _mybir.dt.float32, kind="ExternalOutput").ap()
    const = aps.pop("table")
    two_layers(nc, aps, const, out)
    r = _run(nc, [arrays], core_ids=[0])
    return r.results[0]["out"].reshape(B, TB, D)
```

```python
from contextlib import ExitStack

import concourse.bass as bass
from concourse import mybir

F32 = mybir.dt.float32
U32 = mybir.dt.uint32
ALU = mybir.AluOpType
ACT = mybir.ActivationFunctionType
AX = mybir.AxisListType

P = 128
B, TB, D = 8, 256, 256
TOK = B * TB
NT = TOK // P
H, KC = 16, 4
N = 2 * TB
NB2 = TOK // N
ITERS = H * NB2
E0, F0 = 8, 512
NH1, NKV, HD1 = 16, 4, 16
G1 = NH1 // NKV
H2, HD2, HG = 16, 128, 4
E1, F1 = 4, 256
E8 = 8


class Signal:

    def __init__(self, sem, per, dma):
        self.sem, self.per, self.base = sem, per, 0 if dma else 1

    def at(self, n, k):
        return n * self.per + (k + self.base) if self.per > 1 else n + (k + self.base)


def new_semaphore(nc, T, name):
    T["semaphores"].append(nc.alloc_semaphore(name))
    return T["semaphores"][-1]


def new_signal(nc, T, name, per, dma=False):
    signal = Signal(new_semaphore(nc, T, name), per, dma)
    if not dma:
        T["unprimed"].append(signal)
    return signal


def prime_signals(nc, T):
    with nc.Block() as block:
        @block.sync
        def _(sp):
            for signal in T["unprimed"]:
                sp.sem_inc(signal.sem, 1)
    T["unprimed"] = []


def reuse_semaphores(nc, T):
    nc.clear_and_free_semaphores(T["semaphores"])
    T["semaphores"] = []
    nc.all_engine_barrier()


def kda_phase(nc, ctx, T, W, K):
    def sb(name, shape):
        return ctx.enter_context(nc.sbuf_tensor(name, shape, F32))

    def signal(name, per, dma=False):
        return new_signal(nc, T, name, per, dma)

    xT, f1T, xres = T["xT"], T["f1T"], T["xres"]
    bank = T["bank"]
    w_proj = sb("w_proj", [P, 4, 2, P])
    w_f2 = sb("w_f2", [P, P])
    w_out = sb("w_out", [P, D])
    w_beta = sb("w_beta", [P, 2, P])
    taps = sb("taps", [P, 3, KC])
    head_c = sb("head_c", [P, 4])
    y = [sb(f"y{m}", [P, N]) for m in "qkv"]
    th = [sb(f"th{m}", [P, N]) for m in "qkv"]
    beta, vb, um, ex = sb("beta", [P, N]), sb("vb", [P, N]), sb("um", [P, N]), sb("ex", [P, N])
    zz, tz, za = sb("zz", [P, N]), sb("tz", [P, N]), sb("za", [P, N])
    KQ = [sb("KQ0", [P, 2, N]), sb("KQ1", [P, 2, N])]
    KR = [sb("KR0", [P, N]), sb("KR1", [P, N])]
    gate = sb("gate", [P, N])
    tots = sb("tots", [P, N])
    stack = sb("stack", [P, 6, 4, 64])
    near = sb("near", [P, 4, 64])
    Nf, Af = sb("Nf", [P, 4, P]), sb("Af", [P, 4, P])
    Nh = [sb("Nh0", [P, 4, P]), sb("Nh1", [P, 4, P])]
    U, Ti, Xs = sb("U", [P, 4, P]), sb("Ti", [P, 4, P]), sb("Xs", [P, 4, P])
    Xw = sb("Xw", [P, 4, P])
    KQf, KRf = sb("KQf", [P, 2, 2, P]), sb("KRf", [P, 2, P])
    vt, vp, kt = sb("vt", [P, 4, P]), sb("vp", [P, 4, P]), sb("kt", [P, 2, P])
    Ss, r1 = sb("Ss", [P, 2, P]), sb("r1", [P, 2, P])
    osq, orms, on = sb("osq", [P, N]), sb("orms", [P, N]), sb("on", [P, N])

    def tot(half):
        if half == 1:
            return gate[:, :]
        off = N - 2 * N // half
        return tots[:, off:off + N // half]

    s_wproj = signal("kda_weights_landed", 16 * 5, dma=True)
    s_wout = signal("kda_out_weights_landed", 16, dma=True)
    s_head = signal("kda_head_constants", 4)
    s_proj = [signal(f"kda_proj_{m}", 1) for m in "qkvzub"]
    s_tap = [signal(f"kda_tap_{m}", 1) for m in "qkv"]
    s_conv = [signal(f"kda_conv_{m}", 3) for m in "qkv"]
    s_tanh = [signal(f"kda_tanh_{m}", 1) for m in "qkvzb"]
    s_silu = [signal(f"kda_silu_{m}", 1) for m in "qkv"]
    s_sq = [signal(f"kda_square_{m}", 1) for m in "qk"]
    s_ss = [signal(f"kda_sumsq_{m}", 1) for m in "qk"]
    s_ln = [signal(f"kda_ln_{m}", 1) for m in "qk"]
    s_rs = [signal(f"kda_rsqrt_{m}", 1) for m in "qk"]
    s_u = signal("kda_u_clamped", 2)
    s_eu = signal("kda_exp_u", 1)
    s_sp = signal("kda_softplus_low", 1)
    s_exc = signal("kda_softplus_excess", 1)
    s_sp2 = signal("kda_softplus", 1)
    s_gate = signal("kda_gate", 1)
    s_beta = signal("kda_beta", 1)
    s_z = signal("kda_z", 1)
    s_gz = signal("kda_output_gate", 1)
    s_qn = signal("kda_q_normed", 1)
    s_kn = signal("kda_k_normed", 1)
    s_kb = signal("kda_k_beta", 1)
    s_vb = signal("kda_v_beta", 1)
    s_kq = signal("kda_kq_level", 8)
    s_kqc = signal("kda_kq_copied", 7)
    s_kr = signal("kda_kr_level", 7)
    s_krc = signal("kda_kr_copied", 7)
    s_tot = signal("kda_totals", 6)
    s_gram = signal("kda_gram", 8)
    s_mask = signal("kda_gram_masked", 6)
    s_near = signal("kda_near_summed", 1)
    s_place = signal("kda_placed", 14)
    s_nh = signal("kda_level_masked", 7)
    s_ui = signal("kda_inverse_seed", 1)
    s_tt = signal("kda_seed_transposed", 1)
    s_ti = signal("kda_seed_copied", 1)
    s_x = signal("kda_x", 6)
    s_xs = signal("kda_x_copied", 6)
    s_tx = signal("kda_tx_xu", 11)
    s_tu = signal("kda_inverse_grown", 11)
    s_vt = signal("kda_v_transposed", 1)
    s_vtc = signal("kda_v_transposed_copied", 1)
    s_kt = signal("kda_k_transposed", 1)
    s_ktc = signal("kda_k_transposed_copied", 1)
    s_v0 = signal("kda_v_even", 1)
    s_v0c = signal("kda_v_even_copied", 1)
    s_s = signal("kda_state", 1)
    s_sc = signal("kda_state_copied", 1)
    s_yy = signal("kda_state_read", 1)
    s_r1 = signal("kda_rhs_odd", 1)
    s_v1 = signal("kda_v_odd", 1)
    s_v1c = signal("kda_v_odd_copied", 1)
    s_o = signal("kda_o", 1)
    s_osq = signal("kda_o_square", 1)
    s_oss = signal("kda_o_sumsq", 1)
    s_oln = signal("kda_o_ln", 1)
    s_ors = signal("kda_o_rsqrt", 1)
    s_on1 = signal("kda_o_scaled", 1)
    s_on = signal("kda_o_gated", 1)
    s_wo = signal("kda_out", 1)
    s_acc = signal("kda_out_added", 2)

    BQ, BK, BV, BN = bank[0], bank[1], bank[2], bank[3]
    BG0, BG1 = bank[4], bank[5]
    BX, BT, BU = bank[6], bank[7], bank[5]
    BV1, BS, BO, BSS, BW0, BW1 = bank[6], bank[7], bank[0], bank[1], bank[2], bank[3]
    halves = [0, 1, 2, 4, 8, 16, 32, 64]

    def chunks(ap):
        return ap.rearrange("p (c i) -> p c i", c=4)

    def two(ap):
        return ap[:, 0:2 * P].rearrange("p (e i) -> p e i", e=2)

    def side(t, k):
        return t.rearrange("p c (n s h) -> p (c n) s h", s=2, h=32)[:, :, k, :]

    def side1(t, k):
        return t.rearrange("p (n s h) -> p n s h", s=2, h=32)[:, :, k, :]

    def parity(t, k):
        return t[:, :, :].rearrange("p (e k) i -> p e k i", k=2)[:, :, k, :]

    s_zero = new_semaphore(nc, T, "kda_zeroed")
    with nc.Block() as zero_block:
        @zero_block.vector
        def _(dve):
            dve.memset(Nf[:, :, :], 0.0).then_inc(s_zero, 1)
            dve.memset(Af[:, :, :], 0.0).then_inc(s_zero, 1)
            dve.memset(stack[:, :, :, :], 0.0).then_inc(s_zero, 1)
            dve.memset(Xw[:, :, :], 0.0).then_inc(s_zero, 1)
    prime_signals(nc, T)

    block = ctx.enter_context(nc.Block())


    @block.sync
    def _(sp):
        with sp.Fori(0, H) as h:
            sp.wait_ge(s_proj[5].sem, s_proj[5].at(h * NB2, 0))
            for m, name in enumerate(("Wq", "Wk", "Wv", "Wg")):
                sp.dma_start(w_proj[:, m, :, :], W[name].rearrange("(k p) n -> p k n", p=P)[:, :, bass.ds(h * P, P)]).then_inc(s_wproj.sem, 16)
            sp.dma_start(w_f2[:, :], W["Wf2"][:, bass.ds(h * P, P)]).then_inc(s_wproj.sem, 16)
            sp.wait_ge(s_wo.sem, s_wo.at(h * NB2, 0))
            sp.dma_start(w_out[:, :], W["Wo"][bass.ds(h * P, P), :]).then_inc(s_wout.sem, 16)

    @block.gpsimd
    def _(pool):
        def excess(n):
            pool.wait_ge(s_u.sem, s_u.at(n, 2))
            pool.tensor_tensor(ex[:, :], ex[:, :], K["forty"], ALU.subtract).then_inc(s_exc.sem, 1)
            pool.wait_ge(s_sp.sem, s_sp.at(n, 1))
            pool.wait_ge(s_exc.sem, s_exc.at(n, 1))
            pool.tensor_tensor(um[:, :], um[:, :], ex[:, :], ALU.add).then_inc(s_sp2.sem, 1)

        def level(n, i):
            if i == 0:
                pool.wait_ge(s_place.sem, s_place.at(n, 7))
            if i == 2:
                pool.wait_ge(s_ui.sem, s_ui.at(n, 1))
            elif i > 2:
                pool.wait_ge(s_x.sem, s_x.at(n, i - 2))
            pool.tensor_tensor(Nh[i % 2][:, :, :], Nf[:, :, :], K["level"][:, i:i + 1, :].broadcast_to([P, 4, P]), ALU.mult).then_inc(s_nh.sem, 1)

        excess(0)
        with pool.Fori(0, ITERS - 1) as n:
            for i in range(7):
                level(n, i)
            excess(n + 1)
        for i in range(7):
            level(ITERS - 1, i)

    @block.tensor
    def _(pe):
        def project(n, m):
            x0 = (n % NB2) * N
            xs = [xT[:, k, bass.ds(x0, N)] for k in range(2)]
            bk = (BQ, BK, BV)[m % 3]
            if m == 0:
                pe.wait_ge(s_wproj.sem, s_wproj.at(n // NB2, 80))
                pe.wait_ge(s_head.sem, s_head.at(n, 4))
            if m >= 3:
                pe.wait_ge(s_conv[m - 3].sem, s_conv[m - 3].at(n, 3))
            elif type(n) is not int and m == 0:
                pe.wait_ge(s_on1.sem, s_on1.at(n - 1, 0))
            elif type(n) is not int and m == 2:
                pe.wait_ge(s_acc.sem, s_acc.at(n - 1, 0))
            if m == 4:
                pe.matmul(bk, w_f2[:, :], f1T[:, bass.ds(x0, N)], start=True, stop=True).then_inc(s_proj[m].sem, 1)
                return
            lhs = w_beta if m == 5 else w_proj[:, m]
            pe.matmul(bk, lhs[:, 0, :], xs[0], start=True, stop=False)
            pe.matmul(bk, lhs[:, 1, :], xs[1], start=False, stop=True).then_inc(s_proj[m].sem, 1)

        def sumsq(n, m):
            pe.wait_ge(s_sq[m].sem, s_sq[m].at(n, 1))
            if m == 1:
                pe.wait_ge(s_z.sem, s_z.at(n, 1))
            pe.matmul((BN, BQ)[m], K["ones"][:, m, :], th[m][:, :], start=True, stop=True).then_inc(s_ss[m].sem, 1)

        def gram(n, i):
            g = halves[i]
            kq, kr = (KQ[0], KR[0]) if i == 0 else (KQ[i % 2], KR[(i - 1) % 2])
            out = (BG0, BG1)[i % 2]
            if i == 0:
                pe.wait_ge(s_kb.sem, s_kb.at(n, 1))
                pe.wait_ge(s_qn.sem, s_qn.at(n, 1))
            else:
                pe.wait_ge(s_kq.sem, s_kq.at(n, i))
                if i >= 2:
                    pe.wait_ge(s_kqc.sem, s_kqc.at(n, i - 1))
                    pe.wait_ge(s_kr.sem, s_kr.at(n, i - 1))
                    pe.wait_ge(s_krc.sem, s_krc.at(n, i - 1))
            if i >= 2:
                pe.wait_ge(s_mask.sem, s_mask.at(n, i - 1))
            if 1 <= g <= 16:
                for c in range(4):
                    for j0 in range(0, P, 32):
                        rhs = kq[:, :, c * P + j0:c * P + j0 + 32].rearrange("p a (n s h) -> p a n s h", s=2, h=g)[:, :, :, 1, :]
                        o = out[j0:j0 + 32, c * 32:(c + 1) * 32].rearrange("p (a n h) -> p a n h", a=2, h=g)
                        ins = pe.matmul(o, kr[:, c * P + j0:c * P + j0 + 32], rhs, start=True, stop=True)
                ins.then_inc(s_gram.sem, 1)
                return
            spans = {32: [(0, 32, 32), (64, 96, 32)], 64: [(0, 64, 64)]}.get(g, [(32 * j, 32 * j, 32) for j in range(4)])
            for c in range(4):
                t = c * P
                for j0, i0, w in spans:
                    o = out[j0:j0 + w, c * 2 * w:(c + 1) * 2 * w]
                    ins = pe.matmul(o.rearrange("p (a i) -> p a i", a=2), kr[:, t + j0:t + j0 + w], kq[:, :, t + i0:t + i0 + w], start=True, stop=True)
            ins.then_inc(s_gram.sem, 1)

        def turn(n):
            pe.wait_ge(s_place.sem, s_place.at(n, 14))
            for c in range(4):
                ins = pe.transpose(chunks(BG0)[:, c, :], chunks(vb[:, :])[:, c, :], K["ident"])
            ins.then_inc(s_vt.sem, 1)
            pe.wait_ge(s_kr.sem, s_kr.at(n, 7))
            pe.wait_ge(s_krc.sem, s_krc.at(n, 7))
            for e in range(2):
                ins = pe.transpose(two(BG1)[:, e, :], KRf[:, e, :], K["ident"])
            ins.then_inc(s_kt.sem, 1)

        def seed(n):
            pe.wait_ge(s_ui.sem, s_ui.at(n, 1))
            for c in range(4):
                ins = pe.transpose(chunks(BX)[:, c, :], U[:, c, :], K["ident"])
            ins.then_inc(s_tt.sem, 1)

        def grow_x(n, l):
            pe.wait_ge(s_nh.sem, s_nh.at(n, l + 2))
            if l == 0:
                pe.wait_ge(s_ti.sem, s_ti.at(n, 1))
            else:
                pe.wait_ge(s_tu.sem, s_tu.at(n, 2 * l - 1))
            for c in range(4):
                half = BX[:, 64 * c:64 * c + 64]
                if l == 5:
                    o, t = half, Ti[:, c, 0:64]
                elif l == 4:
                    o, t = half.rearrange("p (n h) -> p n h", h=32), side1(Ti[:, c, :], 0)
                else:
                    o, t = chunks(BX)[:, c, :], Ti[:, c, :]
                ins = pe.matmul(o, Nh[(l + 1) % 2][:, c, :], t, start=True, stop=True)
            ins.then_inc(s_x.sem, 1)

        def grow_t(n, l):
            pe.wait_ge(s_xs.sem, s_xs.at(n, l + 1))
            if l == 0:
                pe.wait_ge(s_ktc.sem, s_ktc.at(n, 1))
            else:
                pe.wait_ge(s_tu.sem, s_tu.at(n, 2 * l))
            if l == 5:
                for c in range(4):
                    ins = pe.matmul(BU[0:64, 64 * c:64 * c + 64], Xs[:, c, 0:64], U[:, c, 64:P], start=True, stop=True)
                ins.then_inc(s_tx.sem, 1)
                return
            if l == 4:
                joined = [b[:, 0:256].rearrange("p (c n h) -> p c n h", c=4, h=32) for b in (BT, BU)]
                for c in range(4):
                    ins = pe.matmul(joined[0][:, c, :, :], U[:, c, :], side1(Xw[:, c, :], 0), start=True, stop=True)
                ins.then_inc(s_tx.sem, 1)
                for c in range(4):
                    ins = pe.matmul(joined[1][:, c, :, :], Xw[:, c, :], side1(U[:, c, :], 1), start=True, stop=True)
                ins.then_inc(s_tx.sem, 1)
                return
            for c in range(4):
                ins = pe.matmul(chunks(BT)[:, c, :], U[:, c, :], Xs[:, c, :], start=True, stop=True)
            ins.then_inc(s_tx.sem, 1)
            for c in range(4):
                ins = pe.matmul(chunks(BU)[:, c, :], Xs[:, c, :], U[:, c, :], start=True, stop=True)
            ins.then_inc(s_tx.sem, 1)

        def v_even(n):
            pe.wait_ge(s_tu.sem, s_tu.at(n, 11))
            pe.wait_ge(s_vtc.sem, s_vtc.at(n, 1))
            for e in range(2):
                ins = pe.matmul(two(BV1)[:, e, :], U[:, 2 * e, :], vt[:, 2 * e, :], start=True, stop=True)
            ins.then_inc(s_v0.sem, 1)

        def state(n):
            pe.wait_ge(s_v0c.sem, s_v0c.at(n, 1))
            for e in range(2):
                ins = pe.matmul(two(BS)[:, e, :], kt[:, e, :], vp[:, 2 * e, :], start=True, stop=True)
            ins.then_inc(s_s.sem, 1)

        def read_state(n):
            pe.wait_ge(s_sc.sem, s_sc.at(n, 1))
            for e in range(2):
                ins = pe.matmul(two(BS)[:, e, :], KQf[:, 0, e, :], Ss[:, e, :], start=True, stop=True)
            ins.then_inc(s_yy.sem, 1)

        def v_odd(n):
            pe.wait_ge(s_r1.sem, s_r1.at(n, 1))
            for e in range(2):
                ins = pe.matmul(two(BV1)[:, e, :], U[:, 2 * e + 1, :], r1[:, e, :], start=True, stop=True)
            ins.then_inc(s_v1.sem, 1)

        def output(n):
            if type(n) is not int:
                pe.wait_ge(s_kn.sem, s_kn.at(n + 1, 1))
            for e in range(2):
                pe.matmul(chunks(BO)[:, 2 * e, :], vp[:, 2 * e, :], Af[:, 2 * e, :], start=True, stop=True)
            pe.wait_ge(s_v1c.sem, s_v1c.at(n, 1))
            for e in range(2):
                c = 2 * e + 1
                pe.matmul(chunks(BO)[:, c, :], vp[:, c, :], Af[:, c, :], start=True, stop=False)
                ins = pe.matmul(chunks(BO)[:, c, :], Ss[:, e, :], KQf[:, 1, e, :], start=False, stop=True)
            ins.then_inc(s_o.sem, 1)

        def o_sumsq(n):
            pe.wait_ge(s_osq.sem, s_osq.at(n, 1))
            if type(n) is not int:
                pe.wait_ge(s_u.sem, s_u.at(n + 1, 2))
            pe.matmul(BSS, K["ones"][:, 2, :], osq[:, :], start=True, stop=True).then_inc(s_oss.sem, 1)

        def project_out(n):
            pe.wait_ge(s_on.sem, s_on.at(n, 1))
            pe.wait_ge(s_wout.sem, s_wout.at(n // NB2, 16))
            if type(n) is not int:
                pe.wait_ge(s_tanh[4].sem, s_tanh[4].at(n + 1, 1))
                pe.wait_ge(s_qn.sem, s_qn.at(n + 1, 1))
            for c in range(4):
                o = (BW0, BW1)[c // 2][:, (c % 2) * D:(c % 2 + 1) * D]
                ins = pe.matmul(o, on[:, c * P:(c + 1) * P], w_out[:, :], start=True, stop=True)
            ins.then_inc(s_wo.sem, 1)

        LAST = ITERS - 1
        A1 = [lambda n, m=m: project(n, m) for m in range(6)] + [lambda n, m=m: sumsq(n, m) for m in range(2)]
        A2 = [lambda n, i=i: gram(n, i) for i in range(8)] + [turn]
        for step in A1 + A2:
            step(0)
        with pe.Fori(0, LAST) as n:
            m = n + 1
            seed(n); project(m, 0); grow_x(n, 0); project(m, 1); grow_t(n, 0)
            project(m, 2); grow_x(n, 1); project(m, 3); grow_t(n, 1)
            project(m, 4); grow_x(n, 2); project(m, 5); grow_t(n, 2)
            grow_x(n, 3); grow_t(n, 3)
            sumsq(m, 0); grow_x(n, 4); sumsq(m, 1); grow_t(n, 4)
            grow_x(n, 5); grow_t(n, 5)
            v_even(n); gram(m, 0); state(n); gram(m, 1); read_state(n); gram(m, 2); v_odd(n); gram(m, 3)
            output(n); gram(m, 4); gram(m, 5); o_sumsq(n); gram(m, 6); gram(m, 7); project_out(n); turn(m)
        seed(LAST)
        for l in range(6):
            grow_x(LAST, l)
            grow_t(LAST, l)
        for step in (v_even, state, read_state, v_odd, output, o_sumsq, project_out):
            step(LAST)

    @block.scalar
    def _(act):
        def tap(n, m):
            act.wait_ge(s_proj[m].sem, s_proj[m].at(n, 1))
            act.activation(y[m][:, :], (BQ, BK, BV)[m], ACT.Copy, scale=taps[:, m, KC - 1:KC]).then_inc(s_tap[m].sem, 1)

        def tanh(n, m):
            act.wait_ge(s_conv[m].sem, s_conv[m].at(n, 3))
            act.activation(th[m][:, :], y[m][:, :], ACT.Tanh, scale=0.5).then_inc(s_tanh[m].sem, 1)

        def tanh_zb(n):
            act.wait_ge(s_proj[3].sem, s_proj[3].at(n, 1))
            act.activation(tz[:, :], BQ, ACT.Tanh, scale=0.5, bias=head_c[:, 1:2]).then_inc(s_tanh[3].sem, 1)
            act.wait_ge(s_proj[5].sem, s_proj[5].at(n, 1))
            act.activation(beta[:, :], BV, ACT.Tanh, scale=0.5).then_inc(s_tanh[4].sem, 1)

        def square(n, m):
            act.wait_ge(s_silu[m].sem, s_silu[m].at(n, 1))
            act.activation(th[m][:, :], y[m][:, :], ACT.Square).then_inc(s_sq[m].sem, 1)

        def rsqrt(n, m):
            act.wait_ge(s_ss[m].sem, s_ss[m].at(n, 1))
            act.activation(th[m][:, :], (BN, BQ)[m], ACT.Ln, bias=K["eps"][:, m:m + 1]).then_inc(s_ln[m].sem, 1)
            act.wait_ge(s_ln[m].sem, s_ln[m].at(n, 1))
            act.activation((BN, BQ)[m], th[m][:, :], ACT.Exp, scale=-0.5).then_inc(s_rs[m].sem, 1)

        def softplus(n):
            act.wait_ge(s_u.sem, s_u.at(n, 1))
            act.activation(um[:, :], um[:, :], ACT.Exp).then_inc(s_eu.sem, 1)
            act.wait_ge(s_eu.sem, s_eu.at(n, 1))
            act.activation(um[:, :], um[:, :], ACT.Ln, bias=1.0).then_inc(s_sp.sem, 1)

        def decay(n):
            act.wait_ge(s_sp2.sem, s_sp2.at(n, 1))
            act.activation(gate[:, :], um[:, :], ACT.Exp, scale=head_c[:, 3:4]).then_inc(s_gate.sem, 1)

        def keep(n, s):
            half = 1 << (s - 1)
            src, dst = KQ[s % 2], KQ[(s + 1) % 2]
            act.wait_ge(s_kq.sem, s_kq.at(n, s))
            if s < 7:
                act.wait_ge(s_gram.sem, s_gram.at(n, s))
            else:
                act.wait_ge(s_o.sem, s_o.at(n, 0))
            if s > 1:
                act.wait_ge(s_kqc.sem, s_kqc.at(n, s - 1))
            if s < 7:
                v = lambda t: t[:, :, :].rearrange("p a (n s h) -> p a n s h", s=2, h=half)[:, :, :, 0, :]
                act.copy(v(dst), v(src)).then_inc(s_kqc.sem, 1)
            else:
                act.copy(KQf[:, :, :, 0:half], src[:, :, :].rearrange("p a (e k i) -> p a e k i", k=2, i=P)[:, :, :, 1, 0:half]).then_inc(s_kqc.sem, 1)
            src, dst = KR[(s + 1) % 2], KR[s % 2]
            if s > 1:
                act.wait_ge(s_kr.sem, s_kr.at(n, s - 1))
                act.wait_ge(s_krc.sem, s_krc.at(n, s - 1))
            if s < 7:
                v = lambda t: t[:, :].rearrange("p (n s h) -> p n s h", s=2, h=half)[:, :, 1, :]
                act.copy(v(dst), v(src)).then_inc(s_krc.sem, 1)
            else:
                act.copy(KRf[:, :, half:P], src[:, :].rearrange("p (e k i) -> p e k i", k=2, i=P)[:, :, 0, half:P]).then_inc(s_krc.sem, 1)

        def place(n):
            act.wait_ge(s_near.sem, s_near.at(n, 1))
            act.wait_ge(s_nh.sem, s_nh.at(n, 0))
            act.wait_ge(s_o.sem, s_o.at(n, 0))
            for a, dst in enumerate((Nf, Af)):
                for j in range(4):
                    q = slice(32 * j, 32 * j + 32)
                    act.copy(dst[q, :, q], near[q, :, 32 * a:32 * a + 32]).then_inc(s_place.sem, 1)
                for i, (j0, i0, w) in ((6, (0, 32, 32)), (6, (64, 96, 32)), (7, (0, 64, 64))):
                    act.wait_ge(s_gram.sem, s_gram.at(n, i + 1))
                    g = (BG0, BG1)[i % 2][j0:j0 + w, 0:8 * w].rearrange("p (c a i) -> p c a i", c=4, a=2)
                    act.copy(dst[j0:j0 + w, :, i0:i0 + w], g[:, :, a, :]).then_inc(s_place.sem, 1)

        def turned(n):
            act.wait_ge(s_vt.sem, s_vt.at(n, 1))
            act.copy(vt[:, :, :], chunks(BG0)).then_inc(s_vtc.sem, 1)
            act.wait_ge(s_kt.sem, s_kt.at(n, 1))
            act.copy(kt[:, :, :], two(BG1)).then_inc(s_ktc.sem, 1)

        def seed(n):
            act.wait_ge(s_tt.sem, s_tt.at(n, 1))
            act.copy(Ti[:, :, :], chunks(BX)).then_inc(s_ti.sem, 1)

        def copy_x(n, l):
            act.wait_ge(s_x.sem, s_x.at(n, l + 1))
            if l == 4:
                dst, src = side(Xw[:, :, :], 0), BX[:, 0:256].rearrange("p (m h) -> p m h", h=32)
            elif l == 5:
                dst, src = Xs[:, :, 0:64], BX[:, 0:256].rearrange("p (c i) -> p c i", c=4)
            else:
                dst, src = Xs[:, :, :], chunks(BX)
            act.copy(dst, src).then_inc(s_xs.sem, 1)

        def v_even(n):
            act.wait_ge(s_v0.sem, s_v0.at(n, 1))
            act.copy(parity(vp, 0), two(BV1)).then_inc(s_v0c.sem, 1)

        def state(n):
            act.wait_ge(s_s.sem, s_s.at(n, 1))
            act.copy(Ss[:, :, :], two(BS)).then_inc(s_sc.sem, 1)

        def v_odd(n):
            act.wait_ge(s_v1.sem, s_v1.at(n, 1))
            act.copy(parity(vp, 1), two(BV1)).then_inc(s_v1c.sem, 1)

        def o_square(n):
            act.wait_ge(s_o.sem, s_o.at(n, 1))
            act.activation(osq[:, :], BO, ACT.Square).then_inc(s_osq.sem, 1)

        def o_rsqrt(n):
            act.wait_ge(s_oss.sem, s_oss.at(n, 1))
            act.activation(orms[:, :], BSS, ACT.Ln, bias=K["eps"][:, 2:3]).then_inc(s_oln.sem, 1)
            act.wait_ge(s_oln.sem, s_oln.at(n, 1))
            act.activation(orms[:, :], orms[:, :], ACT.Exp, scale=-0.5).then_inc(s_ors.sem, 1)

        LAST = ITERS - 1
        for m in range(3):
            tap(0, m)
            tanh(0, m)
        tanh_zb(0)
        square(0, 0); square(0, 1)
        act.preload_act_table_set("natural_log_exp_and_others")
        rsqrt(0, 0); rsqrt(0, 1); softplus(0); decay(0)
        for s in range(1, 8):
            keep(0, s)
        place(0); turned(0)
        with act.Fori(0, LAST) as n:
            m = n + 1
            act.preload_act_table_set("exp_and_others")
            seed(n); tap(m, 0); tap(m, 1); copy_x(n, 0); tanh(m, 0); copy_x(n, 1)
            tap(m, 2); tanh(m, 1); copy_x(n, 2); tanh(m, 2); tanh_zb(m)
            copy_x(n, 3); square(m, 0); square(m, 1); copy_x(n, 4)
            act.preload_act_table_set("natural_log_exp_and_others")
            softplus(m); rsqrt(m, 0); copy_x(n, 5); rsqrt(m, 1); decay(m)
            v_even(n); keep(m, 1); state(n); keep(m, 2); v_odd(n); keep(m, 3); keep(m, 4)
            o_square(n); keep(m, 5); keep(m, 6); o_rsqrt(n); keep(m, 7)
            place(m); turned(m)
        seed(LAST)
        for l in range(6):
            copy_x(LAST, l)
        for step in (v_even, state, v_odd, o_square, o_rsqrt):
            step(LAST)

    @block.vector
    def _(dve):
        def head(n):
            h = n // NB2
            dve.wait_ge(s_gate.sem, s_gate.at(n, 0))
            dve.wait_ge(s_proj[5].sem, s_proj[5].at(n, 0))
            dve.tensor_scalar(taps[:, :, :].rearrange("p m k -> p (m k)"), K["conv"][:, bass.ds(h, 1), :].rearrange("p a k -> p (a k)"), 1.0, None, ALU.mult).then_inc(s_head.sem, 1)
            dve.tensor_scalar(head_c[:, :], K["heads"][:, bass.ds(h, 1), :].rearrange("p a k -> p (a k)"), 1.0, None, ALU.mult).then_inc(s_head.sem, 1)
            for k in range(2):
                dve.tensor_scalar(w_beta[:, k, :], K["wb"][:, k, bass.ds(h, 1)].broadcast_to([P, P]), 1.0, None, ALU.mult).then_inc(s_head.sem, 1)
            dve.wait_ge(s_head.sem, s_head.at(n, 4))

        def conv(n, m):
            for j in range(1, KC):
                if j == 1:
                    dve.wait_ge(s_tap[m].sem, s_tap[m].at(n, 1))
                else:
                    dve.wait_ge(s_conv[m].sem, s_conv[m].at(n, j - 1))
                src = (BQ, BK, BV)[m].rearrange("p (e t) -> p e t", e=2)[:, :, 0:TB - j]
                dst = y[m][:, :].rearrange("p (e t) -> p e t", e=2)[:, :, j:TB]
                dve.scalar_tensor_tensor(dst, src, taps[:, m, KC - 1 - j:KC - j], dst, ALU.mult, ALU.add).then_inc(s_conv[m].sem, 1)

        def clamp_u(n):
            dve.wait_ge(s_proj[4].sem, s_proj[4].at(n, 1))
            dve.tensor_scalar(um[:, :], BK, head_c[:, 2:3], 40.0, ALU.add, ALU.min).then_inc(s_u.sem, 1)
            dve.tensor_scalar(ex[:, :], BK, head_c[:, 2:3], 40.0, ALU.add, ALU.max).then_inc(s_u.sem, 1)

        def silu(n, m):
            dve.wait_ge(s_tanh[m].sem, s_tanh[m].at(n, 1))
            dve.scalar_tensor_tensor(y[m][:, :], th[m][:, :], 1.0, y[m][:, :], ALU.add, ALU.mult).then_inc(s_silu[m].sem, 1)

        def z_scale(n):
            dve.wait_ge(s_tanh[3].sem, s_tanh[3].at(n, 1))
            dve.tensor_scalar(za[:, :], BQ, head_c[:, 0:1], K["onw"][:, 0:1], ALU.add, ALU.mult).then_inc(s_z.sem, 1)

        def beta_v(n):
            dve.wait_ge(s_tanh[4].sem, s_tanh[4].at(n, 1))
            dve.tensor_scalar(beta[:, :], beta[:, :], 0.5, 0.5, ALU.mult, ALU.add).then_inc(s_beta.sem, 1)
            dve.wait_ge(s_beta.sem, s_beta.at(n, 1))
            dve.wait_ge(s_silu[2].sem, s_silu[2].at(n, 1))
            dve.scalar_tensor_tensor(vb[:, :], y[2][:, :], 0.5, beta[:, :], ALU.mult, ALU.mult).then_inc(s_vb.sem, 1)

        def norm_q(n):
            dve.wait_ge(s_rs[0].sem, s_rs[0].at(n, 1))
            dve.tensor_tensor(KQ[0][:, 1, :], BN, y[0][:, :], ALU.mult).then_inc(s_qn.sem, 1)

        def norm_k(n):
            dve.wait_ge(s_rs[1].sem, s_rs[1].at(n, 1))
            dve.tensor_tensor(KR[0][:, :], BQ, y[1][:, :], ALU.mult).then_inc(s_kn.sem, 1)
            dve.wait_ge(s_kn.sem, s_kn.at(n, 1))
            dve.tensor_tensor(KQ[0][:, 0, :], KR[0][:, :], beta[:, :], ALU.mult).then_inc(s_kb.sem, 1)
            dve.wait_ge(s_kb.sem, s_kb.at(n, 1))
            dve.wait_ge(s_qn.sem, s_qn.at(n, 1))
            dve.wait_ge(s_gate.sem, s_gate.at(n, 1))
            dve.tensor_tensor(KQ[1][:, :, :], KQ[0][:, :, :], gate[:, :].rearrange("p (a t) -> p a t", a=1).broadcast_to([P, 2, N]), ALU.mult).then_inc(s_kq.sem, 1)

        def level(n, s):
            half = 1 << (s - 1)
            nb = N // (2 * half)
            t2 = tot(half).rearrange("p (n s) -> p n s", s=2)
            if s > 1:
                dve.wait_ge(s_tot.sem, s_tot.at(n, s - 1))
            if s < 7:
                dve.tensor_tensor(tot(2 * half), t2[:, :, 0], t2[:, :, 1], ALU.mult).then_inc(s_tot.sem, 1)
            src, dst = KR[(s + 1) % 2], KR[s % 2]
            if s > 1:
                dve.wait_ge(s_kr.sem, s_kr.at(n, s - 1))
                dve.wait_ge(s_krc.sem, s_krc.at(n, s - 1))
            if s < 7:
                dve.wait_ge(s_gram.sem, s_gram.at(n, s))
                v = lambda t: t[:, :].rearrange("p (n s h) -> p n s h", s=2, h=half)[:, :, 0, :]
                dve.tensor_tensor(v(dst), v(src), t2[:, :, 1:2].broadcast_to([P, nb, half]), ALU.mult).then_inc(s_kr.sem, 1)
            else:
                v = src[:, :].rearrange("p (e k i) -> p e k i", k=2, i=P)[:, :, 0, 0:half]
                dve.tensor_tensor(KRf[:, :, 0:half], v, t2[:, 0:nb:2, 1:2].broadcast_to([P, 2, half]), ALU.mult).then_inc(s_kr.sem, 1)
            src, dst = KQ[s % 2], KQ[(s + 1) % 2]
            dve.wait_ge(s_kq.sem, s_kq.at(n, s))
            if s > 1:
                dve.wait_ge(s_kqc.sem, s_kqc.at(n, s - 1))
            if s == 7:
                dve.wait_ge(s_o.sem, s_o.at(n, 0))
            for a in range(2):
                if s < 7:
                    v = lambda t: t[:, a, :].rearrange("p (n s h) -> p n s h", s=2, h=half)[:, :, 1, :]
                    ins = dve.tensor_tensor(v(dst), v(src), t2[:, :, 0:1].broadcast_to([P, nb, half]), ALU.mult)
                else:
                    v = src[:, a, :].rearrange("p (e k i) -> p e k i", k=2, i=P)[:, :, 1, half:P]
                    ins = dve.tensor_tensor(KQf[:, a, :, half:P], v, t2[:, 1:nb:2, 0:1].broadcast_to([P, 2, half]), ALU.mult)
            ins.then_inc(s_kq.sem, 1)

        def mask(n, i):
            dve.wait_ge(s_gram.sem, s_gram.at(n, i + 1))
            keep = K["near"][:, i:i + 1, :]
            if i == 0:
                g = BG0[:, 0:256].rearrange("p (c x) -> p c x", c=4)
                dve.tensor_tensor(stack[:, i, :, :], g, keep.broadcast_to([P, 4, 64]), ALU.mult).then_inc(s_mask.sem, 1)
                return
            right = lambda t: t.rearrange("p c (m s h) -> p c m s h", s=2, h=halves[i])[:, :, :, 1, :]
            g = (BG0, BG1)[i % 2][:, 0:128].rearrange("p (c m h) -> p c m h", c=4, h=halves[i])
            dve.tensor_tensor(right(stack[:, i, :, :]), g, right(keep).broadcast_to([P, 4, 32 // halves[i], halves[i]]), ALU.mult).then_inc(s_mask.sem, 1)

        def near_sum(n):
            dve.wait_ge(s_mask.sem, s_mask.at(n, 6))
            dve.tensor_reduce(near[:, :, :], stack[:, :, :, :].rearrange("p l c x -> p c x l"), AX.X, ALU.add).then_inc(s_near.sem, 1)

        def z_gate(n):
            dve.wait_ge(s_z.sem, s_z.at(n, 1))
            dve.wait_ge(s_on.sem, s_on.at(n, 0))
            dve.scalar_tensor_tensor(zz[:, :], tz[:, :], 1.0, za[:, :], ALU.add, ALU.mult).then_inc(s_gz.sem, 1)

        def seed(n):
            dve.wait_ge(s_nh.sem, s_nh.at(n, 1))
            dve.tensor_tensor(U[:, :, :], K["ident"].rearrange("p (a i) -> p a i", a=1).broadcast_to([P, 4, P]), Nh[0][:, :, :], ALU.subtract).then_inc(s_ui.sem, 1)

        def grow(n, l):
            dve.wait_ge(s_tx.sem, s_tx.at(n, 2 * l + 1))
            if l == 0:
                dve.wait_ge(s_ti.sem, s_ti.at(n, 1))
                dve.wait_ge(s_ui.sem, s_ui.at(n, 1))
            else:
                dve.wait_ge(s_tu.sem, s_tu.at(n, 2 * l))
            if l == 5:
                u = U[0:64, :, 64:P]
                dve.tensor_tensor(u, u, BU[0:64, 0:256].rearrange("p (c i) -> p c i", c=4), ALU.subtract).then_inc(s_tu.sem, 1)
                return
            for dst, by, k in ((Ti, BT, 0), (U, BU, 1)):
                if l == 4:
                    t, by = side(dst[:, :, :], k), by[:, 0:256].rearrange("p (m h) -> p m h", h=32)
                else:
                    t, by = dst[:, :, :], chunks(by)
                if k == 1:
                    dve.wait_ge(s_tx.sem, s_tx.at(n, 2 * l + 2))
                dve.tensor_tensor(t, t, by, ALU.subtract).then_inc(s_tu.sem, 1)

        def rhs_odd(n):
            dve.wait_ge(s_yy.sem, s_yy.at(n, 1))
            dve.tensor_tensor(r1[:, :, :], parity(vt, 1), two(BS), ALU.subtract).then_inc(s_r1.sem, 1)

        def gate_o(n):
            dve.wait_ge(s_ors.sem, s_ors.at(n, 1))
            dve.tensor_tensor(on[:, :], orms[:, :], BO, ALU.mult).then_inc(s_on1.sem, 1)
            dve.wait_ge(s_on1.sem, s_on1.at(n, 1))
            dve.wait_ge(s_gz.sem, s_gz.at(n, 1))
            dve.tensor_tensor(on[:, :], on[:, :], zz[:, :], ALU.mult).then_inc(s_on.sem, 1)

        def add_out(n):
            dve.wait_ge(s_wo.sem, s_wo.at(n, 1))
            for e in range(2):
                xs = xres[:, bass.ds((n % NB2) * 4 + 2 * e, 2), :]
                dve.tensor_tensor(xs, xs, (BW0, BW1)[e].rearrange("p (a d) -> p a d", a=2), ALU.add).then_inc(s_acc.sem, 1)

        LAST = ITERS - 1
        head(0)
        for m in range(3):
            conv(0, m)
        clamp_u(0)
        z_scale(0)
        for m in range(3):
            silu(0, m)
        beta_v(0); norm_q(0); norm_k(0)
        for s in range(1, 8):
            level(0, s)
            if s <= 6:
                mask(0, s - 1)
        near_sum(0); z_gate(0); seed(0)
        with dve.Fori(0, LAST) as n:
            m = n + 1
            head(m)
            conv(m, 0); grow(n, 0); conv(m, 1); grow(n, 1); conv(m, 2); grow(n, 2)
            clamp_u(m); z_scale(m); silu(m, 0); silu(m, 1); grow(n, 3)
            silu(m, 2); beta_v(m); grow(n, 4); norm_q(m); grow(n, 5)
            norm_k(m); level(m, 1); mask(m, 0); level(m, 2); rhs_odd(n); mask(m, 1)
            level(m, 3); mask(m, 2); level(m, 4); mask(m, 3); level(m, 5); mask(m, 4)
            level(m, 6); mask(m, 5); near_sum(m); level(m, 7); gate_o(n); z_gate(m)
            seed(m)
            add_out(n)
        for l in range(6):
            grow(LAST, l)
        rhs_odd(LAST); gate_o(LAST); add_out(LAST)


def norm_phase(nc, ctx, T, K, name, dst, affine=None, out=None):
    def sb(n, shape):
        return ctx.enter_context(nc.sbuf_tensor(f"{name}_{n}", shape, F32))

    def sem(n):
        return new_semaphore(nc, T, f"{name}_{n}")

    xres, xT, bank = T["xres"], T["xT"], T["bank"]
    stats, mv = sb("stats", [P, NT, 6]), sb("mv", [P, NT, 2])
    rstd, shift = sb("rstd", [P, NT]), sb("shift", [P, NT])
    stats_done, mv_done, ln_done, rstd_done, shift_done = (sem(s) for s in ("stats", "mv", "ln", "rstd", "shift"))
    even_done, odd_done, turned, copied, stored = (sem(s) for s in ("even", "odd", "turned", "copied", "stored"))
    block = ctx.enter_context(nc.Block())

    @block.vector
    def _(dve):
        for t in range(NT):
            dve.bn_stats(stats[:, t, :], xres[:, t, :]).then_inc(stats_done, 1)
        for t in range(NT):
            dve.wait_ge(stats_done, t + 1)
            dve.bn_aggr(mv[:, t, :], stats[:, t, :]).then_inc(mv_done, 1)
        dve.wait_ge(mv_done, NT)
        dve.wait_ge(rstd_done, 1)
        dve.scalar_tensor_tensor(shift[:, :], mv[:, :, 0], -1.0, rstd[:, :], ALU.mult, ALU.mult).then_inc(shift_done, 1)
        for t in range(0, NT, 2):
            dve.tensor_scalar(dst[:, t, :], xres[:, t, :], mv[:, t, 0:1], rstd[:, t:t + 1], ALU.subtract, ALU.mult).then_inc(even_done, 1)
        if out is None and affine is None:
            for g in range(NT // 4):
                dve.wait_ge(turned, 2 * g + 1)
                dve.tensor_copy(xT[:, 0, g * 512:(g + 1) * 512], bank[(2 * g) % 8]).then_inc(copied, 1)

    @block.scalar
    def _(act):
        act.preload_act_table_set("natural_log_exp_and_others")
        act.wait_ge(mv_done, NT)
        act.activation(rstd[:, :], mv[:, :, 1], ACT.Ln, bias=K["eps"][:, 2:3]).then_inc(ln_done, 1)
        act.wait_ge(ln_done, 1)
        act.activation(rstd[:, :], rstd[:, :], ACT.Exp, scale=-0.5).then_inc(rstd_done, 1)
        act.wait_ge(shift_done, 1)
        for t in range(1, NT, 2):
            act.activation(dst[:, t, :], xres[:, t, :], ACT.Identity, bias=shift[:, t:t + 1], scale=rstd[:, t:t + 1]).then_inc(odd_done, 1)
        if out is None:
            for g in range(NT // 4):
                for k in range(2):
                    if affine is None and k == 0:
                        continue
                    act.wait_ge(turned, 2 * g + k + 1)
                    d = xT[:, k, g * 512:(g + 1) * 512]
                    if affine is None:
                        act.copy(d, bank[(2 * g + k) % 8]).then_inc(copied, 1)
                    else:
                        act.activation(d, bank[(2 * g + k) % 8], ACT.Identity, scale=K[affine][:, k:k + 1], bias=K[affine][:, 2 + k:3 + k]).then_inc(copied, 1)

    @block.tensor
    def _(pe):
        if out is None:
            for g in range(NT // 4):
                pe.wait_ge(even_done, 2 * g + 2)
                pe.wait_ge(odd_done, 2 * g + 2)
                for k in range(2):
                    for t in range(4):
                        ins = pe.transpose(bank[(2 * g + k) % 8][:, t * P:(t + 1) * P], dst[:, 4 * g + t, k * P:(k + 1) * P], K["ident"])
                    ins.then_inc(turned, 1)

    @block.sync
    def _(sp):
        if out is not None:
            for g in range(NT // 4):
                sp.wait_ge(even_done, 2 * g + 2)
                sp.wait_ge(odd_done, 2 * g + 2)
                sp.dma_start(out[:, 4 * g:4 * g + 4, :], dst[:, 4 * g:4 * g + 4, :]).then_inc(stored, 16)
            sp.wait_ge(stored, 16 * NT // 4)


def route_phase(nc, ctx, T, K, name, experts, softmax_of_top, scale, add_input=False):
    def sb(n, shape, dt=F32):
        return ctx.enter_context(nc.sbuf_tensor(f"{name}_{n}", shape, dt))

    def sem(n):
        return new_semaphore(nc, T, f"{name}_{n}")

    xT, bank, comb = T["xT"], T["bank"], T["comb"]
    wr = K[name + "_wr"]
    lg, pr, hot = sb("lg", [P, NT, E8]), sb("pr", [P, NT, E8]), sb("hot", [P, NT, E8])
    mx, top, at, atf = sb("mx", [P, NT]), sb("top", [P, NT, 8]), sb("at", [P, NT, 8], U32), sb("atf", [P, NT, 8])
    w = sb("w", [P, 2, NT])
    logits_done, chain, expd, two_exp = sem("logits"), sem("chain"), sem("exp"), sem("exp2")
    block = ctx.enter_context(nc.Block())
    L = bank[0][:, 0:NT * experts].rearrange("p (t e) -> p t e", e=experts)

    def wide(a, e):
        return a.rearrange("p (t a) -> p t a", a=1).broadcast_to([P, NT, e])

    @block.gpsimd
    def _(pool):
        if add_input:
            added = sem("input_added")
            for i in range(4):
                q = slice(4 * i, 4 * i + 4)
                pool.tensor_tensor(T["xres"][:, q, :], T["xres"][:, q, :], T["x_in"][:, q, :], ALU.add).then_inc(added, 1)

    @block.tensor
    def _(pe):
        for t in range(NT):
            for k in range(2):
                ins = pe.matmul(L[:, t, :], xT[:, k, t * P:(t + 1) * P], wr[:, k, 0:experts], start=(k == 0), stop=(k == 1))
        ins.then_inc(logits_done, 1)

    @block.scalar
    def _(act):
        act.wait_ge(chain, 3)
        act.activation(pr[:, :, 0:experts], lg[:, :, 0:experts], ACT.Exp).then_inc(expd, 1)
        if softmax_of_top:
            act.wait_ge(chain, 6 + 2 * NT + 1)
            act.activation(w[:, 1, :], w[:, 0, :], ACT.Exp).then_inc(two_exp, 1)

    @block.vector
    def _(dve):
        done = [0]

        def step(ins):
            ins.then_inc(chain, 1)
            done[0] += 1
            dve.wait_ge(chain, done[0])

        step(dve.memset(pr[:, :, :], -1.0))
        dve.wait_ge(logits_done, 1)
        step(dve.tensor_reduce(mx[:, :], L, AX.X, ALU.max))
        step(dve.tensor_tensor(lg[:, :, 0:experts], L, wide(mx[:, :], experts), ALU.subtract))
        dve.wait_ge(expd, 1)
        step(dve.tensor_reduce(mx[:, :], pr[:, :, 0:experts], AX.X, ALU.add))
        step(dve.reciprocal(mx[:, :], mx[:, :]))
        step(dve.tensor_tensor(pr[:, :, 0:experts], pr[:, :, 0:experts], wide(mx[:, :], experts), ALU.mult))
        for t in range(NT):
            dve.max(top[:, t, :], pr[:, t, :]).then_inc(chain, 1)
        dve.wait_ge(chain, 6 + NT)
        for t in range(NT):
            dve.max_index(at[:, t, :], top[:, t, :], pr[:, t, :]).then_inc(chain, 1)
        done[0] += 2 * NT
        dve.wait_ge(chain, done[0])
        if softmax_of_top:
            step(dve.tensor_tensor(w[:, 0, :], top[:, :, 1], top[:, :, 0], ALU.subtract))
            dve.wait_ge(two_exp, 1)
            step(dve.tensor_scalar(mx[:, :], w[:, 1, :], 1.0, None, ALU.add))
            step(dve.reciprocal(mx[:, :], mx[:, :]))
            step(dve.tensor_scalar(w[:, 0, :], mx[:, :], scale, None, ALU.mult))
            step(dve.tensor_tensor(w[:, 1, :], w[:, 1, :], w[:, 0, :], ALU.mult))
        else:
            step(dve.tensor_tensor(mx[:, :], top[:, :, 1], top[:, :, 0], ALU.add))
            step(dve.reciprocal(mx[:, :], mx[:, :]))
            step(dve.tensor_scalar(mx[:, :], mx[:, :], scale, None, ALU.mult))
            for i in range(2):
                step(dve.tensor_tensor(w[:, i, :], top[:, :, i], mx[:, :], ALU.mult))
        step(dve.tensor_copy(atf[:, :, :], at[:, :, :]))
        iota = K["iota"].rearrange("p (a e) -> p a e", a=1).broadcast_to([P, NT, E8])
        for i, d in enumerate((comb, hot)):
            step(dve.tensor_tensor(d[:, :, :], iota, atf[:, :, i:i + 1].broadcast_to([P, NT, E8]), ALU.is_equal))
            step(dve.tensor_tensor(d[:, :, :], d[:, :, :], wide(w[:, i, :], E8), ALU.mult))
        step(dve.tensor_tensor(comb[:, :, :], comb[:, :, :], hot[:, :, :], ALU.add))


def expert_phase(nc, ctx, T, K, W, name, experts, F, glu):
    def sb(n, shape):
        return ctx.enter_context(nc.sbuf_tensor(f"{name}_{n}", shape, F32))

    def signal(n, per, dma=False):
        return new_signal(nc, T, f"{name}_{n}", per, dma)

    xT, xres, comb, bank = T["xT"], T["xres"], T["comb"], T["bank"]
    FT = F // P
    up = 2 if glu else 1
    TBL = TOK // 512
    w_in = [sb(f"w_in{s}", [P, up, 2, F]) for s in range(2)]
    w_dn = [sb(f"w_dn{s}", [P, FT, D]) for s in range(2)]
    b_dn = [sb(f"b_dn{s}", [P, D]) for s in range(2)]
    b_in = sb("b_in", [P, experts, FT])
    th = [sb(f"th{s}", [P, 512]) for s in range(2)]
    hid = sb("hid", [P, FT, 512])
    landed = [signal(f"landed{s}", 16 * 3, dma=True) for s in range(2)]
    s_in, s_act, s_g, s_hid = signal("in", FT), signal("act", FT), signal("g", FT), signal("hid", FT)
    s_dn = [signal(f"down{s}", 2) for s in range(2)]
    s_add = signal("added", 4)
    prime_signals(nc, T)
    block = ctx.enter_context(nc.Block())

    def pairs(eng, body):
        if glu:
            with eng.Fori(0, experts // 2) as e2:
                body(e2)
        else:
            for e2 in range(experts // 2):
                body(e2)

    @block.sync
    def _(sp):
        def load(e2):
            for s in range(2):
                e = e2 * 2 + s
                sp.wait_ge(s_dn[s].sem, s_dn[s].at(e2 * TBL, 0))
                if glu:
                    for i, m in enumerate(("gate", "up")):
                        sp.dma_start(w_in[s][:, i, :, :], W[m][bass.ds(e, 1), :, :].rearrange("a (k p) f -> p (a k) f", p=P)).then_inc(landed[s].sem, 16)
                else:
                    sp.dma_start(w_in[s][:, 0, :, :], W["up"][e, :, :].rearrange("(k p) f -> p k f", p=P)).then_inc(landed[s].sem, 16)
                    sp.dma_start(b_dn[s][0:1, :], W["b_dn"][e:e + 1, :]).then_inc(landed[s].sem, 16)
                sp.dma_start(w_dn[s][:, :, :], W["down"][bass.ds(e, 1), :, :].rearrange("a (f p) d -> p (a f) d", p=P)).then_inc(landed[s].sem, 16)
        pairs(sp, load)

    @block.tensor
    def _(pe):
        read = s_hid if glu else s_act

        def enter(e2, s, tb, f, early=False):
            n = (e2 * 2 + s) * TBL + tb
            if f == 0:
                pe.wait_ge(landed[s].sem, landed[s].at(e2, landed[s].per))
            pe.wait_ge(read.sem, read.at(n, f - 1 if early or f else 0))
            for i, o in enumerate((bank[f % 2], bank[2 + f % 2])[:up]):
                for k in range(2):
                    x = xT[:, k, bass.ds(tb * 512, 512)] if type(tb) is not int else xT[:, k, tb * 512:(tb + 1) * 512]
                    ins = pe.matmul(o, w_in[s][:, i, k, f * P:(f + 1) * P], x, start=(k == 0), stop=(k == 1))
            ins.then_inc(s_in.sem, 1)

        def leave(e2, s, tb):
            n = (e2 * 2 + s) * TBL + tb
            pe.wait_ge(read.sem, read.at(n, FT))
            pe.wait_ge(s_add.sem, s_add.at(n, 0))
            for t in range(4):
                o = bank[4 + t][:, 0:D]
                for f in range(FT):
                    ins = pe.matmul(o, hid[:, f, t * P:(t + 1) * P], w_dn[s][:, f, :], start=(f == 0), stop=(glu and f == FT - 1))
                if not glu:
                    ins = pe.matmul(o, K["onerow"], b_dn[s][0:1, :], start=False, stop=True)
                if t % 2:
                    ins.then_inc(s_dn[s].sem, 1)

        def work(e2):
            for s in range(2):
                enter(e2, s, 0, 0)
                with pe.Fori(0, TBL - 1) as tb:
                    for f in range(1, FT):
                        enter(e2, s, tb, f)
                    enter(e2, s, tb + 1, 0, early=True)
                    leave(e2, s, tb)
                for f in range(1, FT):
                    enter(e2, s, TBL - 1, f)
                leave(e2, s, TBL - 1)
        pairs(pe, work)

    @block.scalar
    def _(act):
        def work(e2):
            for s in range(2):
                with act.Fori(0, TBL) as tb:
                    n = (e2 * 2 + s) * TBL + tb
                    for f in range(FT):
                        act.wait_ge(s_in.sem, s_in.at(n, f + 1))
                        if glu:
                            act.activation(th[f % 2][:, :], bank[f % 2], ACT.Tanh, scale=0.5).then_inc(s_act.sem, 1)
                        else:
                            if f == 0:
                                act.wait_ge(s_add.sem, s_add.at(n, 0))
                            act.activation(hid[:, f, :], bank[f % 2], ACT.Gelu, bias=K["be1"][:, e2 * 2 + s, f:f + 1]).then_inc(s_act.sem, 1)
        pairs(act, work)

    @block.vector
    def _(dve):
        def work(e2):
            for s in range(2):
                with dve.Fori(0, TBL) as tb:
                    n = (e2 * 2 + s) * TBL + tb
                    if glu:
                        for f in range(FT):
                            dve.wait_ge(s_act.sem, s_act.at(n, f + 1))
                            dve.scalar_tensor_tensor(th[f % 2][:, :], th[f % 2][:, :], 1.0, bank[f % 2], ALU.add, ALU.mult).then_inc(s_g.sem, 1)
                            dve.wait_ge(s_g.sem, s_g.at(n, f + 1))
                            dve.tensor_tensor(hid[:, f, :], th[f % 2][:, :], bank[2 + f % 2], ALU.mult).then_inc(s_hid.sem, 1)
                    for t in range(4):
                        if t % 2 == 0:
                            dve.wait_ge(s_dn[s].sem, s_dn[s].at(e2 * TBL + tb, t // 2 + 1))
                        row = xres[:, bass.ds(tb * 4 + t, 1), :].rearrange("p a d -> p (a d)")
                        c = comb[:, :, :].rearrange("p t e -> p (t e)")[:, bass.ds(tb * (4 * E8) + e2 * 2 + (t * E8 + s), 1)]
                        dve.scalar_tensor_tensor(row, bank[4 + t][:, 0:D], c, row, ALU.mult, ALU.add).then_inc(s_add.sem, 1)
        pairs(dve, work)


def gqa_phase(nc, ctx, T, K):
    def sb(n, shape):
        return ctx.enter_context(nc.sbuf_tensor(f"gqa_{n}", shape, F32))

    def signal(n, per, dma=False):
        return new_signal(nc, T, f"gqa_{n}", per, dma)

    xT, xres, bank = T["xT"], T["xres"], T["bank"]
    wqkv, wo = K["gqa_qkv"], K["gqa_out"]
    QW, KW = NH1 * HD1, NKV * HD1
    xs = sb("xs", [P, 2, TB])
    sq, ss = sb("sq", [P, QW]), sb("ss", [P, 4])
    t1, t2, t3 = sb("t1", [P, 4, QW]), sb("t2", [P, 4, QW]), sb("zero", [P, 1])
    qpad, kpad = sb("qpad", [P, 2, G1, NKV, 32]), sb("kpad", [P, 2, NKV, 32])
    v1 = sb("v1", [P, 2, NKV, HD1 + 1])
    qT, kT = sb("qT", [P, G1, TB]), sb("kT", [P, TB])
    pT = [sb(f"pT{i}", [P, 2, 512]) for i in range(4)]
    rec, enc, encT = sb("rec", [P, 2, NH1]), sb("enc", [P, 2, QW]), sb("encT", [P, 2, TB])
    s_pad = signal("pads_zeroed", 4)
    s_xs, s_qkv, s_ssq, s_ln, s_rs = signal("xs", 2), signal("qkv", 2), signal("sumsq", 4), signal("ln", 2), signal("rsqrt", 1)
    s_v, s_t1, s_t2, s_rope = signal("v", 2), signal("t1", 4), signal("t2", 8), signal("rope", 4)
    s_qt, s_kt, s_qtc, s_ktc = signal("q_turned", 2), signal("k_turned", 1), signal("q_copied", 2), signal("k_copied", 1)
    s_sc, s_ex, s_pv = signal("scores", 16), signal("exp", 16), signal("pv", 8)
    s_rec, s_enc, s_et, s_etc = signal("rec", 2), signal("enc", 2), signal("enc_turned", 1), signal("enc_copied", 1)
    s_out, s_add = signal("out", 1), signal("added", 1)
    prime_signals(nc, T)
    block = ctx.enter_context(nc.Block())
    heads = lambda a: a.rearrange("p (h d) -> p h d", d=HD1)

    @block.tensor
    def _(pe):
        pe.wait_ge(s_pad.sem, s_pad.at(0, 4))
        with pe.Fori(0, B) as n:
            pe.wait_ge(s_xs.sem, s_xs.at(n, 2))
            for t in range(2):
                for k in range(2):
                    ins = pe.matmul(bank[t][:, 0:384], xs[:, k, t * P:(t + 1) * P], wqkv[:, k, :], start=(k == 0), stop=(k == 1))
                ins.then_inc(s_qkv.sem, 1)
            pe.wait_ge(s_rope.sem, s_rope.at(n, 4))
            pe.wait_ge(s_v.sem, s_v.at(n, 2))
            for g2 in range(2):
                for g in range(2):
                    for t in range(2):
                        ins = pe.transpose(bank[2 + g2][:, (g * 2 + t) * P:(g * 2 + t + 1) * P], qpad[:, t, 2 * g2 + g, :, :].rearrange("p a b -> p (a b)"), K["ident"])
                ins.then_inc(s_qt.sem, 1)
            for t in range(2):
                ins = pe.transpose(bank[4][:, t * P:(t + 1) * P], kpad[:, t, :, :].rearrange("p a b -> p (a b)"), K["ident"])
            ins.then_inc(s_kt.sem, 1)
            pe.wait_ge(s_qtc.sem, s_qtc.at(n, 2))
            pe.wait_ge(s_ktc.sem, s_ktc.at(n, 1))

            def score(u):
                for s in range(2):
                    for kp in range(2):
                        j, kk = 4 * u + 2 * s + kp, 2 * (u // 2) + kp
                        r = slice(32 * kk, 32 * kk + 32)
                        if j >= 4:
                            pe.wait_ge(s_ex.sem, s_ex.at(n, j - 3))
                        pe.matmul(bank[2 + j % 4], kT[r, s * P:(s + 1) * P], qT[r, 2 * (u % 2):2 * (u % 2) + 2, :].rearrange("p g t -> p (g t)"), start=True, stop=True).then_inc(s_sc.sem, 1)

            def mix(u, kp):
                kk, g2 = 2 * (u // 2) + kp, u % 2
                pe.wait_ge(s_ex.sem, s_ex.at(n, 4 * u + kp + 3))
                for g in range(2):
                    head = kk * G1 + 2 * g2 + g
                    for t in range(2):
                        for s in range(2):
                            ins = pe.matmul(bank[6 + t][:, head * 17:head * 17 + 17], pT[2 * (u % 2) + kp][:, s, g * TB + t * P:g * TB + (t + 1) * P], v1[:, s, kk, :], start=(s == 0), stop=(s == 1))
                ins.then_inc(s_pv.sem, 1)

            score(0)
            for u in range(4):
                if u < 3:
                    score(u + 1)
                mix(u, 0)
                mix(u, 1)
            pe.wait_ge(s_enc.sem, s_enc.at(n, 2))
            for k in range(2):
                for t in range(2):
                    ins = pe.transpose(bank[0][:, (k * 2 + t) * P:(k * 2 + t + 1) * P], enc[:, t, k * P:(k + 1) * P], K["ident"])
            ins.then_inc(s_et.sem, 1)
            pe.wait_ge(s_etc.sem, s_etc.at(n, 1))
            for t in range(2):
                for k in range(2):
                    ins = pe.matmul(bank[1][:, t * D:(t + 1) * D], encT[:, k, t * P:(t + 1) * P], wo[:, k, :], start=(k == 0), stop=(k == 1))
            ins.then_inc(s_out.sem, 1)

    @block.scalar
    def _(act):
        act.preload_act_table_set("natural_log_exp_and_others")
        with act.Fori(0, B) as n:
            for t in range(2):
                act.wait_ge(s_qkv.sem, s_qkv.at(n, t + 1))
                if t > 0:
                    act.wait_ge(s_ssq.sem, s_ssq.at(n, 2 * t))
                act.activation(sq[:, :], bank[t][:, 0:QW], ACT.Square, accum_out=ss[:, t:t + 1]).then_inc(s_ssq.sem, 1)
                act.wait_ge(s_ssq.sem, s_ssq.at(n, 2 * t + 1))
                act.activation(sq[:, 0:KW], bank[t][:, QW:QW + KW], ACT.Square, accum_out=ss[:, 2 + t:3 + t]).then_inc(s_ssq.sem, 1)
            act.wait_ge(s_ssq.sem, s_ssq.at(n, 4))
            act.activation(ss[:, 0:2], ss[:, 0:2], ACT.Ln, scale=1.0 / QW, bias=K["eps"][:, 3:4]).then_inc(s_ln.sem, 1)
            act.activation(ss[:, 2:4], ss[:, 2:4], ACT.Ln, scale=1.0 / KW, bias=K["eps"][:, 3:4]).then_inc(s_ln.sem, 1)
            act.wait_ge(s_ln.sem, s_ln.at(n, 2))
            act.activation(ss[:, :], ss[:, :], ACT.Exp, scale=-0.5).then_inc(s_rs.sem, 1)
            for t in range(2):
                act.copy(v1[:, t, :, 0:HD1], bank[t][:, QW + KW:QW + 2 * KW].rearrange("p (k d) -> p k d", d=HD1)).then_inc(s_v.sem, 1)
            for g2 in range(2):
                act.wait_ge(s_qt.sem, s_qt.at(n, g2 + 1))
                act.copy(qT[:, 2 * g2:2 * g2 + 2, :].rearrange("p g t -> p (g t)"), bank[2 + g2]).then_inc(s_qtc.sem, 1)
            act.wait_ge(s_kt.sem, s_kt.at(n, 1))
            act.copy(kT[:, :], bank[4][:, 0:TB]).then_inc(s_ktc.sem, 1)
            for j in range(16):
                u, s, kp = j // 4, j % 4 // 2, j % 2
                act.wait_ge(s_sc.sem, s_sc.at(n, j + 1))
                if u >= 2:
                    act.wait_ge(s_pv.sem, s_pv.at(n, 2 * u + kp - 3))
                act.activation(pT[2 * (u % 2) + kp][:, s, :], bank[2 + j % 4], ACT.Exp, scale=float(HD1) ** -0.5).then_inc(s_ex.sem, 1)
            act.wait_ge(s_et.sem, s_et.at(n, 1))
            act.copy(encT[:, :, :].rearrange("p k t -> p (k t)"), bank[0]).then_inc(s_etc.sem, 1)

    @block.vector
    def _(dve):
        dve.memset(qpad[:, :, :, :, :], 0.0).then_inc(s_pad.sem, 1)
        dve.memset(kpad[:, :, :, :], 0.0).then_inc(s_pad.sem, 1)
        dve.memset(v1[:, :, :, :], 1.0).then_inc(s_pad.sem, 1)
        dve.wait_ge(s_pad.sem, s_pad.at(0, 3))
        dve.memset(t3[:, :], 0.0).then_inc(s_pad.sem, 1)
        half = HD1 // 2
        with dve.Fori(0, B) as n:
            for k in range(2):
                dve.tensor_scalar(xs[:, k, :], xT[:, k, bass.ds(n * TB, TB)], 1.0, None, ALU.mult).then_inc(s_xs.sem, 1)
            dve.wait_ge(s_rs.sem, s_rs.at(n, 1))
            dve.wait_ge(s_v.sem, s_v.at(n, 2))
            for j in range(4):
                t, isk = j % 2, j // 2
                w = KW if isk else QW
                nh = w // HD1
                src = heads(bank[t][:, QW:QW + KW] if isk else bank[t][:, 0:QW])
                r = ss[:, j:j + 1]
                cos = K["rope16"][:, t:t + 1, 0:HD1].broadcast_to([P, nh, HD1])
                sin = K["rope16"][:, t:t + 1, HD1:2 * HD1]
                dve.scalar_tensor_tensor(heads(t1[:, j, 0:w]), src, r, cos, ALU.mult, ALU.mult).then_inc(s_t1.sem, 1)
                for s in range(2):
                    o, i = slice(s * half, (s + 1) * half), slice((1 - s) * half, (2 - s) * half)
                    dve.scalar_tensor_tensor(heads(t2[:, j, 0:w])[:, :, o], src[:, :, i], r, sin[:, :, o].broadcast_to([P, nh, half]), ALU.mult, ALU.mult).then_inc(s_t2.sem, 1)
            for j in range(4):
                t, isk = j % 2, j // 2
                dve.wait_ge(s_t1.sem, s_t1.at(n, 4))
                dve.wait_ge(s_t2.sem, s_t2.at(n, 8))
                if isk:
                    dve.tensor_tensor(kpad[:, t, :, 0:HD1], heads(t1[:, j, 0:KW]), heads(t2[:, j, 0:KW]), ALU.add).then_inc(s_rope.sem, 1)
                else:
                    v = lambda a: a[:, j, :].rearrange("p (k g d) -> p g k d", k=NKV, g=G1)
                    dve.tensor_tensor(qpad[:, t, :, :, 0:HD1], v(t1), v(t2), ALU.add).then_inc(s_rope.sem, 1)
            dve.wait_ge(s_pv.sem, s_pv.at(n, 8))
            for t in range(2):
                o = bank[6 + t][:, 0:NH1 * 17].rearrange("p (h d) -> p h d", d=17)
                dve.reciprocal(rec[:, t, :], o[:, :, 16]).then_inc(s_rec.sem, 1)
            for t in range(2):
                o = bank[6 + t][:, 0:NH1 * 17].rearrange("p (h d) -> p h d", d=17)
                dve.wait_ge(s_rec.sem, s_rec.at(n, 2))
                dve.tensor_tensor(heads(enc[:, t, :]), o[:, :, 0:HD1], rec[:, t, :].rearrange("p (h a) -> p h a", a=1).broadcast_to([P, NH1, HD1]), ALU.mult).then_inc(s_enc.sem, 1)
            dve.wait_ge(s_out.sem, s_out.at(n, 1))
            x = xres[:, bass.ds(n * 2, 2), :]
            dve.tensor_tensor(x, x, bank[1].rearrange("p (t d) -> p t d", t=2), ALU.add).then_inc(s_add.sem, 1)


def mha_phase(nc, ctx, T, K, W):
    def sb(n, shape):
        return ctx.enter_context(nc.sbuf_tensor(f"mha_{n}", shape, F32))

    def signal(n, per, dma=False):
        return new_signal(nc, T, f"mha_{n}", per, dma)

    xT, xres, bank = T["xT"], T["xres"], T["bank"]
    NG = H2 // HG
    GW = HG * HD2
    wm = [sb(f"w{m}", [P, 2, H2 * HD2]) for m in "qkv"]
    wo = sb("wo", [P, H2, D])
    bias = sb("bias", [P, 3, GW])
    rb = sb("rb", [P, 2, 2, GW])
    xs = sb("xs", [P, 2, TB])
    t1, t2 = [sb(f"t1_{j}", [P, GW]) for j in range(4)], [sb(f"t2_{j}", [P, GW]) for j in range(2)]
    v = sb("v", [P, 2, GW])
    qT, kT = sb("qT", [P, HG, TB]), sb("kT", [P, HG, TB])
    sc0, sc1 = sb("sc0", [P, HG, P]), sb("sc1", [P, HG, TB])
    mx, sm = sb("mx", [P, 2 * HG]), sb("sm", [P, 2 * HG])
    pt = sb("pt", [P, HG, 3, P])
    oT = sb("oT", [P, HG, TB])
    s_w, s_bias, s_xs = signal("weights", 64, dma=True), signal("bias", 48, dma=True), signal("xs", 2)
    s_qkv, s_t1, s_t2 = signal("qkv", 6), signal("t1", 4), signal("t2", 8)
    s_r1, s_r2, s_rb, s_rbt = signal("rope", 4), signal("rope_bias", 4), signal("rb", 4), signal("rbt", 12)
    s_v = signal("v", 2)
    s_tq, s_tqc = signal("turned", 4), signal("turned_copied", 4)
    s_s, s_sm, s_mx, s_neg, s_e = signal("scores", 3), signal("masked", 3), signal("max", 2), signal("neg", 1), signal("exp", 8)
    s_rec, s_p = signal("rec", 1), signal("probs", 8)
    s_pt, s_ptc, s_o, s_oc = signal("probs_turned", 3), signal("probs_copied", 3), signal("o", 2), signal("o_copied", 2)
    s_out, s_add = signal("out", 1), signal("added", 1)
    prime_signals(nc, T)
    block = ctx.enter_context(nc.Block())
    rows = lambda a, j=HG: a.rearrange("p (h d) -> p h d", h=j)

    @block.sync
    def _(sp):
        for m, name in enumerate(("wq", "wk", "wv")):
            sp.dma_start(wm[m][:, :, :], W[name].rearrange("(k p) n -> p k n", p=P)).then_inc(s_w.sem, 16)
        sp.dma_start(wo[:, :, :], W["wo"].rearrange("(h p) n -> p h n", p=P)).then_inc(s_w.sem, 16)
        with sp.Fori(0, NG) as g:
            sp.wait_ge(s_add.sem, s_add.at(g * B, 0))
            for m, name in enumerate(("bq", "bk", "bv")):
                sp.dma_start(bias[:, m, :], W[name][:, bass.ds(g * GW, GW)].broadcast_to([P, GW])).then_inc(s_bias.sem, 16)

    def over(eng, first, both, last, before=None):
        with eng.Fori(0, NG) as g:
            if before is not None:
                before(g)
            first(g, 0)
            with eng.Fori(0, B - 1) as b:
                both(g, b)
            last(g, B - 1)

    @block.tensor
    def _(pe):
        def project(g, b, m):
            n = g * B + b
            if m == 0:
                pe.wait_ge(s_xs.sem, s_xs.at(n, 2))
                pe.wait_ge(s_tqc.sem, s_tqc.at(n, 0))
            elif m == 1:
                pe.wait_ge(s_sm.sem, s_sm.at(n, 0))
            else:
                pe.wait_ge(s_v.sem, s_v.at(n, 0))
            for t in range(2):
                for k in range(2):
                    ins = pe.matmul(bank[2 * m + t], xs[:, k, t * P:(t + 1) * P], wm[m][:, k, bass.ds(g * GW, GW)], start=(k == 0), stop=(k == 1))
                ins.then_inc(s_qkv.sem, 1)

        def turn(n):
            for j in range(4):
                m, hh = j // 2, j % 2
                if hh == 0:
                    pe.wait_ge(s_r2.sem, s_r2.at(n, 2 * m + 2))
                if j >= 2:
                    pe.wait_ge(s_tqc.sem, s_tqc.at(n, j - 1))
                for h in range(2):
                    for t in range(2):
                        ins = pe.transpose(bank[hh][:, (h * 2 + t) * P:(h * 2 + t + 1) * P], t1[2 * m + t][:, (2 * hh + h) * P:(2 * hh + h + 1) * P], K["ident"])
                ins.then_inc(s_tq.sem, 1)

        def scores(n):
            pe.wait_ge(s_tqc.sem, s_tqc.at(n, 4))
            pe.wait_ge(s_v.sem, s_v.at(n, 2))
            for h in range(HG):
                ins = pe.matmul(rows(bank[2])[:, h, :], qT[:, h, 0:P], kT[:, h, 0:P], start=True, stop=True)
            ins.then_inc(s_s.sem, 1)
            for hh in range(2):
                for h in range(2):
                    ins = pe.matmul(bank[3 + hh][:, h * TB:(h + 1) * TB], qT[:, 2 * hh + h, P:TB], kT[:, 2 * hh + h, :], start=True, stop=True)
                ins.then_inc(s_s.sem, 1)

        def turn_probs(n):
            for j in range(3):
                pe.wait_ge(s_p.sem, s_p.at(n, 4 if j == 0 else 8))
                if j == 0:
                    pe.wait_ge(s_oc.sem, s_oc.at(n, 0))
                elif j == 1:
                    pe.wait_ge(s_add.sem, s_add.at(n, 0))
                else:
                    pe.wait_ge(s_ptc.sem, s_ptc.at(n, 1))
                for h in range(HG):
                    src = sc0[:, h, :] if j == 0 else sc1[:, h, (j - 1) * P:j * P]
                    ins = pe.transpose(bank[6 + j % 2][:, h * P:(h + 1) * P], src, K["ident"])
                ins.then_inc(s_pt.sem, 1)

        def mix(n):
            for hh in range(2):
                pe.wait_ge(s_ptc.sem, s_ptc.at(n, 3))
                for h in range(2):
                    i = 2 * hh + h
                    o = bank[6 + hh][:, h * TB:(h + 1) * TB]
                    pe.matmul(o, v[:, 0, i * P:(i + 1) * P], pt[:, i, 0:2, :].rearrange("p a t -> p (a t)"), start=True, stop=False)
                    ins = pe.matmul(o[:, P:TB], v[:, 1, i * P:(i + 1) * P], pt[:, i, 2, :], start=False, stop=True)
                ins.then_inc(s_o.sem, 1)

        def project_out(g, n):
            pe.wait_ge(s_oc.sem, s_oc.at(n, 2))
            for t in range(2):
                for h in range(HG):
                    ins = pe.matmul(bank[7][:, t * D:(t + 1) * D], oT[:, h, t * P:(t + 1) * P], wo[:, bass.ds(g * HG + h, 1), :].rearrange("p a d -> p (a d)"), start=(h == 0), stop=(h == HG - 1))
            ins.then_inc(s_out.sem, 1)

        def first(g, b):
            for m in range(3):
                project(g, b, m)
            turn(g * B + b)

        def both(g, b):
            n = g * B + b
            scores(n)
            for m in range(3):
                project(g, b + 1, m)
            turn_probs(n)
            mix(n)
            turn(n + 1)
            project_out(g, n)

        def last(g, b):
            n = g * B + b
            scores(n); turn_probs(n); mix(n); project_out(g, n)

        pe.wait_ge(s_w.sem, s_w.at(0, 64))
        over(pe, first, both, last)

    @block.gpsimd
    def _(pool):
        with pool.Fori(0, NG * B) as n:
            for j in range(4):
                pool.wait_ge(s_t1.sem, s_t1.at(n, j + 1))
                pool.wait_ge(s_t2.sem, s_t2.at(n, 2 * j + 2))
                pool.tensor_tensor(t1[j][:, :], t1[j][:, :], t2[j % 2][:, :], ALU.add).then_inc(s_r1.sem, 1)
                pool.wait_ge(s_r1.sem, s_r1.at(n, j + 1))
                pool.tensor_tensor(t1[j][:, :], t1[j][:, :], rb[:, j // 2, j % 2, :], ALU.add).then_inc(s_r2.sem, 1)

    @block.scalar
    def _(act):
        def copy_turned(n):
            for j in range(4):
                act.wait_ge(s_tq.sem, s_tq.at(n, j + 1))
                d = (qT, kT)[j // 2][:, 2 * (j % 2):2 * (j % 2) + 2, :].rearrange("p h t -> p (h t)")
                act.copy(d, bank[j % 2]).then_inc(s_tqc.sem, 1)

        def attend(n):
            act.wait_ge(s_neg.sem, s_neg.at(n, 1))
            for t in range(2):
                for h in range(HG):
                    s = (sc0, sc1)[t][:, h, :]
                    i = t * HG + h
                    act.activation(s, s, ACT.Exp, bias=mx[:, i:i + 1], accum_out=sm[:, i:i + 1]).then_inc(s_e.sem, 1)
            for j in range(3):
                act.wait_ge(s_pt.sem, s_pt.at(n, j + 1))
                act.copy(pt[:, :, j, :], rows(bank[6 + j % 2])).then_inc(s_ptc.sem, 1)
            for hh in range(2):
                act.wait_ge(s_o.sem, s_o.at(n, hh + 1))
                act.copy(oT[:, 2 * hh:2 * hh + 2, :].rearrange("p h t -> p (h t)"), bank[6 + hh]).then_inc(s_oc.sem, 1)

        def both(g, b):
            attend(g * B + b)
            copy_turned(g * B + (b + 1))

        over(act, lambda g, b: copy_turned(g * B + b), both, lambda g, b: attend(g * B + b))

    @block.vector
    def _(dve):
        half = HD2 // 2
        cos = [K["rope128"][:, t:t + 1, 0:HD2].broadcast_to([P, HG, HD2]) for t in range(2)]
        sin = [[K["rope128"][:, t:t + 1, HD2 + s * half:HD2 + (s + 1) * half].broadcast_to([P, HG, half]) for s in range(2)] for t in range(2)]

        def turn(dst1, dst2, src, t, c_sem, s_sem):
            dve.tensor_tensor(rows(dst1), rows(src), cos[t], ALU.mult).then_inc(c_sem, 1)
            for s in range(2):
                o, i = slice(s * half, (s + 1) * half), slice((1 - s) * half, (2 - s) * half)
                dve.tensor_tensor(rows(dst2)[:, :, o], rows(src)[:, :, i], sin[t][s], ALU.mult).then_inc(s_sem, 1)

        def turn_biases(g):
            dve.wait_ge(s_bias.sem, s_bias.at(g, 48))
            dve.wait_ge(s_r2.sem, s_r2.at(g * B, 0))
            for j in range(4):
                if j >= 1:
                    dve.wait_ge(s_rb.sem, s_rb.at(g, j))
                turn(rb[:, j // 2, j % 2, :], t2[j % 2][:, :], bias[:, j // 2, :], j % 2, s_rbt.sem, s_rbt.sem)
                dve.wait_ge(s_rbt.sem, s_rbt.at(g, 3 * j + 3))
                dve.tensor_tensor(rb[:, j // 2, j % 2, :], rb[:, j // 2, j % 2, :], t2[j % 2][:, :], ALU.add).then_inc(s_rb.sem, 1)

        def fix_x(g, b):
            for k in range(2):
                if k == 0:
                    dve.wait_ge(s_rb.sem, s_rb.at(g, 4))
                dve.tensor_scalar(xs[:, k, :], xT[:, k, bass.ds(b * TB, TB)], 1.0, None, ALU.mult).then_inc(s_xs.sem, 1)

        def rope(n, m):
            for j in (2 * m, 2 * m + 1):
                dve.wait_ge(s_qkv.sem, s_qkv.at(n, j + 1))
                if j >= 2:
                    dve.wait_ge(s_r1.sem, s_r1.at(n, j - 1))
                turn(t1[j][:, :], t2[j % 2][:, :], bank[j], j % 2, s_t1.sem, s_t2.sem)

        def values(n):
            dve.wait_ge(s_o.sem, s_o.at(n, 0))
            for t in range(2):
                dve.wait_ge(s_qkv.sem, s_qkv.at(n, 5 + t))
                dve.tensor_tensor(v[:, t, :], bias[:, 2, :], bank[4 + t], ALU.add).then_inc(s_v.sem, 1)

        def maxima(n):
            tri = K["causal"].rearrange("p (a t) -> p a t", a=1)
            dve.wait_ge(s_s.sem, s_s.at(n, 1))
            dve.scalar_tensor_tensor(sc0[:, :, :], rows(bank[2]), float(HD2) ** -0.5, tri[:, :, P:2 * P].broadcast_to([P, HG, P]), ALU.mult, ALU.add).then_inc(s_sm.sem, 1)
            for hh in range(2):
                dve.wait_ge(s_s.sem, s_s.at(n, hh + 2))
                dve.scalar_tensor_tensor(sc1[:, 2 * hh:2 * hh + 2, :], rows(bank[3 + hh], 2), float(HD2) ** -0.5, tri.broadcast_to([P, 2, TB]), ALU.mult, ALU.add).then_inc(s_sm.sem, 1)
            dve.wait_ge(s_sm.sem, s_sm.at(n, 3))
            dve.tensor_reduce(mx[:, 0:HG], sc0[:, :, :], AX.X, ALU.max).then_inc(s_mx.sem, 1)
            dve.tensor_reduce(mx[:, HG:2 * HG], sc1[:, :, :], AX.X, ALU.max).then_inc(s_mx.sem, 1)
            dve.wait_ge(s_mx.sem, s_mx.at(n, 2))
            dve.tensor_scalar(mx[:, :], mx[:, :], -1.0, None, ALU.mult).then_inc(s_neg.sem, 1)

        def probs(n):
            dve.wait_ge(s_e.sem, s_e.at(n, 8))
            dve.reciprocal(sm[:, :], sm[:, :]).then_inc(s_rec.sem, 1)
            dve.wait_ge(s_rec.sem, s_rec.at(n, 1))
            for i in range(8):
                s = (sc0, sc1)[i // HG][:, i % HG, :]
                dve.tensor_scalar(s, s, sm[:, i:i + 1], None, ALU.mult).then_inc(s_p.sem, 1)

        def add_out(g, b):
            n = g * B + b
            dve.wait_ge(s_out.sem, s_out.at(n, 1))
            x = xres[:, bass.ds(b * 2, 2), :] if type(b) is not int else xres[:, 2 * b:2 * b + 2, :]
            dve.tensor_tensor(x, x, bank[7].rearrange("p (t d) -> p t d", t=2), ALU.add).then_inc(s_add.sem, 1)

        def first(g, b):
            n = g * B + b
            fix_x(g, b); rope(n, 0); rope(n, 1); values(n)

        def both(g, b):
            n = g * B + b
            fix_x(g, b + 1); maxima(n); rope(n + 1, 0); probs(n); rope(n + 1, 1); values(n + 1); add_out(g, b)

        def last(g, b):
            n = g * B + b
            maxima(n); probs(n); add_out(g, b)

        over(dve, first, both, last, turn_biases)


def _const_layout():
    widths = [("ident", P), ("ones", 3 * P), ("eps", 4), ("forty", N), ("level", 7 * P), ("near", 6 * 64), ("iota", E8),
              ("causal", TB), ("rope16", 2 * 2 * HD1), ("rope128", 2 * 2 * HD2)]
    at, out = 0, {}
    for name, w in widths:
        out[name] = (at, w)
        at += w
    return out, at


def two_layers(nc, W, const, out):
    with ExitStack() as ctx:
        def sb(name, shape, dt=F32):
            return ctx.enter_context(nc.sbuf_tensor(name, shape, dt))

        psum = ctx.enter_context(nc.psum_tensor("psum", [P, 8, 512], F32))
        T = {"semaphores": [], "unprimed": [], "bank": [psum[:, i, :] for i in range(8)], "xres": sb("xres", [P, NT, D]), "xT": sb("xT", [P, 2, TOK]), "comb": sb("comb", [P, NT, E8])}
        layout, width = _const_layout()
        table = sb("table", [P, width])
        K = {k: table[:, a:a + w] for k, (a, w) in layout.items()}
        K["onerow"] = K["ones"][0:1, P:2 * P]
        K["ones"] = K["ones"].rearrange("p (m i) -> p m i", m=3)
        K["level"] = K["level"].rearrange("p (l i) -> p l i", l=7)
        K["near"] = K["near"].rearrange("p (l i) -> p l i", l=6)
        K["rope16"] = K["rope16"].rearrange("p (t i) -> p t i", t=2)
        K["rope128"] = K["rope128"].rearrange("p (t i) -> p t i", t=2)
        K["ln1"], K["ln2"] = sb("ln1", [P, 4]), sb("ln2", [P, 4])
        K["r0_wr"], K["r1_wr"] = sb("r0_wr", [P, 2, E0]), sb("r1_wr", [P, 2, E1])
        K["gqa_qkv"], K["gqa_out"] = sb("gqa_qkv", [P, 2, 384]), sb("gqa_out", [P, 2, D])
        K["be1"] = sb("be1", [P, E1, F1 // P])
        xdram = W["x"].rearrange("(t p) d -> p t d", p=P)
        bo = sb("bo", [P, D])
        loads = [(T["xres"][:, 4 * i:4 * i + 4, :], xdram[:, 4 * i:4 * i + 4, :]) for i in range(4)]
        loads += [(table[:, :], const)]
        loads += [(bo[:, :], W["bo"].broadcast_to([P, D]))]
        for m, wb in (("ln1", ("ln1_w", "ln1_b")), ("ln2", ("ln2_w", "ln2_b"))):
            for i, a in enumerate(wb):
                loads.append((K[m][:, 2 * i:2 * i + 2], W[a]))
        loads += [(K["r0_wr"][:, :, :], W["gate_w"].rearrange("(k p) e -> p k e", p=P)),
                  (K["r1_wr"][:, :, :], W["w_gate"].rearrange("(k p) e -> p k e", p=P)),
                  (K["gqa_out"][:, :, :], W["out_kernel"].rearrange("(k p) e -> p k e", p=P)),
                  (K["be1"][:, :, :], W["be1"])]
        for name, a, w in (("q_kernel", 0, 256), ("k_kernel", 256, 64), ("v_kernel", 320, 64)):
            loads.append((K["gqa_qkv"][:, :, a:a + w], W[name].rearrange("(k p) e -> p k e", p=P)))

        with ExitStack() as c1:
            def sb1(name, shape):
                return c1.enter_context(nc.sbuf_tensor(name, shape, F32))

            K["conv"], K["heads"], K["wb"] = sb1("conv", [P, H, 3 * KC]), sb1("heads", [P, H, 4]), sb1("wb", [P, 2, H])
            K["onw"], T["f1T"] = sb1("onw", [P, 1]), sb1("f1T", [P, TOK])
            w_f1, alog, bg, dt_bias = sb1("w_f1", [P, 2, P]), sb1("alog", [P, H]), sb1("bg", [P, H]), sb1("dt_bias", [P, H])
            loads += [(w_f1[:, :, :], W["Wf1"].rearrange("(k p) e -> p k e", p=P)), (K["wb"][:, :, :], W["Wb"].rearrange("(k p) e -> p k e", p=P)),
                      (alog[:, :], W["A_log"].broadcast_to([P, H])), (K["onw"][:, :], W["o_norm_w"]),
                      (bg[:, :], W["bg"]), (dt_bias[:, :], W["dt_bias"])]
            for m, name in enumerate(("conv_q", "conv_k", "conv_v")):
                loads.append((K["conv"][:, :, m * KC:(m + 1) * KC], W[name].rearrange("(h p) k -> p h k", p=P)))
            with ExitStack() as c2:
                landed, turned, copied = (new_semaphore(nc, T, s) for s in ("inputs_landed", "x_turned", "x_copied"))
                f1_done, f1_copied, a_exp, prep = (new_semaphore(nc, T, s) for s in ("f1_done", "f1_copied", "a_exp", "prep"))
                block = c2.enter_context(nc.Block())
                bank, xT = T["bank"], T["xT"]

                @block.sync
                def _(sp):
                    for d, s in loads:
                        sp.dma_start(d, s).then_inc(landed, 16)

                @block.tensor
                def _(pe):
                    pe.wait_ge(landed, 16 * len(loads))
                    for i in range(8):
                        for t in range(4):
                            ins = pe.transpose(bank[i][:, t * P:(t + 1) * P], T["xres"][:, 4 * (i // 2) + t, (i % 2) * P:(i % 2 + 1) * P], K["ident"])
                        ins.then_inc(turned, 1)
                    for i in range(4):
                        pe.wait_ge(copied, 8)
                        for k in range(2):
                            ins = pe.matmul(bank[i], w_f1[:, k, :], xT[:, k, i * 512:(i + 1) * 512], start=(k == 0), stop=(k == 1))
                        ins.then_inc(f1_done, 1)

                @block.scalar
                def _(act):
                    for i in range(8):
                        act.wait_ge(turned, i + 1)
                        act.copy(xT[:, i % 2, (i // 2) * 512:(i // 2 + 1) * 512], bank[i]).then_inc(copied, 1)
                    act.activation(alog[:, :], alog[:, :], ACT.Exp).then_inc(a_exp, 1)
                    for i in range(4):
                        act.wait_ge(f1_done, i + 1)
                        act.copy(T["f1T"][:, i * 512:(i + 1) * 512], bank[i]).then_inc(f1_copied, 1)

                @block.vector
                def _(dve):
                    dve.wait_ge(landed, 16 * len(loads))
                    hd = K["heads"]
                    for i, (src, by) in enumerate(((bg, 1.0), (bg, 0.5), (dt_bias, 1.0))):
                        dve.tensor_scalar(hd[:, :, i], src[:, :], by, None, ALU.mult).then_inc(prep, 1)
                    dve.tensor_scalar(K["onw"][:, :], K["onw"][:, :], 0.5, None, ALU.mult).then_inc(prep, 1)
                    dve.wait_ge(a_exp, 1)
                    dve.tensor_scalar(hd[:, :, 3], alog[:, :], -1.0, None, ALU.mult).then_inc(prep, 1)
            with ExitStack() as c2:
                kda_phase(nc, c2, T, W, K)
        reuse_semaphores(nc, T)
        with ExitStack() as c2:
            norm_phase(nc, c2, T, K, "norm0", T["xres"])
        with ExitStack() as c2:
            route_phase(nc, c2, T, K, "r0", E0, False, 0.5)
        with ExitStack() as c2:
            expert_phase(nc, c2, T, K, {"gate": W["moe0_gate"], "up": W["moe0_up"], "down": W["moe0_down"]}, "moe0", E0, F0, True)
        with ExitStack() as c2:
            norm_phase(nc, c2, T, K, "norm1", T["xres"])
        with ExitStack() as c2:
            gqa_phase(nc, c2, T, K)
        reuse_semaphores(nc, T)
        with ExitStack() as c2:
            norm_phase(nc, c2, T, K, "norm2", T["xres"])
        with ExitStack() as c2:
            xn = c2.enter_context(nc.sbuf_tensor("xn1", [P, NT, D], F32))
            norm_phase(nc, c2, T, K, "ln1", xn, affine="ln1")
        T["x_in"] = sb("x_in", [P, NT, D])
        with ExitStack() as c2:
            x_kept, bo_added = (new_semaphore(nc, T, s) for s in ("x_kept", "bo_added"))
            block = c2.enter_context(nc.Block())

            @block.scalar
            def _(act):
                act.copy(T["x_in"][:, :, :], T["xres"][:, :, :]).then_inc(x_kept, 1)

            @block.vector
            def _(dve):
                dve.wait_ge(x_kept, 1)
                dve.tensor_tensor(T["xres"][:, :, :], T["xres"][:, :, :], bo[:, :].rearrange("p (a d) -> p a d", a=1).broadcast_to([P, NT, D]), ALU.add).then_inc(bo_added, 1)
        with ExitStack() as c2:
            mha_phase(nc, c2, T, K, W)
        with ExitStack() as c2:
            xn = c2.enter_context(nc.sbuf_tensor("xn2", [P, NT, D], F32))
            norm_phase(nc, c2, T, K, "ln2", xn, affine="ln2")
        with ExitStack() as c2:
            route_phase(nc, c2, T, K, "r1", E1, True, 1.0, add_input=True)
        with ExitStack() as c2:
            expert_phase(nc, c2, T, K, {"up": W["we1"], "down": W["we2"], "b_dn": W["be2"]}, "moe1", E1, F1, False)
        with ExitStack() as c2:
            norm_phase(nc, c2, T, K, "last", T["xres"], out=out.rearrange("(t p) d -> p t d", p=P))


def _constants():
    import numpy as np

    layout, width = _const_layout()
    c = np.zeros((P, width), np.float32)

    def put(name, a):
        a0, w = layout[name]
        c[:, a0:a0 + w] = a.reshape(P, w)

    i, j = np.arange(P)[None, :], np.arange(P)[:, None]

    def split(g, j, i):
        return (j // (2 * g) == i // (2 * g)) & (j // g % 2 == 0) & (i // g % 2 == 1)

    put("ident", np.eye(P))
    put("ones", np.stack([np.full((P, P), v) for v in (128.0, 1.0, 1.0 / 128)], 1))
    put("eps", np.tile(np.array([4e-6 * 128, 4e-6, 1e-5, 1e-6]), (P, 1)))
    put("forty", np.full((P, N), 40.0))
    put("level", np.stack([split(1 << l, j, i) for l in range(7)], 1))
    i32, j32 = np.arange(32)[None, :], np.arange(P)[:, None] % 32
    near = [np.concatenate([np.zeros((P, 32)), j32 == i32], 1)]
    near += [np.concatenate([split(1 << l, j32, i32)] * 2, 1) for l in range(5)]
    put("near", np.stack(near, 1))
    put("iota", np.tile(np.arange(E8), (P, 1)))
    tri = np.zeros((P, TB))
    tri[:, P:] = np.where(i > j, -1e30, 0.0)
    put("causal", tri)
    for name, hd in (("rope16", HD1), ("rope128", HD2)):
        inv = (1.0 / 10000.0 ** (np.arange(0, hd, 2, dtype=np.float32) / hd)).astype(np.float32)
        ang = np.arange(TB, dtype=np.float32)[:, None] * inv[None, :]
        cos, sin = np.cos(ang), np.sin(ang)
        tab = np.concatenate([cos, cos, -sin, sin], 1).reshape(2, P, 2 * hd).transpose(1, 0, 2)
        put(name, tab)
    return c


def kernel(**inputs):
    import numpy as _np
    import concourse.bacc as _bacc
    from concourse import mybir as _mybir
    from concourse.bass_utils import run_bass_kernel_spmd as _run

    a0, f0, a1, f1 = "L0_attn_", "L0_ffn_", "L1_attn_", "L1_ffn_"
    get = lambda n: _np.asarray(inputs[n])
    row = lambda n: get(n).reshape(1, -1)
    arrays = {"x": get(a0 + "hidden_states").reshape(TOK, D)}
    for n in ("Wq", "Wk", "Wv", "Wg", "Wo", "Wf1", "Wf2", "Wb", "conv_q", "conv_k", "conv_v"):
        arrays[n] = get(a0 + n)
    arrays["A_log"] = row(a0 + "A_log")
    for n in ("dt_bias", "bg", "o_norm_w"):
        arrays[n] = get(a0 + n).reshape(-1, P).T
    arrays["gate_w"] = get(f0 + "gate_w").T
    for n, m in (("moe0_gate", "w_gate"), ("moe0_up", "w_up"), ("moe0_down", "w_down")):
        arrays[n] = get(f0 + m).transpose(0, 2, 1)
    for n in ("q_kernel", "k_kernel", "v_kernel", "out_kernel"):
        arrays[n] = get(a1 + n)
    for n in ("wq", "wk", "wv", "wo", "w_gate", "we1", "be1", "we2", "be2"):
        arrays[n] = get(f1 + n)
    arrays["be1"] = arrays["be1"].reshape(E1, F1 // P, P).transpose(2, 0, 1)
    for n in ("bq", "bk", "bv", "bo"):
        arrays[n] = row(f1 + n)
    for n in ("ln1_w", "ln1_b", "ln2_w", "ln2_b"):
        arrays[n] = get(f1 + n).reshape(-1, P).T
    arrays["table"] = _constants()
    arrays = {"in_" + n: _np.ascontiguousarray(a) for n, a in arrays.items()}

    nc = _bacc.Bacc("TRN2", target_bir_lowering=False, num_devices=1)
    aps = {n[3:]: nc.dram_tensor(n, a.shape, _mybir.dt.from_np(a.dtype), kind="ExternalInput").ap() for n, a in arrays.items()}
    out = nc.dram_tensor("out", (TOK, D), _mybir.dt.float32, kind="ExternalOutput").ap()
    const = aps.pop("table")
    two_layers(nc, aps, const, out)
    r = _run(nc, [arrays], core_ids=[0])
    return r.results[0]["out"].reshape(B, TB, D)
```
